# Optimizing a Trainium2 kernel written in Bass

```python
import numpy as np
import jax
import jax.numpy as jnp

def _softmax(x, axis=-1):
    return jax.nn.softmax(x, axis=axis)

def _gelu(x):
    return jax.nn.gelu(x, approximate=True)

def _silu(x):
    return jax.nn.silu(x)

def _sigmoid(x):
    return jax.nn.sigmoid(x)

def _layernorm(x, axis=-1, eps=1e-05):
    m = jnp.mean(x, axis=axis, keepdims=True)
    v = jnp.var(x, axis=axis, keepdims=True)
    return (x - m) / jnp.sqrt(v + eps)

def _scatter_add(tgt, idx, src, axis=0):
    return tgt.at[idx].add(src)

def _segment_sum(src, seg, n):
    return jax.ops.segment_sum(src, seg, n)
kernel_name = 'mk_gnn_resnorm_d2_gnn_r8_bbcfd7'

def setup_inputs(seed: int=0):
    np.random.seed(seed)
    _w = jnp.asarray

    def _rec_inputs():
        import jax
        import jax.numpy as jnp
        _gk = jax.random.key(seed)
        x = -0.0005121 + 1.001 * jax.random.normal(jax.random.fold_in(_gk, 1), (6250, 64), jnp.float32)
        src = jax.random.randint(jax.random.fold_in(_gk, 2), (200000,), 0, 6250, jnp.int32)
        dst = jax.random.randint(jax.random.fold_in(_gk, 3), (200000,), 0, 6250, jnp.int32)
        _o = jnp.argsort(dst, stable=True)
        src = src[_o]
        dst = dst[_o]
        edge_attr_64 = -5.3897e-05 + 0.999841 * jax.random.normal(jax.random.fold_in(_gk, 12), (200000, 64), jnp.float32)
        edge_weight1 = jax.random.uniform(jax.random.fold_in(_gk, 14), (200000, 1), jnp.float32, 0.0, 1)
        return (x, src, dst, edge_attr_64, edge_weight1)
    x, src, dst, edge_attr_64, edge_weight1 = _rec_inputs()

    def _L0_gnn_setup():
        import jax, jax.numpy as jnp
        import numpy as np
        N_NODES = 6250
        N_EDGES = 100000
        IN_DIM = 64
        OUT_DIM = 64
        NEG_SLOPE = 0.01

        def _forward(v, pre_w, Wa, att_w, Wg, gate_w, src, dst):
            N = v.shape[0]
            z = v @ Wa
            z_src = z[src]
            z_dst = z[dst]
            e = jnp.concatenate([pre_w * z_src, z_dst], axis=1) @ att_w
            e = jax.nn.leaky_relu(e, NEG_SLOPE)[:, 0]
            e_max = jax.ops.segment_max(e, dst, num_segments=N)
            e_max = jnp.where(jnp.isfinite(e_max), e_max, 0.0)
            ex = jnp.exp(e - e_max[dst])
            denom = jax.ops.segment_sum(ex, dst, num_segments=N)
            alpha = ex / jnp.maximum(denom[dst], 1e-30)
            h = jax.ops.segment_sum(alpha[:, None] * z_src, dst, num_segments=N)
            pw = pre_w * v[src]
            gate_proj = pw @ Wg
            deg = jax.ops.segment_sum(jnp.ones((src.shape[0],), v.dtype), dst, num_segments=N)
            max_feat = jax.ops.segment_max(gate_proj, dst, num_segments=N)
            max_feat = jnp.where(deg[:, None] > 0, max_feat, 0.0)
            mean_feat = jax.ops.segment_sum(pw, dst, num_segments=N) / jnp.maximum(deg, 1.0)[:, None]
            g_comb = jnp.concatenate([v, max_feat, mean_feat], axis=1)
            g_val = jax.nn.sigmoid(g_comb @ gate_w)
            return g_val * h
        key = jax.random.key(seed)
        ks = jax.random.split(key, 8)
        gain = np.sqrt(2.0)

        def xavier(k, shape):
            fan_in, fan_out = (shape[0], shape[1])
            std = gain * np.sqrt(2.0 / (fan_in + fan_out))
            return jax.random.normal(k, shape, dtype=jnp.float32) * std
        return {'v': jax.random.normal(ks[0], (N_NODES, IN_DIM), dtype=jnp.float32), 'pre_w': jax.random.uniform(ks[1], (N_EDGES, 1), dtype=jnp.float32), 'Wa': xavier(ks[2], (IN_DIM, OUT_DIM)), 'att_w': xavier(ks[3], (2 * OUT_DIM, 1)), 'Wg': xavier(ks[4], (IN_DIM, OUT_DIM)), 'gate_w': xavier(ks[5], (2 * IN_DIM + OUT_DIM, 1)), 'src': jax.random.randint(ks[6], (N_EDGES,), 0, N_NODES, dtype=jnp.int32), 'dst': jax.random.randint(ks[7], (N_EDGES,), 0, N_NODES, dtype=jnp.int32)}
    _L0_gnn_all = _L0_gnn_setup()
    _L0_gnn_in = {k: v for k, v in _L0_gnn_all.items() if k in ('Wa', 'att_w', 'Wg', 'gate_w')}
    del _L0_gnn_all

    def _L1_gnn_setup():
        import jax, jax.numpy as jnp
        import numpy as np
        N, E, D, H, L = (2500, 50000, 64, 8, 3)
        HD = D // H
        HID = 4 * D

        def _ln(x, g, b):
            m = x.mean(-1, keepdims=True)
            v = ((x - m) ** 2).mean(-1, keepdims=True)
            return (x - m) / jnp.sqrt(v + 1e-05) * g + b

        def _mlp(x, W1, b1, W2, b2):
            return jax.nn.relu(x @ W1 + b1) @ W2 + b2

        def _forward(x, edge_embed, eng, enb, eW1, eb1, eW2, eb2, Wq, bq, Wkn, bkn, Wke, bke, Wvn, bvn, Wve, bve, Wself, bself, Wih, bih, Whh, bhh, Wout, bout, n1g, n1b, n2g, n2b, mW1, mb1, mW2, mb2, ng, nb, edge_index):
            src, dst = (edge_index[0], edge_index[1])
            n = x.shape[0]
            scale = HD ** 0.5
            edge_attr = _mlp(_ln(edge_embed, eng, enb), eW1, eb1, eW2, eb2)
            for l in range(L):
                h = _ln(x, n1g[l], n1b[l])
                xi, xj = (h[dst], h[src])
                q = (xi @ Wq[l] + bq[l]).reshape(-1, H, HD)
                kn = (xj @ Wkn[l] + bkn[l]).reshape(-1, H, HD)
                ke = (edge_attr @ Wke[l] + bke[l]).reshape(-1, H, HD)
                vn = (xj @ Wvn[l] + bvn[l]).reshape(-1, H, HD)
                ve = (edge_attr @ Wve[l] + bve[l]).reshape(-1, H, HD)
                alpha = (q * (kn + ke)).sum(-1) / scale
                amax = jax.ops.segment_max(alpha, dst, num_segments=n)
                ex = jnp.exp(alpha - amax[dst])
                den = jax.ops.segment_sum(ex, dst, num_segments=n)
                alpha = ex / (den[dst] + 1e-16)
                msg = ((vn + ve) * alpha[..., None]).reshape(-1, D)
                agg = jax.ops.segment_sum(msg, dst, num_segments=n)
                gate = jax.nn.sigmoid(agg @ Wih[l] + bih[l] + h @ Whh[l] + bhh[l])
                upd = agg + gate * (h @ Wself[l] + bself[l] - agg)
                x = x + upd @ Wout[l] + bout[l]
                h2 = _ln(x, n2g[l], n2b[l])
                x = x + _mlp(h2, mW1[l], mb1[l], mW2[l], mb2[l])
            return _ln(x, ng, nb)
        key = jax.random.key(seed)
        ks = jax.random.split(key, 40)
        f32 = jnp.float32

        def w(k, *s):
            return jax.random.normal(k, s, f32) * 0.02
        inp = {'x': jax.random.normal(ks[0], (N, D), f32), 'edge_embed': jax.random.normal(ks[1], (E, D), f32), 'eng': jnp.ones((D,), f32), 'enb': jnp.zeros((D,), f32), 'eW1': w(ks[2], D, HID), 'eb1': jnp.zeros((HID,), f32), 'eW2': w(ks[3], HID, D), 'eb2': jnp.zeros((D,), f32), 'n1g': jnp.ones((L, D), f32), 'n1b': jnp.zeros((L, D), f32), 'n2g': jnp.ones((L, D), f32), 'n2b': jnp.zeros((L, D), f32), 'mW1': w(ks[4], L, D, HID), 'mb1': jnp.zeros((L, HID), f32), 'mW2': w(ks[5], L, HID, D), 'mb2': jnp.zeros((L, D), f32), 'ng': jnp.ones((D,), f32), 'nb': jnp.zeros((D,), f32), 'edge_index': jax.random.randint(ks[6], (2, E), 0, N)}
        names = ['Wq', 'Wkn', 'Wke', 'Wvn', 'Wve', 'Wself', 'Wih', 'Whh', 'Wout']
        for i, nm in enumerate(names):
            inp[nm] = w(ks[7 + i], L, D, D)
            inp['b' + nm[1:]] = jnp.zeros((L, D), f32)
        return inp
    _L1_gnn_all = _L1_gnn_setup()
    _L1_gnn_in = {k: v for k, v in _L1_gnn_all.items() if k in ('eng', 'enb', 'eW1', 'eb1', 'eW2', 'eb2', 'Wq', 'bq', 'Wkn', 'bkn', 'Wke', 'bke', 'Wvn', 'bvn', 'Wve', 'bve', 'Wself', 'bself', 'Wih', 'bih', 'Whh', 'bhh', 'Wout', 'bout', 'n1g', 'n1b', 'n2g', 'n2b', 'mW1', 'mb1', 'mW2', 'mb2', 'ng', 'nb')}
    del _L1_gnn_all
    return {'x': x, 'src': src, 'dst': dst, 'edge_attr_64': edge_attr_64, 'edge_weight1': edge_weight1, 'L0_gnn_Wa': _L0_gnn_in['Wa'], 'L0_gnn_att_w': _L0_gnn_in['att_w'], 'L0_gnn_Wg': _L0_gnn_in['Wg'], 'L0_gnn_gate_w': _L0_gnn_in['gate_w'], 'L1_gnn_eng': _L1_gnn_in['eng'], 'L1_gnn_enb': _L1_gnn_in['enb'], 'L1_gnn_eW1': _L1_gnn_in['eW1'], 'L1_gnn_eb1': _L1_gnn_in['eb1'], 'L1_gnn_eW2': _L1_gnn_in['eW2'], 'L1_gnn_eb2': _L1_gnn_in['eb2'], 'L1_gnn_Wq': _L1_gnn_in['Wq'], 'L1_gnn_bq': _L1_gnn_in['bq'], 'L1_gnn_Wkn': _L1_gnn_in['Wkn'], 'L1_gnn_bkn': _L1_gnn_in['bkn'], 'L1_gnn_Wke': _L1_gnn_in['Wke'], 'L1_gnn_bke': _L1_gnn_in['bke'], 'L1_gnn_Wvn': _L1_gnn_in['Wvn'], 'L1_gnn_bvn': _L1_gnn_in['bvn'], 'L1_gnn_Wve': _L1_gnn_in['Wve'], 'L1_gnn_bve': _L1_gnn_in['bve'], 'L1_gnn_Wself': _L1_gnn_in['Wself'], 'L1_gnn_bself': _L1_gnn_in['bself'], 'L1_gnn_Wih': _L1_gnn_in['Wih'], 'L1_gnn_bih': _L1_gnn_in['bih'], 'L1_gnn_Whh': _L1_gnn_in['Whh'], 'L1_gnn_bhh': _L1_gnn_in['bhh'], 'L1_gnn_Wout': _L1_gnn_in['Wout'], 'L1_gnn_bout': _L1_gnn_in['bout'], 'L1_gnn_n1g': _L1_gnn_in['n1g'], 'L1_gnn_n1b': _L1_gnn_in['n1b'], 'L1_gnn_n2g': _L1_gnn_in['n2g'], 'L1_gnn_n2b': _L1_gnn_in['n2b'], 'L1_gnn_mW1': _L1_gnn_in['mW1'], 'L1_gnn_mb1': _L1_gnn_in['mb1'], 'L1_gnn_mW2': _L1_gnn_in['mW2'], 'L1_gnn_mb2': _L1_gnn_in['mb2'], 'L1_gnn_ng': _L1_gnn_in['ng'], 'L1_gnn_nb': _L1_gnn_in['nb']}

def reference(x, src, dst, edge_attr_64, edge_weight1, L0_gnn_Wa, L0_gnn_att_w, L0_gnn_Wg, L0_gnn_gate_w, L1_gnn_eng, L1_gnn_enb, L1_gnn_eW1, L1_gnn_eb1, L1_gnn_eW2, L1_gnn_eb2, L1_gnn_Wq, L1_gnn_bq, L1_gnn_Wkn, L1_gnn_bkn, L1_gnn_Wke, L1_gnn_bke, L1_gnn_Wvn, L1_gnn_bvn, L1_gnn_Wve, L1_gnn_bve, L1_gnn_Wself, L1_gnn_bself, L1_gnn_Wih, L1_gnn_bih, L1_gnn_Whh, L1_gnn_bhh, L1_gnn_Wout, L1_gnn_bout, L1_gnn_n1g, L1_gnn_n1b, L1_gnn_n2g, L1_gnn_n2b, L1_gnn_mW1, L1_gnn_mb1, L1_gnn_mW2, L1_gnn_mb2, L1_gnn_ng, L1_gnn_nb):
    import jax
    import jax.numpy as jnp

    def _L0_gnn_ref(v, pre_w, Wa, att_w, Wg, gate_w, src, dst):
        import jax, jax.numpy as jnp
        import numpy as np
        N_NODES = 6250
        N_EDGES = 100000
        IN_DIM = 64
        OUT_DIM = 64
        NEG_SLOPE = 0.01

        def _forward(v, pre_w, Wa, att_w, Wg, gate_w, src, dst):
            N = v.shape[0]
            z = v @ Wa
            z_src = z[src]
            z_dst = z[dst]
            e = jnp.concatenate([pre_w * z_src, z_dst], axis=1) @ att_w
            e = jax.nn.leaky_relu(e, NEG_SLOPE)[:, 0]
            e_max = jax.ops.segment_max(e, dst, num_segments=N)
            e_max = jnp.where(jnp.isfinite(e_max), e_max, 0.0)
            ex = jnp.exp(e - e_max[dst])
            denom = jax.ops.segment_sum(ex, dst, num_segments=N)
            alpha = ex / jnp.maximum(denom[dst], 1e-30)
            h = jax.ops.segment_sum(alpha[:, None] * z_src, dst, num_segments=N)
            pw = pre_w * v[src]
            gate_proj = pw @ Wg
            deg = jax.ops.segment_sum(jnp.ones((src.shape[0],), v.dtype), dst, num_segments=N)
            max_feat = jax.ops.segment_max(gate_proj, dst, num_segments=N)
            max_feat = jnp.where(deg[:, None] > 0, max_feat, 0.0)
            mean_feat = jax.ops.segment_sum(pw, dst, num_segments=N) / jnp.maximum(deg, 1.0)[:, None]
            g_comb = jnp.concatenate([v, max_feat, mean_feat], axis=1)
            g_val = jax.nn.sigmoid(g_comb @ gate_w)
            return g_val * h
        return _forward(v, pre_w, Wa, att_w, Wg, gate_w, src, dst)

    def _L1_gnn_ref(x, edge_embed, edge_index, eng, enb, eW1, eb1, eW2, eb2, Wq, bq, Wkn, bkn, Wke, bke, Wvn, bvn, Wve, bve, Wself, bself, Wih, bih, Whh, bhh, Wout, bout, n1g, n1b, n2g, n2b, mW1, mb1, mW2, mb2, ng, nb):
        import jax, jax.numpy as jnp
        import numpy as np
        N, E, D, H, L = (2500, 50000, 64, 8, 3)
        HD = D // H
        HID = 4 * D

        def _ln(x, g, b):
            m = x.mean(-1, keepdims=True)
            v = ((x - m) ** 2).mean(-1, keepdims=True)
            return (x - m) / jnp.sqrt(v + 1e-05) * g + b

        def _mlp(x, W1, b1, W2, b2):
            return jax.nn.relu(x @ W1 + b1) @ W2 + b2

        def _forward(x, edge_embed, eng, enb, eW1, eb1, eW2, eb2, Wq, bq, Wkn, bkn, Wke, bke, Wvn, bvn, Wve, bve, Wself, bself, Wih, bih, Whh, bhh, Wout, bout, n1g, n1b, n2g, n2b, mW1, mb1, mW2, mb2, ng, nb, edge_index):
            src, dst = (edge_index[0], edge_index[1])
            n = x.shape[0]
            scale = HD ** 0.5
            edge_attr = _mlp(_ln(edge_embed, eng, enb), eW1, eb1, eW2, eb2)
            for l in range(L):
                h = _ln(x, n1g[l], n1b[l])
                xi, xj = (h[dst], h[src])
                q = (xi @ Wq[l] + bq[l]).reshape(-1, H, HD)
                kn = (xj @ Wkn[l] + bkn[l]).reshape(-1, H, HD)
                ke = (edge_attr @ Wke[l] + bke[l]).reshape(-1, H, HD)
                vn = (xj @ Wvn[l] + bvn[l]).reshape(-1, H, HD)
                ve = (edge_attr @ Wve[l] + bve[l]).reshape(-1, H, HD)
                alpha = (q * (kn + ke)).sum(-1) / scale
                amax = jax.ops.segment_max(alpha, dst, num_segments=n)
                ex = jnp.exp(alpha - amax[dst])
                den = jax.ops.segment_sum(ex, dst, num_segments=n)
                alpha = ex / (den[dst] + 1e-16)
                msg = ((vn + ve) * alpha[..., None]).reshape(-1, D)
                agg = jax.ops.segment_sum(msg, dst, num_segments=n)
                gate = jax.nn.sigmoid(agg @ Wih[l] + bih[l] + h @ Whh[l] + bhh[l])
                upd = agg + gate * (h @ Wself[l] + bself[l] - agg)
                x = x + upd @ Wout[l] + bout[l]
                h2 = _ln(x, n2g[l], n2b[l])
                x = x + _mlp(h2, mW1[l], mb1[l], mW2[l], mb2[l])
            return _ln(x, ng, nb)
        return _forward(x, edge_embed, eng, enb, eW1, eb1, eW2, eb2, Wq, bq, Wkn, bkn, Wke, bke, Wvn, bvn, Wve, bve, Wself, bself, Wih, bih, Whh, bhh, Wout, bout, n1g, n1b, n2g, n2b, mW1, mb1, mW2, mb2, ng, nb, edge_index)
    edge_index = jnp.stack([src, dst])
    x = _layernorm(x + _L0_gnn_ref(x, edge_weight1, L0_gnn_Wa, L0_gnn_att_w, L0_gnn_Wg, L0_gnn_gate_w, src, dst), axis=-1)
    x = _layernorm(x + _L1_gnn_ref(x, edge_attr_64, edge_index, L1_gnn_eng, L1_gnn_enb, L1_gnn_eW1, L1_gnn_eb1, L1_gnn_eW2, L1_gnn_eb2, L1_gnn_Wq, L1_gnn_bq, L1_gnn_Wkn, L1_gnn_bkn, L1_gnn_Wke, L1_gnn_bke, L1_gnn_Wvn, L1_gnn_bvn, L1_gnn_Wve, L1_gnn_bve, L1_gnn_Wself, L1_gnn_bself, L1_gnn_Wih, L1_gnn_bih, L1_gnn_Whh, L1_gnn_bhh, L1_gnn_Wout, L1_gnn_bout, L1_gnn_n1g, L1_gnn_n1b, L1_gnn_n2g, L1_gnn_n2b, L1_gnn_mW1, L1_gnn_mb1, L1_gnn_mW2, L1_gnn_mb2, L1_gnn_ng, L1_gnn_nb), axis=-1)
    return x

_drawn_inputs = setup_inputs


def setup_inputs(seed=0):
    import zlib

    import numpy as np

    out = dict(_drawn_inputs(seed))
    spreads = {'L1_gnn_eng': (1.0, 0.6),
     'L1_gnn_enb': (0.0, 0.8),
     'L1_gnn_eb1': (0.0, 0.8),
     'L1_gnn_eb2': (0.0, 0.8),
     'L1_gnn_bq': (0.0, 0.8),
     'L1_gnn_bkn': (0.0, 2.0),
     'L1_gnn_bke': (0.0, 2.0),
     'L1_gnn_bvn': (0.0, 0.8),
     'L1_gnn_bve': (0.0, 0.8),
     'L1_gnn_bself': (0.0, 0.8),
     'L1_gnn_bih': (0.0, 0.8),
     'L1_gnn_bhh': (0.0, 0.8),
     'L1_gnn_bout': (0.0, 0.1),
     'L1_gnn_n1g': (1.0, 0.6),
     'L1_gnn_n1b': (0.0, 0.8),
     'L1_gnn_n2g': (1.0, 0.6),
     'L1_gnn_n2b': (0.0, 2.0),
     'L1_gnn_mb1': (0.0, 0.513),
     'L1_gnn_mb2': (0.0, 0.1),
     'L1_gnn_ng': (1.0, 0.2),
     'L1_gnn_nb': (0.0, 0.1)}
    factors = {'edge_attr_64': 8.0,
     'L1_gnn_eW1': 8.0,
     'L1_gnn_eW2': 8.0,
     'L1_gnn_Wq': 8.0,
     'L1_gnn_Wkn': 8.0,
     'L1_gnn_Wke': 8.0,
     'L1_gnn_Wvn': 8.0,
     'L1_gnn_Wve': 8.0,
     'L1_gnn_Wself': 4.871,
     'L1_gnn_Wih': 8.0,
     'L1_gnn_Whh': 8.0,
     'L1_gnn_Wout': 3.724}
    for name, (base, spread) in spreads.items():
        noise = np.random.default_rng([zlib.crc32(name.encode()), seed]).standard_normal(out[name].shape)
        drawn = base * np.exp(spread * noise) if base else spread * noise
        out[name] = jnp.asarray(drawn.astype(out[name].dtype))
    for name, factor in factors.items():
        out[name] = (out[name] * factor).astype(out[name].dtype)
    return out
```

```python
import concourse.bass as bass
from concourse import mybir
from contextlib import ExitStack

P = 128
N = 6250
E = 200000
D = 64
H = 8
HD = D // H
L = 3
HID = 4 * D
C = 56
NCH = 28
T = C * NCH
EP = P * T
NT = 49
NP = NT * P
TG = 7
NG = NT // TG
GN = TG * P
HN = GN // 2
PAIRS = C // 2
PT = C // 8
BIG = 1e30
R0 = 3 + 2 * D
V0 = 2 + D
R1 = 2 * H + D
V1 = H + D
W0 = 2 * D + 3
SCALE = float(HD) ** -0.5
NWIN = 18
NLW = 30
PD_RP, PD_END = 8, 9
BSELF, BIH, BHH, BOUT, MB2, N1G, N1B, N2G, N2B, NGC, NBC = range(11)


def build(nc, A, out):
    f32, bf16, i32 = mybir.dt.float32, mybir.dt.bfloat16, mybir.dt.int32
    ALU, ACT, AX = mybir.AluOpType, mybir.ActivationFunctionType, mybir.AxisListType
    IND = bass.IndirectOffsetOnAxis
    ctx = ExitStack()

    def dram(name, shape, dt=f32):
        return nc.dram_tensor(name, shape, dt, kind="Internal").ap()

    tab0 = dram("tab0", (NP, W0))
    tabkv = dram("tabkv", (NP, 2 * D))
    tabq = dram("tabq", (NP, D))
    s2exp = dram("s2exp", (EP + NP, 1))
    qexp = dram("qexp", (EP + NP, D))
    st0 = dram("st0", (EP + 1 + P, R0))
    st1 = dram("st1", (EP + 1 + P, R1))
    eaT = dram("eaT", (NCH, P, PAIRS * P))
    xTd = dram("xTd", (D, NP))
    x1Td = dram("x1Td", (D, NP))
    hTd = dram("hTd", (D, NP))
    rptr = dram("rptr", (NP, 2))

    def chunk_rows(t, width, c):
        return t[0:EP, :].rearrange("(p t) w -> p (t w)", p=P)[:, bass.ds(c * (C * width), C * width)]

    src_pt = A["src"].rearrange("(p t) -> p t", p=P)
    ew_pt = A["edge_weight1"].rearrange("(p t) o -> p (t o)", p=P)

    with ctx:
        def sbx(stack):
            return lambda name, shape, dt=f32: stack.enter_context(nc.sbuf_tensor(name, shape, dt))

        def sem(name):
            return ctx.enter_context(nc.semaphore(name))

        sb = sbx(ctx)
        ident = sb("ident", [P, P])
        onesD = sb("onesD", [D, D])
        cont = sb("cont", [P, T])
        srcI = sb("srcI", [P, 2, C], i32)
        firstI = sb("firstI", [P, 1], i32)
        endI = sb("endI", [P, NT], i32)
        startI = sb("startI", [P, NT], i32)
        fixI = sb("fixI", [P, 1], i32)
        gmask = sb("gmask", [V1, P])
        contC = sb("contC", [P, C])
        maskC = sb("maskC", [P, C])
        zeros = sb("zeros", [P, 896])
        iotaFX = sb("iotaFX", [P, 1])
        epsc = sb("epsc", [P, 1])
        MX = sb("MX", [P, V1])
        MXT = sb("MXT", [V1, P])
        MT = sb("MT", [V1, P])
        VT = sb("VT", [V1, P])
        sh = sb("sh", [V1, 2, P])
        ab = sb("ab", [P, 2, P])
        abE = sb("abE", [P, 2, P])
        FMT = sb("FMT", [D, 2, P])
        wide = sb("wide", [P, 2, V1])
        rfix = sb("rfix", [P, R0])
        wfix = sb("wfix", [P, R0])
        PS = ctx.enter_context(nc.psum_tensor("PS", [P, 8, 512], f32))
        PSf = PS[:, :, :].rearrange("p b n -> p (b n)")

        w_in = sem("w_in")
        pool_c = sem("pool_c")
        p_dve = sem("p_dve")
        p_pe = sem("p_pe")
        p_rp = sem("p_rp")
        rp_first = sem("rp_first")
        p_z = sem("p_z")
        oh_ready = sem("oh_ready")
        oh_used = sem("oh_used")
        waits_sp, waits_pool, waits_pe = sem("waits_sp"), sem("waits_pool"), sem("waits_pe")
        n0_x, n0_pe, n0_act, n0_tab, n0_free = (sem(n) for n in ("n0_x", "n0_pe", "n0_act", "n0_tab", "n0_free"))
        s2_put = sem("s2_put")
        s2_first = sem("s2_first")
        idx0 = [sem(f"idx0_{u}") for u in range(2)]
        in0 = [sem(f"in0_{u}") for u in range(2)]
        xe_in = [sem(f"xe_in{u}") for u in range(2)]
        got0 = [sem(f"got0_{u}") for u in range(2)]
        seen0 = sem("seen0")
        done0 = sem("done0")
        xe_free = sem("xe_free")
        d0_ready, e0_ready = sem("d0_ready"), sem("e0_ready")
        var_ready, sqrt_ready, xn_ready = sem("var_ready"), sem("sqrt_ready"), sem("xn_ready")
        st0_out = [sem(f"st0_out{u}") for u in range(2)]
        m_pe, m_act = sem("m_pe"), sem("m_act")
        ea_out = sem("ea_out")
        zq = sem("zq")
        f_pe, f_dve, f_act, f_got, f_put = (sem(n) for n in ("f_pe", "f_dve", "f_act", "f_got", "f_put"))
        rows_got = sem("rows_got")
        u_x, u_dve, u_act, u_pe, u_out = (sem(n) for n in ("u_x", "u_dve", "u_act", "u_pe", "u_out"))
        l_w = sem("l_w")
        l_b = sem("l_b")
        a_x, a_pe, a_dve, a_act, a_out = (sem(n) for n in ("a_x", "a_pe", "a_dve", "a_act", "a_out"))
        q_dram, q_put, q_first, q_done = (sem(n) for n in ("q_dram", "q_put", "q_first", "q_done"))
        idx1 = [sem(f"idx1_{u}") for u in range(2)]
        q_in = [sem(f"q_in{u}") for u in range(2)]
        ea_in = [sem(f"ea_in{u}") for u in range(2)]
        got1 = [sem(f"got1_{u}") for u in range(2)]
        seen1 = sem("seen1")
        done1 = sem("done1")
        kv_ready = sem("kv_ready")
        k_used = sem("k_used")
        v_moved = sem("v_moved")
        d1_ready, e1_ready = sem("d1_ready"), sem("e1_ready")
        st1_out = [sem(f"st1_out{u}") for u in range(2)]
        b_x, b_pe, b_dve, b_act, b_out = (sem(n) for n in ("b_x", "b_pe", "b_dve", "b_act", "b_out"))
        c_x, c_pe, c_dve, c_act, c_out = (sem(n) for n in ("c_x", "c_pe", "c_dve", "c_act", "c_out"))

        first = ExitStack()
        sb = sbx(first)
        Wcat = sb("Wcat", [D, 132])
        Wa_s = sb("Wa_s", [D, D])
        WaT = sb("WaT", [D, D])
        attc = sb("attc", [D, 2])
        gw2r = sb("gw2r", [P, D])
        W1raw = sb("W1raw", [P, HID])
        engc = sb("engc", [P, 1])
        enbc = sb("enbc", [D, 1])
        eb1c = sb("eb1c", [P, 2])
        b1c = sb("b1c", [P, 2])
        b2c = sb("b2c", [P, 1])
        W1p = sb("W1p", [P, 2, 2, P])
        W2p = sb("W2p", [P, 2, 2, P])
        W2raw = sb("W2raw", [P, 2, D])
        s2n = sb("s2n", [P, NT])
        xg1 = sb("xg1", [P, NT])
        degn = sb("degn", [P, NT])
        G0 = sb("G0", [P, 2, C, W0])
        S0 = sb("S0", [P, 2, C + 1, R0])
        xe = sb("xe", [P, 2, C, D])
        eaC = sb("eaC", [P, PAIRS, P])
        xT8 = sb("xT8", [P, 512])
        hid8 = sb("hid8", [P, 2, 2, 512])
        ewC = sb("ewC", [P, 2, C])
        s2C = sb("s2C", [P, 2, C])
        s2x = sb("s2x", [P, C + 1])
        al0 = sb("al0", [P, C])
        uw0 = sb("uw0", [P, C])
        dd0 = sb("dd0", [P, 2, C])
        ee0 = sb("ee0", [P, 2, C])
        mu8 = sb("mu8", [P, C])
        sd8 = sb("sd8", [P, C])
        rs8 = sb("rs8", [P, C])
        G0f = G0[:, :, :, :].rearrange("p u c w -> p (u c w)")
        S0f = S0[:, :, :, :].rearrange("p u c w -> p (u c w)")
        xef = xe[:, :, :, :].rearrange("p u c w -> p (u c w)")
        eaf = eaC[:, :, :].rearrange("p a b -> p (a b)")
        dstI = G0f[:, 0:T].bitcast(i32)
        hiI = G0f[:, T:2 * T].bitcast(i32)
        loI = G0f[:, 2 * T:3 * T].bitcast(i32)
        dstF = G0f[:, 3 * T:4 * T]
        hiF = G0f[:, 4 * T:5 * T]
        loF = G0f[:, 5 * T:6 * T]
        OHW = NT + P
        oh = [S0f[:, u * (C * OHW // 2):(u + 1) * (C * OHW // 2)].bitcast(bf16)
              .rearrange("p (c w) -> p c w", c=C) for u in range(2)]
        at = [0]

        def eview(n):
            at[0] += n
            return eaf[:, at[0] - n:at[0]]

        iotaR = eview(P)
        iotaC = eview(1)
        iotaPT = eview(1)
        nodeE = eview(NT)
        tri = eview(P)
        degR = eview(P)
        cumR = eview(P)
        baseC = eview(1)
        endxR = eview(P)
        lastF = eview(NT)
        firstF = eview(NT)
        neF = eview(NT)
        tmpN = eview(NT)
        F1b = eview(V1)
        F2b = eview(V1)
        rowF = eview(P)
        rowL = eview(P)
        gF = eview(P)
        rpF = eview(2)
        vF = eview(4)
        rp_s = eview(2 * NT).rearrange("p (t o) -> p t o", o=2)
        zw = eview(P)
        xg = xef[:, 0:TG * D].rearrange("p (t d) -> p t d", t=TG)
        xTg = xef[:, 512:512 + GN]
        tg = xef[:, 1536:1536 + TG * 132].rearrange("p (t w) -> p t w", t=TG)
        rows0 = G0f[:, 0:NT * R0].rearrange("p (t w) -> p t w", t=NT)
        xn0 = S0f[:, 0:NT * D].rearrange("p (t d) -> p t d", t=NT)
        tp0 = S0f[:, NT * D:2 * NT * D].rearrange("p (t d) -> p t d", t=NT)
        tq0 = S0f[:, 2 * NT * D:3 * NT * D].rearrange("p (t d) -> p t d", t=NT)
        n49 = [S0f[:, 3 * NT * D + NT * k:3 * NT * D + NT * (k + 1)] for k in range(8)]
        xT0 = G0f[0:D, NT * R0:NT * R0 + NP]
        first.close()

        second = ExitStack()
        sb = sbx(second)
        G1 = sb("G1", [P, 2, C, 2 * D])
        Q1 = sb("Q1", [P, 2, C, D])
        PR = sb("PR", [P, C, D])
        S1 = sb("S1", [P, 2, C + 1, R1])
        EA = sb("EA", [P, 2, PAIRS, P])
        al1 = sb("al1", [P, C, H])
        dd1 = sb("dd1", [P, 2, C, H])
        ee1 = sb("ee1", [P, 2, C, H])
        qb = sb("qb", [P, D])
        ql = sb("ql", [P, D])
        qlb = sb("qlb", [P, D])
        Wkvp = sb("Wkvp", [P, 4 * D])
        Wqkv = sb("Wqkv", [D, 3 * D])
        Wn = sb("Wn", [D, 4, D])
        mW1s = sb("mW1s", [D, HID])
        mW2s = sb("mW2s", [P, 2, D])
        mb1c = sb("mb1c", [P, 2])
        bqkv = sb("bqkv", [P, 5, D])
        cb = sb("cb", [D, 12])
        bgc = sb("bgc", [D, 1])
        G1f = G1[:, :, :, :].rearrange("p u c w -> p (u c w)")
        gat = [0]

        def gview(n, parts=P):
            gat[0] += n
            return G1f[0:parts, gat[0] - n:gat[0]]

        nx = gview(GN, D)
        nh = gview(GN, D)
        nxc = gview(GN, D)
        nsq = gview(GN, D)
        nsd = gview(GN, D)
        nrs = gview(GN, D)
        nagT = gview(GN, D)
        ngt = gview(GN, D)
        nsl = gview(GN, D)
        nx1 = gview(GN, D)
        nhid = gview(2 * GN).rearrange("p (k n) -> p k n", k=2)
        nkv = gview(TG * 2 * D).rearrange("p (t d) -> p t d", t=TG)
        Q1f = Q1[:, :, :, :].rearrange("p u c w -> p (u c w)")
        q_all = Q1f[:, 0:NT * D].rearrange("p (t d) -> p t d", t=NT)
        rows1 = Q1f[:, 0:NT * R1].rearrange("p (t w) -> p t w", t=NT)
        PRf = PR[:, :, :].rearrange("p c w -> p (c w)")
        rden = PRf[:, 0:NT * H].rearrange("p (t h) -> p t h", t=NT)
        nag = PRf[:, 512:512 + TG * D].rearrange("p (t d) -> p t d", t=TG)

        def halves(bank, parts=D):
            return PS[0:parts, bank:bank + 2, 0:HN]

        def two(ap):
            return ap.rearrange("p (k n) -> p k n", k=2)

        def hold(eng, passed, s, value):
            eng.wait_ge(s, value)
            eng.sem_inc(passed, 1)

        block = ctx.enter_context(nc.Block())

        @block.sync
        def _(sp):
            loads = ((dstI[:, :], A["dst"].rearrange("(p t) -> p t", p=P)),
                     (Wa_s[:, :], A["Wa"]), (Wcat[:, 0:D], A["Wa"]), (Wcat[:, D:2 * D], A["Wg"]),
                     (attc[:, 0:1], A["att_w"][0:D, :]), (attc[:, 1:2], A["att_w"][D:2 * D, :]),
                     (Wcat[:, 131:132], A["gate_w"][0:D, :]), (Wcat[:, 129:130], A["gate_w"][2 * D:3 * D, :]),
                     (gw2r[:, :], A["gate_w"][D:2 * D, :].rearrange("d o -> o d").broadcast_to([P, D])),
                     (W1raw[0:D, :], A["eW1"]), (W1raw[D:P, :], A["eW1"]),
                     (engc[0:D, :], A["eng"].unsqueeze(1)), (engc[D:P, :], A["eng"].unsqueeze(1)),
                     (enbc[:, :], A["enb"].unsqueeze(1)),
                     (eb1c[:, :], A["eb1"].rearrange("(k p) -> p k", p=P)),
                     (b2c[0:D, :], A["eb2"].unsqueeze(1)), (b2c[D:P, :], A["eb2"].unsqueeze(1)),
                     (W2raw[:, :, :], A["eW2"].rearrange("(k p) d -> p k d", p=P)))
            assert len(loads) == NWIN
            for dst, s in loads:
                sp.dma_start(dst, s, allow_slow_non_contiguous=True).then_inc(w_in, 16)
            sp.wait_ge(p_dve, 1)
            sp.dma_start(s2exp[0:EP, :].rearrange("(p k t) o -> p k (t o)", p=P, k=2),
                         zeros[:, 0:T // 2].unsqueeze(1).broadcast_to([P, 2, T // 2])).then_inc(p_z, 16)
            sp.dma_start(st0[EP:EP + 1, :], zeros[0:1, 0:R0]).then_inc(st0_out[0], 16)
            sp.dma_start(st0[EP + 1:EP + 1 + P, :], zeros[:, 0:R0]).then_inc(st0_out[1], 16)
            sp.dma_start(st1[EP:EP + 1, :], zeros[0:1, 0:R1]).then_inc(st1_out[0], 16)
            sp.dma_start(st1[EP + 1:EP + 2, :], zeros[0:1, 0:R1]).then_inc(ea_out, 16)
            sp.dma_start(st1[EP + 2:EP + 1 + P, :], zeros[0:P - 1, 0:R1]).then_inc(st1_out[1], 16)
            with sp.Fori(0, NG) as g:
                sp.wait_ge(n0_free, g + 1)
                sp.dma_start(xg[:, :, :], A["x"][bass.ds(g * GN, GN), :].rearrange("(t p) d -> p t d", p=P)).then_inc(n0_x, 16)
                sp.wait_ge(n0_act, 4 * g + 4)
                sp.dma_start(tab0[bass.ds(g * GN, GN), :].rearrange("(t p) w -> p t w", p=P), tg[:, :, 0:W0]).then_inc(n0_tab, 16)
                sp.wait_ge(n0_tab, 16 * g + 16)
                sp.sem_inc(n0_free, 1)
            sp.wait_ge(p_dve, PD_RP)
            sp.dma_start(rptr[:, :].rearrange("(t p) o -> p t o", p=P), rp_s[:, :, :]).then_inc(p_rp, 16)
            sp.wait_ge(p_dve, PD_END)
            sp.wait_ge(s2_put, 16 * NT)
            sp.wait_ge(s2_first, 16)
            sp.dma_start(s2exp[0:EP, :].rearrange("(p t) o -> p (t o)", p=P)[:, 0:1], rfix[:, W0 - 1:W0],
                         allow_slow_non_contiguous=True).then_inc(p_z, 16)
            sp.wait_ge(p_z, 32)
            with sp.Fori(0, NCH // 2) as i:
                for u in range(2):
                    c = 2 * i + u
                    sp.wait_ge(seen0, c + 1)
                    sp.dma_start(srcI[:, u, :], src_pt[:, bass.ds(c * C, C)]).then_inc(idx0[u], 16)
                    sp.wait_ge(xe_free, c + 1)
                    sp.dma_start(xe[:, u, :, :].rearrange("p c d -> p (c d)"), chunk_rows(A["edge_attr_64"], D, c)).then_inc(xe_in[u], 16)
                    sp.wait_ge(done0, c + 1)
                    sp.dma_start(ewC[:, u, :], ew_pt[:, bass.ds(c * C, C)]).then_inc(in0[u], 16)
                    sp.dma_start(s2C[:, u, :], chunk_rows(s2exp, 1, c)).then_inc(in0[u], 16)
                    sp.dma_start(chunk_rows(qexp, D, c).rearrange("p (k n) -> p k n", k=4),
                                 zeros[:, :].unsqueeze(1).broadcast_to([P, 4, 896])).then_inc(zq, 16)
            sp.wait_ge(f_dve, 5)
            for u in range(2):
                sp.wait_ge(st0_out[u], 16 * (NCH // 2 + 1))
            sp.dma_start(xn0[:, :, :], A["x"].rearrange("(t p) d -> p t d", p=P)).then_inc(u_x, 16)
            sp.wait_ge(u_act, 2 + NG)
            sp.dma_start(xTd[:, :], xT0[:, :]).then_inc(u_out, 16)
            sp.dma_start(x1Td[:, :], xT0[:, :]).then_inc(u_out, 16)
            sp.wait_ge(u_out, 32)
            sp.wait_ge(zq, 16 * NCH)
            sp.wait_ge(ea_out, 16 * (NCH + 1))
            sp.wait_ge(l_b, 1)
            with sp.Fori(0, L) as l:
                def row(name):
                    return A[name][bass.ds(l, 1), :]

                n = 0
                for dst, name in ((Wkvp[0:D, 0:D], "Wke"), (Wkvp[D:P, D:2 * D], "Wke"),
                                  (Wkvp[0:D, 2 * D:3 * D], "Wve"), (Wkvp[D:P, 3 * D:4 * D], "Wve"),
                                  (Wqkv[:, 0:D], "Wq"), (Wqkv[:, D:2 * D], "Wkn"), (Wqkv[:, 2 * D:3 * D], "Wvn"),
                                  (Wn[:, 0, :], "Wself"), (Wn[:, 1, :], "Wih"), (Wn[:, 2, :], "Whh"), (Wn[:, 3, :], "Wout"),
                                  (mW1s[:, :], "mW1")):
                    sp.dma_start(dst, A[name][bass.ds(l, 1), :, :].rearrange("o a b -> (o a) b")).then_inc(l_w, 16)
                    n += 1
                for kh in range(2):
                    sp.dma_start(mW2s[:, kh, :], A["mW2"][bass.ds(l, 1), kh * P:(kh + 1) * P, :].rearrange("o a b -> (o a) b")).then_inc(l_w, 16)
                    sp.dma_start(mb1c[:, kh:kh + 1], A["mb1"][bass.ds(l, 1), kh * P:(kh + 1) * P].rearrange("o d -> d o"),
                                 allow_slow_non_contiguous=True).then_inc(l_w, 16)
                    n += 2
                for j, name in enumerate(("bq", "bkn", "bvn", "bke", "bve")):
                    sp.dma_start(bqkv[:, j, :], row(name).broadcast_to([P, D])).then_inc(l_w, 16)
                    n += 1
                for j, name in ((BSELF, "bself"), (BIH, "bih"), (BHH, "bhh"), (BOUT, "bout"), (MB2, "mb2"),
                                (N1G, "n1g"), (N1B, "n1b"), (N2G, "n2g"), (N2B, "n2b")):
                    sp.dma_start(cb[:, j:j + 1], row(name).rearrange("o d -> d o"), allow_slow_non_contiguous=True).then_inc(l_w, 16)
                    n += 1
                assert n == NLW
                with sp.Fori(0, NG) as g:
                    q = l * NG + g
                    sp.dma_start(nx[:, :], xTd[:, bass.ds(g * GN, GN)]).then_inc(a_x, 16)
                    sp.wait_ge(a_dve, q * 3 + 2)
                    sp.dma_start(hTd[:, bass.ds(g * GN, GN)], nh[:, :]).then_inc(a_out, 16)
                    sp.wait_ge(a_dve, q * 3 + 3)
                    sp.dma_start(tabkv[bass.ds(g * GN, GN), :].rearrange("(t p) w -> p t w", p=P), nkv[:, :, :]).then_inc(a_out, 16)
                    hold(sp, waits_sp, a_out, q * 32 + 32)
                sp.dma_start(tabq[:, :].rearrange("(t p) d -> p t d", p=P), q_all[:, :, :]).then_inc(q_dram, 16)
                hold(sp, waits_sp, q_put, (l + 1) * (16 * NT))
                sp.wait_ge(q_first, (l + 1) * 16)
                sp.dma_start(qexp[0:EP, :].rearrange("(p t) d -> p t d", p=P)[:, 0, :], qb[:, :]).then_inc(q_done, 16)
                hold(sp, waits_sp, q_done, (l + 1) * 16)
                with sp.Fori(0, NCH // 2) as i:
                    for u in range(2):
                        c = 2 * i + u
                        sp.wait_ge(seen1, l * NCH + c + 1)
                        sp.dma_start(srcI[:, u, :], src_pt[:, bass.ds(c * C, C)]).then_inc(idx1[u], 16)
                        sp.wait_ge(done1, l * NCH + c + 1)
                        sp.dma_start(EA[:, u, :, :].rearrange("p a b -> p (a b)"),
                                     eaT[bass.ds(c, 1), :, :].rearrange("o p n -> (o p) n")).then_inc(ea_in[u], 16)
                        sp.dma_start(Q1[:, u, :, :].rearrange("p c d -> p (c d)"), chunk_rows(qexp, D, c)).then_inc(q_in[u], 16)
                hold(sp, waits_sp, f_dve, l * 5 + 10)
                with sp.Fori(0, NG) as g:
                    q = l * NG + g
                    sp.dma_start(nx[:, :], xTd[:, bass.ds(g * GN, GN)]).then_inc(b_x, 16)
                    sp.dma_start(nh[:, :], hTd[:, bass.ds(g * GN, GN)]).then_inc(b_x, 16)
                    sp.wait_ge(b_dve, q * 7 + 7)
                    sp.dma_start(xTd[:, bass.ds(g * GN, GN)], nx[:, :]).then_inc(b_out, 16)
                    hold(sp, waits_sp, b_out, q * 16 + 16)
            sp.dma_start(cb[:, NGC:NGC + 1], A["ng"].unsqueeze(1), allow_slow_non_contiguous=True).then_inc(c_x, 16)
            sp.dma_start(cb[:, NBC:NBC + 1], A["nb"].unsqueeze(1), allow_slow_non_contiguous=True).then_inc(c_x, 16)
            with sp.Fori(0, NG) as g:
                sp.dma_start(nx[:, :], xTd[:, bass.ds(g * GN, GN)]).then_inc(c_x, 16)
                sp.dma_start(nx1[:, :], x1Td[:, bass.ds(g * GN, GN)]).then_inc(c_x, 16)
                sp.wait_ge(c_dve, g * 5 + 5)
                sp.dma_start(out[bass.ds(g * GN, GN), :].rearrange("(t p) d -> p t d", p=P), nag[:, :, :]).then_inc(c_out, 16)
                hold(sp, waits_sp, c_out, g * 16 + 16)

        @block.gpsimd
        def _(pool):
            exact = dict(allow_small_or_imprecise_dtypes=True)
            nc.gpsimd.iota(iotaR[:, :], [[1, P]], base=0, channel_multiplier=0, **exact)
            nc.gpsimd.iota(iotaC[:, :], [[1, 1]], base=0, channel_multiplier=1, **exact)
            nc.gpsimd.iota(iotaPT[:, :], [[1, 1]], base=0, channel_multiplier=T, **exact)
            nc.gpsimd.iota(iotaFX[:, :], [[1, 1]], base=EP + 1, channel_multiplier=1, **exact)
            nc.gpsimd.iota(nodeE[:, :], [[P, NT]], base=EP, channel_multiplier=1, **exact).then_inc(pool_c, 1)
            pool.wait_ge(p_rp, 16)
            nc.gpsimd.indirect_dma_start(out=rpF[:, :], out_offset=None, in_=rptr[:, :],
                                         in_offset=IND(ap=firstI[:, 0:1], axis=0)).then_inc(rp_first, 16)
            pool.wait_ge(p_z, 16)
            pool.wait_ge(n0_tab, 16 * NG)
            for j in range(NT):
                nc.gpsimd.indirect_dma_start(out=s2exp[:, :], out_offset=IND(ap=startI[:, j:j + 1], axis=0),
                                             in_=s2n[:, j:j + 1], in_offset=None).then_inc(s2_put, 16)
            nc.gpsimd.indirect_dma_start(out=rfix[:, 0:W0], out_offset=None, in_=tab0[:, :],
                                         in_offset=IND(ap=firstI[:, 0:1], axis=0)).then_inc(s2_first, 16)

            pool.wait_ge(p_dve, PD_END)
            with pool.Fori(0, NCH // 2) as i:
                for u in range(2):
                    c = 2 * i + u
                    pool.wait_ge(idx0[u], 16 * i + 16)
                    hold(pool, waits_pool, done0, c + 1)
                    for t in range(C):
                        nc.gpsimd.indirect_dma_start(out=G0[:, u, t, :], out_offset=None, in_=tab0[:, :],
                                                     in_offset=IND(ap=srcI[:, u, t:t + 1], axis=0)).then_inc(got0[u], 16)

            def fix_and_fetch(st, R, o, outs, stored, rows):
                for u in range(2):
                    hold(pool, waits_pool, outs[u], stored)
                nc.gpsimd.indirect_dma_start(out=rfix[:, 0:R], out_offset=None, in_=st[:, :],
                                             in_offset=IND(ap=fixI[:, 0:1], axis=0)).then_inc(f_got, 16)
                hold(pool, waits_pool, f_dve, o * 5 + 5)
                nc.gpsimd.indirect_dma_start(out=st[:, :], out_offset=IND(ap=fixI[:, 0:1], axis=0),
                                             in_=wfix[:, 0:R], in_offset=None).then_inc(f_put, 16)
                hold(pool, waits_pool, f_put, o * 16 + 16)
                for j in range(NT):
                    nc.gpsimd.indirect_dma_start(out=rows[:, j, :], out_offset=None, in_=st[:, :],
                                                 in_offset=IND(ap=endI[:, j:j + 1], axis=0)).then_inc(rows_got, 16)

            fix_and_fetch(st0, R0, 0, st0_out, 16 * (NCH // 2 + 1), rows0)

            with pool.Fori(0, L) as l:
                hold(pool, waits_pool, a_dve, l * (NG * 3) + NG * 3)
                for j in range(NT):
                    nc.gpsimd.indirect_dma_start(out=qexp[:, :], out_offset=IND(ap=startI[:, j:j + 1], axis=0),
                                                 in_=q_all[:, j, :], in_offset=None).then_inc(q_put, 16)
                hold(pool, waits_pool, q_dram, l * 16 + 16)
                nc.gpsimd.indirect_dma_start(out=qb[:, :], out_offset=None, in_=tabq[:, :],
                                             in_offset=IND(ap=firstI[:, 0:1], axis=0)).then_inc(q_first, 16)
                hold(pool, waits_pool, a_out, l * (NG * 32) + NG * 32)
                with pool.Fori(0, NCH // 2) as i:
                    for u in range(2):
                        c = 2 * i + u
                        pool.wait_ge(idx1[u], l * (NCH // 2 * 16) + i * 16 + 16)
                        hold(pool, waits_pool, done1, l * NCH + c + 1)
                        for t in range(C):
                            nc.gpsimd.indirect_dma_start(out=G1[:, u, t, :], out_offset=None, in_=tabkv[:, :],
                                                         in_offset=IND(ap=srcI[:, u, t:t + 1], axis=0)).then_inc(got1[u], 16)
                fix_and_fetch(st1, R1, l + 1, st1_out, l * (NCH // 2 * 16) + 16 * (NCH // 2 + 1), rows1)

        @block.tensor
        def _(pe):
            mm, tr = nc.tensor.matmul, nc.tensor.transpose
            pe.wait_ge(w_in, 16 * NWIN)
            pe.wait_ge(p_dve, 2)
            tr(PS[0:D, 6, 0:D], Wa_s[:, :], ident[0:D, 0:D])
            mm(PS[:, 7, 0:1], W1raw[0:D, 0:P], enbc[:, :], start=True, stop=True)
            mm(PS[:, 7, 1:2], W1raw[0:D, P:2 * P], enbc[:, :], start=True, stop=True).then_inc(p_pe, 1)
            pe.wait_ge(p_dve, 4)
            mm(PS[0:D, 6, 64:66], WaT[:, :], attc[:, :], start=True, stop=True).then_inc(p_pe, 1)
            pe.wait_ge(p_dve, 5)
            pe.sem_inc(n0_free, 1)
            with pe.Fori(0, NG) as g:
                hold(pe, waits_pe, n0_x, 16 * g + 16)
                for j in range(TG):
                    last = tr(PSf[0:D, 2048 + j * P:2048 + (j + 1) * P], xg[:, j, :], ident[:, :])
                last.then_inc(n0_pe, 1)
                pe.wait_ge(n0_act, 4 * g + 1)
                for j in range(TG):
                    last = mm(PSf[:, j * 256:j * 256 + 132], xTg[0:D, j * P:(j + 1) * P], Wcat[:, :], start=True, stop=True)
                last.then_inc(n0_pe, 1)
            pe.wait_ge(n0_act, 4 * NG)
            pe.sem_inc(oh_used, 2)
            zb = zw[:, :].bitcast(bf16)
            mm(PS[0:NT, 0, 0:P], zb[:, 0:NT], zb[:, 0:P], start=True, stop=False, skip_group_check=True)
            with pe.Fori(0, NCH // 2) as i:
                for u in range(2):
                    c = 2 * i + u
                    pe.wait_ge(oh_ready, 2 * c + 2)
                    for t in range(C):
                        last = mm(PS[0:NT, 0, 0:P], oh[u][:, t, 0:NT], oh[u][:, t, NT:OHW], start=False, stop=False,
                                  skip_group_check=True)
                    last.then_inc(oh_used, 1)
            mm(PS[0:NT, 0, 0:P], zb[:, 0:NT], zb[:, 0:P], start=False, stop=True, skip_group_check=True).then_inc(p_pe, 1)
            pe.wait_ge(p_dve, 6)
            mm(PS[0:NT, 1, 0:1], tri[0:NT, 0:NT], cumR[0:NT, P - 1:P], start=True, stop=True).then_inc(p_pe, 1)
            pe.wait_ge(p_dve, 7)
            tr(PS[:, 2, 0:NT], endxR[0:NT, :], ident[0:NT, 0:NT])
            tr(PS[:, 3, 0:NT], degR[0:NT, :], ident[0:NT, 0:NT])
            tr(PS[0:V1, 4, 0:P], F1b[:, :], ident[:, :])
            tr(PS[0:V1, 5, 0:P], F2b[:, :], ident[:, :]).then_inc(p_pe, 1)
            pe.wait_ge(p_dve, PD_END)

            def turn(u, s):
                for j in range(4):
                    t = 8 * s + 2 * j
                    last = tr(PS[:, 0, j * P:(j + 1) * P], xe[:, u, t:t + 2, :].rearrange("p a d -> p (a d)"), ident[:, :])
                last.then_inc(m_pe, 1)

            with pe.Fori(0, NCH // 2) as i:
                for u in range(2):
                    c = 2 * i + u
                    pe.wait_ge(xn_ready, c + 1)
                    turn(u, 0)
                    for s in range(PT):
                        pe.wait_ge(m_act, 42 * c + (1 if s == 0 else 6 * s))
                        for r in range(2):
                            for kh in range(2):
                                last = mm(PS[:, 1 + 2 * r + kh, :], W1p[:, r, kh, :], xT8[:, :], start=True, stop=True)
                            last.then_inc(m_pe, 1)
                        if s < PT - 1:
                            turn(u, s + 1)
                        for r in range(2):
                            pe.wait_ge(m_act, 42 * c + 6 * s + 3 + 2 * r)
                            for kh in range(2):
                                last = mm(PS[:, 5, :], W2p[:, kh, r, :], hid8[:, r, kh, :],
                                          start=(r == 0 and kh == 0), stop=(r == 1 and kh == 1))
                        last.then_inc(m_pe, 1)

            def fix(V, o, maxes, fm):
                pe.wait_ge(f_dve, o * 5 + 1)
                if fm is not None:
                    tr(PS[0:D, 2, 0:P], fm, ident[:, :])
                tr(PS[0:V, 0, 0:P], MX[:, 0:V], ident[:, :])
                tr(PS[0:V, 1, 0:P], maxes, ident[:, :]).then_inc(f_pe, 1)
                pe.wait_ge(f_dve, o * 5 + 3)
                if fm is not None:
                    tr(PS[:, 5, 0:D], FMT[:, 1, :], ident[0:D, 0:D])
                tr(PS[:, 3, 0:V], sh[0:V, 0, :], ident[0:V, 0:V])
                tr(PS[:, 4, 0:V], sh[0:V, 1, :], ident[0:V, 0:V]).then_inc(f_pe, 1)

            fix(V0, 0, S0[:, 1, C, 1:1 + V0], S0[:, 1, C, 1 + V0:R0])
            pe.wait_ge(u_dve, 3)
            for g in range(NG):
                if g >= 2:
                    pe.wait_ge(u_act, 2 + g - 1)
                for j in range(TG):
                    last = tr(PSf[0:D, (g % 2) * 1024 + j * P:(g % 2) * 1024 + (j + 1) * P], xn0[:, g * TG + j, :], ident[:, :])
                last.then_inc(u_pe, 1)

            def means(bank, src):
                for k in range(2):
                    last = mm(PS[0:D, bank + k, 0:HN], onesD[:, :], src[:, k * HN:(k + 1) * HN], start=True, stop=True)
                return last

            with pe.Fori(0, L) as l:
                hold(pe, waits_pe, l_w, l * (16 * NLW) + 16 * NLW)
                with pe.Fori(0, NG) as g:
                    q = l * NG + g
                    hold(pe, waits_pe, a_x, q * 16 + 16)
                    means(0, nx).then_inc(a_pe, 1)
                    hold(pe, waits_pe, a_act, q * 2 + 1)
                    means(2, nsq).then_inc(a_pe, 1)
                    pe.wait_ge(a_dve, q * 3 + 2)
                    for j in range(TG):
                        last = mm(PSf[:, 2048 + j * 256:2048 + j * 256 + 3 * D], nh[:, j * P:(j + 1) * P], Wqkv[:, :], start=True, stop=True)
                    last.then_inc(a_pe, 1)
                with pe.Fori(0, NCH // 2) as i:
                    for u in range(2):
                        n = l * NCH + 2 * i + u
                        pe.wait_ge(got1[u], l * (NCH // 2 * 16 * C) + i * (16 * C) + 16 * C)
                        pe.sem_inc(seen1, 1)
                        pe.wait_ge(ea_in[u], l * (NCH // 2 * 16) + i * 16 + 16)
                        for s in range(PT):
                            b = 2 * ((PT * u + s) % 2)
                            pe.wait_ge(k_used, n * PT + s + 1)
                            pe.wait_ge(v_moved, n * PT + s + 1)
                            for k in range(2):
                                mm(PS[:, b + k, :], ident[:, :], G1[:, u, 8 * s:8 * s + 8, k * D:(k + 1) * D],
                                   start=True, stop=False, skip_group_check=True)
                            for j in range(4):
                                for k in range(2):
                                    last = mm(PS[:, b + k, P * j:P * j + P], EA[:, u, 4 * s + j, :], Wkvp[:, k * P:(k + 1) * P],
                                              start=False, stop=True, skip_group_check=True)
                            last.then_inc(kv_ready, 1)
                fix(V1, l + 1, S1[:, 1, C, H:R1], None)
                with pe.Fori(0, NG) as g:
                    q = l * NG + g
                    hold(pe, waits_pe, b_dve, q * 7 + 1)
                    for j in range(TG):
                        last = tr(PSf[0:D, j * P:(j + 1) * P], nag[:, j, :], ident[:, :])
                    last.then_inc(b_pe, 1)
                    hold(pe, waits_pe, b_act, q * 6 + 1)
                    hold(pe, waits_pe, b_x, q * 32 + 32)
                    for k in range(2):
                        cols = slice(k * HN, (k + 1) * HN)
                        mm(PS[0:D, 4 + k, 0:HN], Wn[:, 0, :], nh[:, cols], start=True, stop=True)
                        mm(PS[0:D, 2 + k, 0:HN], Wn[:, 1, :], nagT[:, cols], start=True, stop=False)
                        last = mm(PS[0:D, 2 + k, 0:HN], Wn[:, 2, :], nh[:, cols], start=False, stop=True)
                    last.then_inc(b_pe, 1)
                    hold(pe, waits_pe, b_dve, q * 7 + 3)
                    for k in range(2):
                        last = mm(PS[0:D, 6 + k, 0:HN], Wn[:, 3, :], nsl[:, k * HN:(k + 1) * HN], start=True, stop=True)
                    last.then_inc(b_pe, 1)
                    hold(pe, waits_pe, b_dve, q * 7 + 4)
                    means(0, nx1).then_inc(b_pe, 1)
                    hold(pe, waits_pe, b_act, q * 6 + 3)
                    means(2, nsq).then_inc(b_pe, 1)
                    hold(pe, waits_pe, b_dve, q * 7 + 6)
                    for kh in range(2):
                        for k in range(2):
                            last = mm(PS[:, 4 + 2 * kh + k, 0:HN], mW1s[:, kh * P:(kh + 1) * P], nrs[:, k * HN:(k + 1) * HN], start=True, stop=True)
                    last.then_inc(b_pe, 1)
                    hold(pe, waits_pe, b_act, q * 6 + 6)
                    for k in range(2):
                        for kh in range(2):
                            last = mm(PS[0:D, k, 0:HN], mW2s[:, kh, :], nhid[:, kh, k * HN:(k + 1) * HN], start=(kh == 0), stop=(kh == 1))
                    last.then_inc(b_pe, 1)
            with pe.Fori(0, NG) as g:
                hold(pe, waits_pe, c_x, g * 32 + 64)
                means(0, nx).then_inc(c_pe, 1)
                hold(pe, waits_pe, c_act, g * 4 + 1)
                means(2, nsq).then_inc(c_pe, 1)
                hold(pe, waits_pe, c_dve, g * 5 + 2)
                means(0, nsl).then_inc(c_pe, 1)
                hold(pe, waits_pe, c_act, g * 4 + 3)
                means(2, nsq).then_inc(c_pe, 1)
                hold(pe, waits_pe, c_dve, g * 5 + 4)
                for j in range(TG):
                    last = tr(PSf[:, 2048 + j * D:2048 + (j + 1) * D], nrs[:, j * P:(j + 1) * P], ident[0:D, 0:D])
                last.then_inc(c_pe, 1)

        @block.scalar
        def _(act):
            f = nc.scalar.activation
            with act.Fori(0, NG) as g:
                act.wait_ge(n0_pe, 2 * g + 1)
                f(xTg[0:D, :], PSf[0:D, 2048:2048 + GN], ACT.Copy).then_inc(n0_act, 1)
                act.wait_ge(n0_pe, 2 * g + 2)
                w = PSf[:, 0:2048].rearrange("p (t w) -> p t w", w=256)
                f(tg[:, :, :], w[:, 0:TG, 0:132], ACT.Copy).then_inc(n0_act, 1)
                f(s2n[:, bass.ds(g * TG, TG)], w[:, 0:TG, 130], ACT.Copy).then_inc(n0_act, 1)
                f(xg1[:, bass.ds(g * TG, TG)], w[:, 0:TG, 131], ACT.Copy).then_inc(n0_act, 1)

            act.wait_ge(p_dve, PD_END)
            act.sem_inc(xe_free, 2)

            def features(c, k):
                act.wait_ge(m_pe, 28 * c + k)
                f(xT8[:, :], PS[:, 0, :], ACT.Copy).then_inc(m_act, 1)

            with act.Fori(0, NCH // 2) as i:
                for u in range(2):
                    c = 2 * i + u
                    act.wait_ge(var_ready, c + 1)
                    f(sd8[:, :], rs8[:, :], ACT.Sqrt, bias=epsc[:, 0:1], scale=1.0 / D).then_inc(sqrt_ready, 1)
                    features(c, 1)
                    for s in range(PT):
                        for r in range(2):
                            act.wait_ge(m_pe, 28 * c + 4 * s + 2 + r)
                            for kh in range(2):
                                f(hid8[:, r, kh, :], PS[:, 1 + 2 * r + kh, :], ACT.Relu, bias=b1c[:, kh:kh + 1]).then_inc(m_act, 1)
                        if s < PT - 1:
                            features(c, 4 * s + 4)
                        if s == 0:
                            act.wait_ge(d0_ready, c + 1)
                            f(ee0[:, :, :], dd0[:, :, :], ACT.Exp).then_inc(e0_ready, 1)
                            act.wait_ge(ea_out, 16 * c + 16)
                        act.wait_ge(m_pe, 28 * c + (4 * s + 5 if s < PT - 1 else 28))
                        f(eaC[:, 4 * s:4 * s + 4, :].rearrange("p a b -> p (a b)"), PS[:, 5, :], ACT.Identity,
                          bias=b2c[:, 0:1]).then_inc(m_act, 1)
                    act.wait_ge(m_act, 42 * c + 42)
                    act.sem_inc(xe_free, 1)
                    act.dma_start(eaT[bass.ds(c, 1), :, :].rearrange("o p n -> (o p) n"),
                                  eaC[:, :, :].rearrange("p a b -> p (a b)")).then_inc(ea_out, 16)
                    act.wait_ge(done0, c + 3)
                    act.dma_start(chunk_rows(st0, R0, c), S0[:, u, 1:C + 1, :].rearrange("p c w -> p (c w)")).then_inc(st0_out[u], 16)

            def fix(V, o, scale):
                act.wait_ge(f_dve, o * 5 + 2)
                f(abE[0:V, :, :], ab[0:V, :, :], ACT.Exp, scale=scale).then_inc(f_act, 1)
                act.wait_ge(f_dve, o * 5 + 4)
                f(abE[:, :, 0:V], ab[:, :, 0:V], ACT.Exp, scale=scale).then_inc(f_act, 1)

            fix(V0, 0, 1.0)
            act.wait_ge(u_dve, 1)
            f(n49[4], n49[3], ACT.Sigmoid).then_inc(u_act, 1)
            act.wait_ge(u_dve, 2)
            f(n49[0], n49[7], ACT.Sqrt, bias=epsc[:, 0:1], scale=1.0 / D).then_inc(u_act, 1)
            for g in range(NG):
                act.wait_ge(u_pe, g + 1)
                f(xT0[:, g * GN:(g + 1) * GN], PSf[0:D, (g % 2) * 1024:(g % 2) * 1024 + GN], ACT.Copy).then_inc(u_act, 1)

            with act.Fori(0, L) as l:
                with act.Fori(0, NG) as g:
                    q = l * NG + g
                    act.wait_ge(a_dve, q * 3 + 1)
                    f(nsq, nxc, ACT.Square).then_inc(a_act, 1)
                    act.wait_ge(a_pe, q * 3 + 2)
                    f(two(nsd), halves(2), ACT.Sqrt, bias=epsc[0:D, 0:1]).then_inc(a_act, 1)
                with act.Fori(0, NCH // 2) as i:
                    for u in range(2):
                        n = l * NCH + 2 * i + u
                        for s in range(PT):
                            b = 2 * ((PT * u + s) % 2)
                            act.wait_ge(kv_ready, n * PT + s + 1)
                            f(G1[:, u, 8 * s:8 * s + 8, D:2 * D], PS[:, b + 1, :].rearrange("p (t d) -> p t d", t=8), ACT.Copy).then_inc(v_moved, 1)
                        act.wait_ge(d1_ready, n + 1)
                        f(ee1[:, :, :, :], dd1[:, :, :, :], ACT.Exp, scale=SCALE).then_inc(e1_ready, 1)
                        act.wait_ge(done1, n + 3)
                        act.dma_start(chunk_rows(st1, R1, 2 * i + u), S1[:, u, 1:C + 1, :].rearrange("p c w -> p (c w)")).then_inc(st1_out[u], 16)
                fix(V1, l + 1, SCALE)
                with act.Fori(0, NG) as g:
                    q = l * NG + g
                    act.wait_ge(b_pe, q * 7 + 1)
                    f(nagT, PSf[0:D, 0:GN], ACT.Copy).then_inc(b_act, 1)
                    act.wait_ge(b_pe, q * 7 + 2)
                    f(two(ngt), halves(2), ACT.Sigmoid, bias=bgc[:, 0:1]).then_inc(b_act, 1)
                    act.wait_ge(b_dve, q * 7 + 5)
                    f(nsq, nxc, ACT.Square).then_inc(b_act, 1)
                    act.wait_ge(b_pe, q * 7 + 5)
                    f(two(nsd), halves(2), ACT.Sqrt, bias=epsc[0:D, 0:1]).then_inc(b_act, 1)
                    act.wait_ge(b_pe, q * 7 + 6)
                    for kh in range(2):
                        f(two(nhid[:, kh, :]), halves(4 + 2 * kh, P), ACT.Relu, bias=mb1c[:, kh:kh + 1]).then_inc(b_act, 1)
            with act.Fori(0, NG) as g:
                for k in range(2):
                    act.wait_ge(c_dve, g * 5 + 1 + 2 * k)
                    f(nsq, nxc, ACT.Square).then_inc(c_act, 1)
                    act.wait_ge(c_pe, g * 5 + 2 + 2 * k)
                    f(two(nsd), halves(2), ACT.Sqrt, bias=epsc[0:D, 0:1]).then_inc(c_act, 1)

        @block.vector
        def _(dve):
            v = nc.vector
            tt, ts, stt, cp, red = v.tensor_tensor, v.tensor_scalar, v.scalar_tensor_tensor, v.tensor_copy, v.tensor_reduce
            scan = v.tensor_tensor_scan
            settle = dve.drain

            def along(ap, shape):
                return ap.unsqueeze(len(shape) - 1).broadcast_to(shape)

            v.memset(zeros[:, :], 0.0)
            v.memset(epsc[:, :], 1e-5)
            v.memset(onesD[:, :], 1.0 / D)
            v.memset(zw[:, :], 0.0)
            v.memset(cont[:, 0:1], 0.0)
            v.memset(W1p[:, :, :, :], 0.0)
            v.memset(W2p[:, :, :, :], 0.0)
            v.memset(s2x[:, :], 0.0).then_inc(p_dve, 1)
            dve.wait_ge(pool_c, 1)
            ts(ident[:, :], iotaR[:, :], iotaC[:, 0:1], None, ALU.is_equal)
            ts(tri[:, :], iotaR[:, :], iotaC[:, 0:1], None, ALU.is_gt).then_inc(p_dve, 1)
            dve.wait_ge(w_in, 16 * NWIN)
            ts(hiI[:, :], dstI[:, :], 7, None, ALU.logical_shift_right)
            ts(loI[:, :], dstI[:, :], 127, None, ALU.bitwise_and)
            cp(firstI[:, :], dstI[:, 0:1])
            cp(dstF[:, :], dstI[:, :])
            settle()
            cp(hiF[:, :], hiI[:, :])
            cp(loF[:, :], loI[:, :])
            tt(cont[:, 1:T], dstF[:, 1:T], dstF[:, 0:T - 1], ALU.is_equal)
            cp(F1b[:, :], dstF[:, 0:1].broadcast_to([P, V1]))
            cp(F2b[:, :], dstF[:, T - 1:T].broadcast_to([P, V1]))
            for r in range(2):
                rows = slice(r * D, (r + 1) * D)
                ts(W1p[rows, r, :, :].rearrange("p k n -> p (k n)"), W1raw[rows, :], engc[rows, 0:1], None, ALU.mult)
                cp(W2p[:, :, r, r * D:(r + 1) * D], W2raw[:, :, :])
            settle().then_inc(p_dve, 1)
            dve.wait_ge(p_pe, 1)
            cp(WaT[:, :], PS[0:D, 6, 0:D])
            tt(b1c[:, :], PS[:, 7, 0:2], eb1c[:, :], ALU.add).then_inc(p_dve, 1)
            dve.wait_ge(p_pe, 2)
            cp(Wcat[:, 128:129], PS[0:D, 6, 64:65])
            cp(Wcat[:, 130:131], PS[0:D, 6, 65:66]).then_inc(p_dve, 1)
            with dve.Fori(0, NCH // 2) as i:
                for u in range(2):
                    c = 2 * i + u
                    dve.wait_ge(oh_used, c + 1)
                    tt(oh[u][:, :, 0:NT], iotaR[:, 0:NT].unsqueeze(1).broadcast_to([P, C, NT]),
                       along(hiF[:, bass.ds(c * C, C)], [P, C, NT]), ALU.is_equal).then_inc(oh_ready, 1)
                    tt(oh[u][:, :, NT:OHW], iotaR[:, :].unsqueeze(1).broadcast_to([P, C, P]),
                       along(loF[:, bass.ds(c * C, C)], [P, C, P]), ALU.is_equal).then_inc(oh_ready, 1)
            dve.wait_ge(p_pe, 3)
            cp(degR[0:NT, :], PS[0:NT, 0, 0:P])
            settle()
            scan(cumR[0:NT, :], zeros[0:NT, 0:P], degR[0:NT, :], 0.0, ALU.add, ALU.add).then_inc(p_dve, 1)
            dve.wait_ge(p_pe, 4)
            cp(baseC[0:NT, :], PS[0:NT, 1, 0:1])
            settle()
            ts(endxR[0:NT, :], cumR[0:NT, :], baseC[0:NT, 0:1], None, ALU.add).then_inc(p_dve, 1)
            dve.wait_ge(p_pe, 5)
            ts(lastF[:, :], PS[:, 2, 0:NT], -1.0, None, ALU.add)
            cp(degn[:, :], PS[:, 3, 0:NT])
            settle()
            ts(neF[:, :], degn[:, :], 0.0, None, ALU.is_gt)
            tt(tmpN[:, :], lastF[:, :], degn[:, :], ALU.subtract)
            settle()
            ts(firstF[:, :], tmpN[:, :], 1.0, None, ALU.add)
            settle()
            stt(tmpN[:, :], lastF[:, :], -float(EP), neF[:, :], ALU.add, ALU.mult)
            settle()
            ts(endI[:, :], tmpN[:, :], float(EP), None, ALU.add)
            settle()
            tt(tmpN[:, :], firstF[:, :], nodeE[:, :], ALU.subtract)
            settle()
            tt(tmpN[:, :], tmpN[:, :], neF[:, :], ALU.mult)
            settle()
            tt(startI[:, :], tmpN[:, :], nodeE[:, :], ALU.add)
            cp(rp_s[:, :, 0], firstF[:, :])
            cp(rp_s[:, :, 1], lastF[:, :])
            settle().then_inc(p_dve, 1)
            cp(rowF[0:V1, :], PS[0:V1, 4, 0:P])
            cp(rowL[0:V1, :], PS[0:V1, 5, 0:P])
            v.memset(gF[0:V1, 0:1], 0.0)
            settle()
            tt(gF[0:V1, 1:P], rowF[0:V1, 1:P], rowL[0:V1, 0:P - 1], ALU.is_equal)
            settle()
            tt(rowF[0:V1, :], rowF[0:V1, :], rowL[0:V1, :], ALU.is_equal)
            settle()
            tt(gF[0:V1, :], gF[0:V1, :], rowF[0:V1, :], ALU.mult)
            settle()
            ts(gmask[:, :], gF[0:V1, :], -1.0, BIG, ALU.add, ALU.mult)
            dve.wait_ge(rp_first, 16)
            tt(vF[:, 0:1], rpF[:, 0:1], iotaPT[:, :], ALU.is_lt)
            ts(vF[:, 1:2], iotaPT[:, :], float(T), None, ALU.add)
            tt(vF[:, 2:3], rpF[:, 1:2], iotaFX[:, :], ALU.subtract)
            settle()
            tt(vF[:, 1:2], rpF[:, 1:2], vF[:, 1:2], ALU.is_lt)
            settle()
            tt(vF[:, 0:1], vF[:, 0:1], vF[:, 1:2], ALU.mult)
            settle()
            tt(vF[:, 0:1], vF[:, 0:1], vF[:, 2:3], ALU.mult)
            settle()
            tt(fixI[:, :], vF[:, 0:1], iotaFX[:, :], ALU.add)
            v.memset(S0[:, :, :, :], 0.0)
            settle().then_inc(p_dve, 1)
            dve.sem_inc(seen0, 2)
            dve.sem_inc(done0, 2)

            with dve.Fori(0, NCH // 2) as i:
                for u in range(2):
                    c = 2 * i + u
                    X = xe[:, u, :, :]
                    S, Sb = S0[:, u, :, :], S0[:, 1 - u, :, :]
                    G = G0[:, u, :, :]
                    sq = S[:, 1:C + 1, R0 - D:R0]
                    dve.wait_ge(xe_in[u], 16 * i + 16)
                    dve.wait_ge(st0_out[u], 16 * i + 16)
                    red(mu8[:, :], X, AX.X, ALU.add)
                    settle()
                    ts(mu8[:, :], mu8[:, :], 1.0 / D, None, ALU.mult)
                    settle()
                    tt(X, X, along(mu8[:, :], [P, C, D]), ALU.subtract)
                    settle()
                    tt(sq, X, X, ALU.mult)
                    settle()
                    red(rs8[:, :], sq, AX.X, ALU.add).then_inc(var_ready, 1)
                    cp(contC[:, :], cont[:, bass.ds(c * C, C)])
                    cp(s2x[:, 0:1], s2x[:, C:C + 1])
                    cp(S[:, 0, :], Sb[:, C, :])
                    settle()
                    ts(maskC[:, :], contC[:, :], -1.0, BIG, ALU.add, ALU.mult)
                    dve.wait_ge(in0[u], 32 * i + 32)
                    scan(s2x[:, 1:C + 1], contC[:, :], s2C[:, u, :], s2x[:, 0:1], ALU.mult, ALU.add)
                    dve.wait_ge(sqrt_ready, c + 1)
                    v.reciprocal(rs8[:, :], sd8[:, :])
                    settle()
                    tt(X, X, along(rs8[:, :], [P, C, D]), ALU.mult).then_inc(xn_ready, 1)
                    dve.wait_ge(got0[u], i * (16 * C) + 16 * C)
                    dve.sem_inc(seen0, 1)
                    tt(al0[:, :], G[:, :, 2 * D], ewC[:, u, :], ALU.mult)
                    tt(uw0[:, :], G[:, :, 2 * D + 1], ewC[:, u, :], ALU.mult)
                    settle()
                    tt(al0[:, :], al0[:, :], s2x[:, 1:C + 1], ALU.add)
                    settle()
                    stt(al0[:, :], al0[:, :], 0.01, al0[:, :], ALU.mult, ALU.max)
                    settle()
                    scan(S[:, 1:C + 1, 0], maskC[:, :], al0[:, :], S[:, 0, 0:1], ALU.add, ALU.max)
                    settle()
                    tt(dd0[:, 0, :], S[:, 0:C, 0], maskC[:, :], ALU.add)
                    tt(dd0[:, 1, :], al0[:, :], S[:, 1:C + 1, 0], ALU.subtract)
                    settle()
                    tt(dd0[:, 0, :], dd0[:, 0, :], S[:, 1:C + 1, 0], ALU.subtract).then_inc(d0_ready, 1)
                    tt(G[:, :, D:2 * D], G[:, :, D:2 * D], along(ewC[:, u, :], [P, C, D]), ALU.mult)
                    settle()
                    scan(S[:, 1:C + 1, 2 + D], contC[:, :], uw0[:, :], S[:, 0, 2 + D:3 + D], ALU.mult, ALU.add)
                    for k in range(D):
                        scan(S[:, 1:C + 1, 3 + D + k], maskC[:, :], G[:, :, D + k], S[:, 0, 3 + D + k:4 + D + k], ALU.add, ALU.max)
                    dve.wait_ge(e0_ready, c + 1)
                    tt(G[:, :, 0:D], G[:, :, 0:D], along(ee0[:, 1, :], [P, C, D]), ALU.mult)
                    scan(S[:, 1:C + 1, 1], ee0[:, 0, :], ee0[:, 1, :], S[:, 0, 1:2], ALU.mult, ALU.add)
                    settle()
                    for k in range(D):
                        last = scan(S[:, 1:C + 1, 2 + k], ee0[:, 0, :], G[:, :, k], S[:, 0, 2 + k:3 + k], ALU.mult, ALU.add)
                    settle().then_inc(done0, 1)

            def fix(V, o, state, spread, copied, fm):
                spread()
                settle().then_inc(f_dve, 1)
                dve.wait_ge(f_pe, o * 2 + 1)
                cp(MXT[0:V, :], PS[0:V, 0, 0:P])
                cp(VT[0:V, :], PS[0:V, 1, 0:P])
                if fm:
                    cp(FMT[:, 0, :], PS[0:D, 2, 0:P])
                settle()
                scan(MT[0:V, :], gmask[0:V, :], MXT[0:V, :], -BIG, ALU.add, ALU.max)
                if fm:
                    v.memset(FMT[:, 1, 0:1], -BIG)
                    settle()
                    scan(FMT[:, 1, 1:P], gmask[0:D, 0:P - 1], FMT[:, 0, 0:P - 1], -BIG, ALU.add, ALU.max)
                settle()
                tt(ab[0:V, 0, 1:P], MT[0:V, 0:P - 1], gmask[0:V, 1:P], ALU.add)
                v.memset(ab[0:V, 0, 0:1], -BIG)
                tt(ab[0:V, 1, :], MXT[0:V, :], MT[0:V, :], ALU.subtract)
                settle()
                tt(ab[0:V, 0, 1:P], ab[0:V, 0, 1:P], MT[0:V, 1:P], ALU.subtract).then_inc(f_dve, 1)
                dve.wait_ge(f_act, o * 2 + 1)
                tt(VT[0:V, :], VT[0:V, :], abE[0:V, 1, :], ALU.mult)
                v.memset(sh[0:V, 0, 0:1], -BIG)
                v.memset(sh[0:V, 1, 0:1], 0.0)
                cp(sh[0:V, 0, 1:P], MT[0:V, 0:P - 1])
                settle()
                scan(sh[0:V, 1, 1:P], abE[0:V, 0, 0:P - 1], VT[0:V, 0:P - 1], 0.0, ALU.mult, ALU.add)
                settle().then_inc(f_dve, 1)
                dve.wait_ge(f_pe, o * 2 + 2)
                dve.wait_ge(f_got, o * 16 + 16)
                copied()
                settle()
                tt(wide[:, 0, 0:V], MX[:, 0:V], PS[:, 3, 0:V], ALU.max)
                cp(wide[:, 1, 0:V], PS[:, 4, 0:V])
                settle()
                tt(ab[:, 0, 0:V], PS[:, 3, 0:V], wide[:, 0, 0:V], ALU.subtract)
                tt(ab[:, 1, 0:V], MX[:, 0:V], wide[:, 0, 0:V], ALU.subtract)
                settle().then_inc(f_dve, 1)
                dve.wait_ge(f_act, o * 2 + 2)
                return

            def join(V, first, nmax, R, fm):
                tt(wide[:, 1, 0:V], wide[:, 1, 0:V], abE[:, 0, 0:V], ALU.mult)
                tt(wfix[:, first:first + V], rfix[:, first:first + V], abE[:, 1, 0:V], ALU.mult)
                cp(wfix[:, 0:nmax], wide[:, 0, 0:nmax])
                if fm:
                    tt(wfix[:, R - D:R], rfix[:, R - D:R], PS[:, 5, 0:D], ALU.max)
                settle()
                tt(wfix[:, first:first + V], wfix[:, first:first + V], wide[:, 1, 0:V], ALU.add)
                settle().then_inc(f_dve, 1)

            def spread0(row):
                cp(MX[:, 0:V0 - 1], row[:, 0:1].broadcast_to([P, V0 - 1]))
                v.memset(MX[:, V0 - 1:V0], 0.0)

            fix(V0, 0, None, lambda: spread0(S0[:, 1, C, :]), lambda: spread0(rfix), True)
            join(V0, 1, 1, R0, True)

            dve.wait_ge(rows_got, 16 * NT)
            ts(n49[0], rows0[:, :, 1], 1e-30, None, ALU.max)
            ts(n49[3], degn[:, :], 1.0, None, ALU.max)
            tt(tp0, rows0[:, :, 3 + D:R0], gw2r[:, :].unsqueeze(1).broadcast_to([P, NT, D]), ALU.mult)
            settle()
            v.reciprocal(n49[1], n49[0])
            v.reciprocal(n49[5], n49[3])
            red(n49[2], tp0, AX.X, ALU.add)
            settle()
            tt(n49[3], rows0[:, :, 2 + D], n49[5], ALU.mult)
            settle()
            tt(n49[3], n49[3], n49[2], ALU.add)
            settle()
            tt(n49[3], n49[3], xg1[:, :], ALU.add).then_inc(u_dve, 1)
            dve.wait_ge(u_act, 1)
            tt(n49[5], n49[4], n49[1], ALU.mult)
            dve.wait_ge(u_x, 16)
            settle()
            tt(tq0, rows0[:, :, 2:2 + D], along(n49[5], [P, NT, D]), ALU.mult)
            settle()
            tt(xn0, xn0, tq0, ALU.add)
            settle()
            red(n49[6], xn0, AX.X, ALU.add)
            settle()
            ts(n49[6], n49[6], 1.0 / D, None, ALU.mult)
            settle()
            tt(xn0, xn0, along(n49[6], [P, NT, D]), ALU.subtract)
            settle()
            tt(tp0, xn0, xn0, ALU.mult)
            settle()
            red(n49[7], tp0, AX.X, ALU.add).then_inc(u_dve, 1)
            dve.wait_ge(u_act, 2)
            v.reciprocal(n49[1], n49[0])
            settle()
            tt(xn0, xn0, along(n49[1], [P, NT, D]), ALU.mult).then_inc(u_dve, 1)

            dve.wait_ge(u_out, 32)
            dve.wait_ge(ea_out, 16 * (NCH + 1))
            v.memset(Wkvp[:, :], 0.0)
            v.memset(S1[:, :, :, :], 0.0)
            v.memset(qlb[:, :], 0.0)
            settle().then_inc(l_b, 1)
            dve.sem_inc(done1, 2)
            dve.sem_inc(seen1, 2)
            dve.sem_inc(k_used, 2)
            dve.sem_inc(v_moved, 2)

            def norm(out_, g_, b_):
                v.reciprocal(nrs, nsd)
                settle()
                tt(nxc, nxc, nrs, ALU.mult)
                settle()
                if g_ is None:
                    return
                return ts(out_, nxc, cb[:, g_:g_ + 1], cb[:, b_:b_ + 1], ALU.mult, ALU.add)

            with dve.Fori(0, L) as l:
                dve.wait_ge(l_w, l * (16 * NLW) + 16 * NLW)
                tt(bqkv[:, 1:3, :], bqkv[:, 1:3, :], bqkv[:, 3:5, :], ALU.add)
                tt(bgc[:, :], cb[:, BIH:BIH + 1], cb[:, BHH:BHH + 1], ALU.add)
                settle().then_inc(l_b, 1)
                with dve.Fori(0, NG) as g:
                    q = l * NG + g
                    dve.wait_ge(a_x, q * 16 + 16)
                    dve.wait_ge(a_pe, q * 3 + 1)
                    tt(two(nxc), two(nx), halves(0), ALU.subtract).then_inc(a_dve, 1)
                    dve.wait_ge(a_act, q * 2 + 2)
                    norm(nh, N1G, N1B).then_inc(a_dve, 1)
                    dve.wait_ge(a_pe, q * 3 + 3)
                    w = PSf[:, 2048:4096].rearrange("p (t w) -> p t w", w=256)
                    tt(nkv[:, :, :], w[:, 0:TG, D:3 * D], bqkv[:, 1:3, :].rearrange("p a d -> p (a d)").unsqueeze(1).broadcast_to([P, TG, 2 * D]), ALU.add)
                    tt(q_all[:, bass.ds(g * TG, TG), :], w[:, 0:TG, 0:D], bqkv[:, 0, :].unsqueeze(1).broadcast_to([P, TG, D]), ALU.add)
                    settle().then_inc(a_dve, 1)
                with dve.Fori(0, NCH // 2) as i:
                    for u in range(2):
                        c = 2 * i + u
                        n = l * NCH + c
                        S, Sb = S1[:, u, :, :], S1[:, 1 - u, :, :]
                        Q, Qb = Q1[:, u, :, :], Q1[:, 1 - u, :, :]
                        G = G1[:, u, :, :]
                        cp(contC[:, :], cont[:, bass.ds(c * C, C)])
                        dve.wait_ge(st1_out[u], l * (16 * (NCH // 2)) + i * 16 + 16)
                        cp(S[:, 0, :], Sb[:, C, :])
                        settle()
                        ts(maskC[:, :], contC[:, :], -1.0, BIG, ALU.add, ALU.mult)
                        dve.wait_ge(q_in[u], l * (16 * (NCH // 2)) + i * 16 + 16)
                        cp(ql[:, :], qlb[:, :])
                        settle()
                        for k in range(D):
                            scan(Q[:, :, k], contC[:, :], Q[:, :, k], ql[:, k:k + 1], ALU.mult, ALU.add)
                        settle()
                        cp(qlb[:, :], Q[:, C - 1, :])
                        for s in range(PT):
                            b = 2 * ((PT * u + s) % 2)
                            dve.wait_ge(kv_ready, n * PT + s + 1)
                            tt(PR[:, 8 * s:8 * s + 8, :], PS[:, b, :].rearrange("p (t d) -> p t d", t=8),
                               Q[:, 8 * s:8 * s + 8, :], ALU.mult).then_inc(k_used, 1)
                        settle()
                        red(al1[:, :, :], PR[:, :, :].rearrange("p t (h d) -> p t h d", h=H), AX.X, ALU.add)
                        settle()
                        for h in range(H):
                            scan(S[:, 1:C + 1, h], maskC[:, :], al1[:, :, h], S[:, 0, h:h + 1], ALU.add, ALU.max)
                        settle()
                        tt(dd1[:, 0, :, :], S[:, 0:C, 0:H], along(maskC[:, :], [P, C, H]), ALU.add)
                        tt(dd1[:, 1, :, :], al1[:, :, :], S[:, 1:C + 1, 0:H], ALU.subtract)
                        settle()
                        tt(dd1[:, 0, :, :], dd1[:, 0, :, :], S[:, 1:C + 1, 0:H], ALU.subtract).then_inc(d1_ready, 1)
                        dve.wait_ge(e1_ready, n + 1)
                        vals = G[:, :, D:2 * D].rearrange("p t (h d) -> p t h d", h=H)
                        tt(vals, vals, along(ee1[:, 1, :, :], [P, C, H, HD]), ALU.mult)
                        for h in range(H):
                            scan(S[:, 1:C + 1, H + h], ee1[:, 0, :, h], ee1[:, 1, :, h], S[:, 0, H + h:H + h + 1], ALU.mult, ALU.add)
                        settle()
                        for k in range(D):
                            scan(S[:, 1:C + 1, 2 * H + k], ee1[:, 0, :, k // HD], G[:, :, D + k], S[:, 0, 2 * H + k:2 * H + k + 1], ALU.mult, ALU.add)
                        settle().then_inc(done1, 1)

                def spread1(row):
                    cp(MX[:, 0:H], row[:, 0:H])
                    cp(MX[:, H:V1].rearrange("p (h d) -> p h d", h=H), along(row[:, 0:H], [P, H, HD]))

                fix(V1, l + 1, None, lambda: spread1(S1[:, 1, C, :]), lambda: spread1(rfix), False)
                join(V1, H, H, R1, False)
                dve.wait_ge(rows_got, l * (16 * NT) + 32 * NT)
                ts(rden[:, :, :], rows1[:, :, H:2 * H], 1e-16, None, ALU.add)
                settle()
                v.reciprocal(rden[:, :, :], rden[:, :, :])
                settle()
                with dve.Fori(0, NG) as g:
                    q = l * NG + g
                    tt(nag[:, :, :].rearrange("p t (h d) -> p t h d", h=H),
                       rows1[:, bass.ds(g * TG, TG), 2 * H:R1].rearrange("p t (h d) -> p t h d", h=H),
                       rden[:, bass.ds(g * TG, TG), :].unsqueeze(3).broadcast_to([P, TG, H, HD]), ALU.mult).then_inc(b_dve, 1)
                    dve.wait_ge(b_pe, q * 7 + 2)
                    stt(two(nsl), halves(4), cb[:, BSELF:BSELF + 1], two(nagT), ALU.add, ALU.subtract).then_inc(b_dve, 1)
                    settle()
                    dve.wait_ge(b_act, q * 6 + 2)
                    tt(nsl, nsl, ngt, ALU.mult)
                    settle()
                    tt(nsl, nsl, nagT, ALU.add).then_inc(b_dve, 1)
                    dve.wait_ge(b_x, q * 32 + 32)
                    dve.wait_ge(b_pe, q * 7 + 3)
                    stt(two(nx1), halves(6), cb[:, BOUT:BOUT + 1], two(nx), ALU.add, ALU.add).then_inc(b_dve, 1)
                    settle()
                    dve.wait_ge(b_pe, q * 7 + 4)
                    tt(two(nxc), two(nx1), halves(0), ALU.subtract).then_inc(b_dve, 1)
                    dve.wait_ge(b_act, q * 6 + 4)
                    norm(nrs, N2G, N2B).then_inc(b_dve, 1)
                    dve.wait_ge(b_pe, q * 7 + 7)
                    stt(two(nx), halves(0), cb[:, MB2:MB2 + 1], two(nx1), ALU.add, ALU.add).then_inc(b_dve, 1)
                    settle()

            with dve.Fori(0, NG) as g:
                dve.wait_ge(c_x, g * 32 + 64)
                dve.wait_ge(c_pe, g * 5 + 1)
                tt(two(nxc), two(nx), halves(0), ALU.subtract).then_inc(c_dve, 1)
                dve.wait_ge(c_act, g * 4 + 2)
                norm(nsl, NGC, NBC)
                settle()
                tt(nsl, nsl, nx1, ALU.add).then_inc(c_dve, 1)
                settle()
                dve.wait_ge(c_pe, g * 5 + 3)
                tt(two(nxc), two(nsl), halves(0), ALU.subtract).then_inc(c_dve, 1)
                dve.wait_ge(c_act, g * 4 + 4)
                v.reciprocal(ngt, nsd)
                settle()
                tt(nrs, nxc, ngt, ALU.mult).then_inc(c_dve, 1)
                dve.wait_ge(c_pe, g * 5 + 5)
                cp(nag[:, :, :].rearrange("p t d -> p (t d)"), PSf[:, 2048:2048 + TG * D]).then_inc(c_dve, 1)

        first.close()
        second.close()


_INS = {'x': 'x', 'src': 'src', 'dst': 'dst', 'edge_attr_64': 'edge_attr_64', 'edge_weight1': 'edge_weight1',
        'Wa': 'L0_gnn_Wa', 'att_w': 'L0_gnn_att_w', 'Wg': 'L0_gnn_Wg', 'gate_w': 'L0_gnn_gate_w'}
_INS.update({n: 'L1_gnn_' + n for n in (
    'eng', 'enb', 'eW1', 'eb1', 'eW2', 'eb2', 'Wq', 'bq', 'Wkn', 'bkn', 'Wke', 'bke', 'Wvn', 'bvn', 'Wve', 'bve',
    'Wself', 'bself', 'Wih', 'bih', 'Whh', 'bhh', 'Wout', 'bout', 'n1g', 'n1b', 'n2g', 'n2b',
    'mW1', 'mb1', 'mW2', 'mb2', 'ng', 'nb')})


def kernel(**inputs):
    import numpy as _np
    import concourse.bacc as _bacc
    from concourse import mybir as _mybir
    from concourse.bass_utils import run_bass_kernel_spmd as _run

    nc = _bacc.Bacc("TRN2", target_bir_lowering=False, num_devices=1)
    rows = {'x': (NP, 0), 'src': (EP, 0), 'dst': (EP, N), 'edge_attr_64': (EP, 0), 'edge_weight1': (EP, 0)}
    arrays, aps = {}, {}
    for short, name in _INS.items():
        a = _np.ascontiguousarray(inputs[name])
        if short in rows:
            n, fill = rows[short]
            padded = _np.full((n,) + a.shape[1:], fill, a.dtype)
            padded[:a.shape[0]] = a
            a = padded
        arrays[f"in_{short}"] = a
        aps[short] = nc.dram_tensor(f"in_{short}", a.shape, _mybir.dt.from_np(a.dtype), kind="ExternalInput").ap()
    out = nc.dram_tensor("out_0", (NP, D), _mybir.dt.float32, kind="ExternalOutput").ap()
    build(nc, aps, out)
    r = _run(nc, [arrays], core_ids=[0])
    return r.results[0]["out_0"][:N]
```

```python
import concourse.bass as bass
from concourse import mybir
from contextlib import ExitStack

P = 128
N = 6250
E = 200000
D = 64
H = 8
HD = D // H
L = 3
HID = 4 * D
C = 56
NCH = 28
T = C * NCH
EP = P * T
NT = 49
NPR = (NT + 1) // 2
NP = 2 * NPR * P
NW = NPR * P
TG = 7
NG = NT // TG
GN = TG * P
BLK = [(512 * k, min(512, NW - 512 * k)) for k in range(-(-NW // 512))]
NB = len(BLK)
PAIRS = C // 2
PT = C // 8
BIG = 1e30
R0 = 3 + 2 * D
V0 = 2 + D
R1 = 2 * H + D
V1 = H + D
W0 = 2 * D + 3
SCALE = float(HD) ** -0.5
NWIN = 18
NLW = 49
A_DVE = 3 * NB
B_DVE = 6 * NB
PD_RP, PD_END = 8, 9
BSELF, BIH, BHH, BOUT, MB2, N1G, N1B, N2G, N2B, NGC, NBC = range(11)


def build(nc, A, out):
    f32, bf16, i32 = mybir.dt.float32, mybir.dt.bfloat16, mybir.dt.int32
    ALU, ACT, AX = mybir.AluOpType, mybir.ActivationFunctionType, mybir.AxisListType
    IND = bass.IndirectOffsetOnAxis
    ctx = ExitStack()

    def dram(name, shape, dt=f32):
        return nc.dram_tensor(name, shape, dt, kind="Internal").ap()

    tab0 = dram("tab0", (NT * P, W0))
    tabkv = dram("tabkv", (NP, 2 * D))
    tabq = dram("tabq", (NP, D))
    s2exp = dram("s2exp", (EP + NP, 1))
    qexp = dram("qexp", (EP + NP, D))
    st0 = dram("st0", (EP + 1 + P, R0))
    st1 = dram("st1", (EP + 1 + P, R1))
    eaT = dram("eaT", (NCH, P, PAIRS * P))
    xTd = dram("xTd", (P, NW))
    x1Td = dram("x1Td", (P, NW))
    hTd = dram("hTd", (P, NW))
    rptr = dram("rptr", (NT * P, 2))

    def chunk_rows(t, width, c):
        return t[0:EP, :].rearrange("(p t) w -> p (t w)", p=P)[:, bass.ds(c * (C * width), C * width)]

    src_pt = A["src"].rearrange("(p t) -> p t", p=P)
    ew_pt = A["edge_weight1"].rearrange("(p t) o -> p (t o)", p=P)

    with ctx:
        def sbx(stack):
            return lambda name, shape, dt=f32: stack.enter_context(nc.sbuf_tensor(name, shape, dt))

        def sem(name):
            return ctx.enter_context(nc.semaphore(name))

        sb = sbx(ctx)
        ident = sb("ident", [P, P])
        onesD = sb("onesD", [P, P])
        cont = sb("cont", [P, T])
        srcI = sb("srcI", [P, 2, C], i32)
        firstI = sb("firstI", [P, 1], i32)
        endI = sb("endI", [P, NT], i32)
        startI = sb("startI", [P, NT], i32)
        fixI = sb("fixI", [P, 1], i32)
        gmask = sb("gmask", [V1, P])
        contC = sb("contC", [P, C])
        maskC = sb("maskC", [P, C])
        zeros = sb("zeros", [P, 896])
        iotaFX = sb("iotaFX", [P, 1])
        epsc = sb("epsc", [P, 1])
        MX = sb("MX", [P, V1])
        MXT = sb("MXT", [V1, P])
        MT = sb("MT", [V1, P])
        VT = sb("VT", [V1, P])
        sh = sb("sh", [V1, 2, P])
        ab = sb("ab", [P, 2, P])
        abE = sb("abE", [P, 2, P])
        FMT = sb("FMT", [D, 2, P])
        wide = sb("wide", [P, 2, V1])
        rfix = sb("rfix", [P, R0])
        wfix = sb("wfix", [P, R0])
        PS = ctx.enter_context(nc.psum_tensor("PS", [P, 8, 512], f32))
        PSf = PS[:, :, :].rearrange("p b n -> p (b n)")

        w_in = sem("w_in")
        pool_c = sem("pool_c")
        p_dve = sem("p_dve")
        p_pe = sem("p_pe")
        p_rp = sem("p_rp")
        rp_first = sem("rp_first")
        p_z = sem("p_z")
        oh_ready = sem("oh_ready")
        oh_used = sem("oh_used")
        waits_sp, waits_pool, waits_pe = sem("waits_sp"), sem("waits_pool"), sem("waits_pe")
        n0_x, n0_pe, n0_act, n0_tab, n0_free = (sem(n) for n in ("n0_x", "n0_pe", "n0_act", "n0_tab", "n0_free"))
        s2_put = sem("s2_put")
        s2_first = sem("s2_first")
        idx0 = [sem(f"idx0_{u}") for u in range(2)]
        in0 = [sem(f"in0_{u}") for u in range(2)]
        xe_in = [sem(f"xe_in{u}") for u in range(2)]
        got0 = [sem(f"got0_{u}") for u in range(2)]
        seen0 = sem("seen0")
        done0 = sem("done0")
        xe_free = sem("xe_free")
        d0_ready, e0_ready = sem("d0_ready"), sem("e0_ready")
        var_ready, sqrt_ready, xn_ready = sem("var_ready"), sem("sqrt_ready"), sem("xn_ready")
        st0_out = [sem(f"st0_out{u}") for u in range(2)]
        m_pe, m_act = sem("m_pe"), sem("m_act")
        ea_out = sem("ea_out")
        zq = sem("zq")
        f_pe, f_dve, f_act, f_got, f_put = (sem(n) for n in ("f_pe", "f_dve", "f_act", "f_got", "f_put"))
        rows_got = sem("rows_got")
        u_x, u_dve, u_act, u_pe, u_out = (sem(n) for n in ("u_x", "u_dve", "u_act", "u_pe", "u_out"))
        l_w = sem("l_w")
        l_b = sem("l_b")
        a_x, a_pe, a_dve, a_act, h_out = (sem(n) for n in ("a_x", "a_pe", "a_dve", "a_act", "h_out"))
        a_out = [sem(f"a_out{k}") for k in range(2)]
        q_dram, q_put, q_first, q_done = (sem(n) for n in ("q_dram", "q_put", "q_first", "q_done"))
        idx1 = [sem(f"idx1_{u}") for u in range(2)]
        q_in = [sem(f"q_in{u}") for u in range(2)]
        ea_in = [sem(f"ea_in{u}") for u in range(2)]
        got1 = [sem(f"got1_{u}") for u in range(2)]
        seen1 = sem("seen1")
        done1 = sem("done1")
        kv_ready = sem("kv_ready")
        k_used = sem("k_used")
        v_moved = sem("v_moved")
        d1_ready, e1_ready = sem("d1_ready"), sem("e1_ready")
        st1_out = [sem(f"st1_out{u}") for u in range(2)]
        b_x, b_pe, b_dve, b_act, b_out = (sem(n) for n in ("b_x", "b_pe", "b_dve", "b_act", "b_out"))
        c_x, c_pe, c_dve, c_act, c_out = (sem(n) for n in ("c_x", "c_pe", "c_dve", "c_act", "c_out"))

        first = ExitStack()
        sb = sbx(first)
        Wcat = sb("Wcat", [D, 132])
        Wa_s = sb("Wa_s", [D, D])
        WaT = sb("WaT", [D, D])
        attc = sb("attc", [D, 2])
        gw2r = sb("gw2r", [P, D])
        W1raw = sb("W1raw", [P, HID])
        engc = sb("engc", [P, 1])
        enbc = sb("enbc", [D, 1])
        eb1c = sb("eb1c", [P, 2])
        b1c = sb("b1c", [P, 2])
        b2c = sb("b2c", [P, 1])
        W1p = sb("W1p", [P, 2, 2, P])
        W2p = sb("W2p", [P, 2, 2, P])
        W2raw = sb("W2raw", [P, 2, D])
        s2n = sb("s2n", [P, NT])
        xg1 = sb("xg1", [P, NT])
        degn = sb("degn", [P, NT])
        G0 = sb("G0", [P, 2, C, W0])
        S0 = sb("S0", [P, 2, C + 1, R0])
        xe = sb("xe", [P, 2, C, D])
        eaC = sb("eaC", [P, PAIRS, P])
        xT8 = sb("xT8", [P, 512])
        hid8 = sb("hid8", [P, 2, 2, 512])
        ewC = sb("ewC", [P, 2, C])
        s2C = sb("s2C", [P, 2, C])
        s2x = sb("s2x", [P, C + 1])
        al0 = sb("al0", [P, C])
        uw0 = sb("uw0", [P, C])
        dd0 = sb("dd0", [P, 2, C])
        ee0 = sb("ee0", [P, 2, C])
        mu8 = sb("mu8", [P, C])
        sd8 = sb("sd8", [P, C])
        rs8 = sb("rs8", [P, C])
        G0f = G0[:, :, :, :].rearrange("p u c w -> p (u c w)")
        S0f = S0[:, :, :, :].rearrange("p u c w -> p (u c w)")
        xef = xe[:, :, :, :].rearrange("p u c w -> p (u c w)")
        eaf = eaC[:, :, :].rearrange("p a b -> p (a b)")
        OHW = NT + P
        dstI, hiI, loI = (xef[:, 2460 + k * T:2460 + (k + 1) * T].bitcast(i32) for k in range(3))
        dstF, hiF, loF = (S0f[:, C * OHW + k * T:C * OHW + (k + 1) * T] for k in range(3))
        oh = [S0f[:, u * (C * OHW // 2):(u + 1) * (C * OHW // 2)].bitcast(bf16)
              .rearrange("p (c w) -> p c w", c=C) for u in range(2)]
        at = [0]

        def eview(n):
            at[0] += n
            return eaf[:, at[0] - n:at[0]]

        iotaR = eview(P)
        iotaC = eview(1)
        iotaPT = eview(1)
        nodeE = eview(NT)
        tri = eview(P)
        degR = eview(P)
        cumR = eview(P)
        baseC = eview(1)
        endxR = eview(P)
        lastF = eview(NT)
        firstF = eview(NT)
        neF = eview(NT)
        tmpN = eview(NT)
        F1b = eview(V1)
        F2b = eview(V1)
        rowF = eview(P)
        rowL = eview(P)
        gF = eview(P)
        rpF = eview(2)
        vF = eview(4)
        rp_s = eview(2 * NT).rearrange("p (t o) -> p t o", o=2)
        zw = eview(P)
        xg = xef[:, 0:TG * D].rearrange("p (t d) -> p t d", t=TG)
        xTg = xef[:, 512:512 + GN]
        tg = xef[:, 1536:1536 + TG * 132].rearrange("p (t w) -> p t w", t=TG)
        rows0 = G0f[:, 0:NT * R0].rearrange("p (t w) -> p t w", t=NT)
        xn0p = S0f[:, 0:2 * NPR * D]
        xn0 = xn0p[:, 0:NT * D].rearrange("p (t d) -> p t d", t=NT)
        tp0 = S0f[:, 2 * NPR * D:(2 * NPR + NT) * D].rearrange("p (t d) -> p t d", t=NT)
        tq0 = S0f[:, (2 * NPR + NT) * D:(2 * NPR + 2 * NT) * D].rearrange("p (t d) -> p t d", t=NT)
        n49 = [S0f[:, 2 * (NPR + NT) * D + NT * k:2 * (NPR + NT) * D + NT * (k + 1)] for k in range(8)]
        xT0 = G0f[:, NT * R0:NT * R0 + NW]
        first.close()

        second = ExitStack()
        sb = sbx(second)
        G1 = sb("G1", [P, 2, C, 2 * D])
        Q1 = sb("Q1", [P, 2, C, D])
        PR = sb("PR", [P, C, D])
        S1 = sb("S1", [P, 2, C + 1, R1])
        EA = sb("EA", [P, 2, PAIRS, P])
        al1 = sb("al1", [P, C, H])
        dd1 = sb("dd1", [P, 2, C, H])
        ee1 = sb("ee1", [P, 2, C, H])
        qb = sb("qb", [P, D])
        ql = sb("ql", [P, D])
        qlb = sb("qlb", [P, D])
        Wkvp = sb("Wkvp", [P, 4 * D])
        Wqkv = sb("Wqkv", [P, 6 * D])
        Wn = sb("Wn", [P, 4, P])
        mW1s = sb("mW1s", [P, 2, HID])
        mW2s = sb("mW2s", [P, 2, 2, P])
        mb1c = sb("mb1c", [P, 2])
        bqkv = sb("bqkv", [P, 5, D])
        cb = sb("cb", [P, 12])
        bgc = sb("bgc", [P, 1])
        G1f = G1[:, :, :, :].rearrange("p u c w -> p (u c w)")
        EAf = EA[:, :, :, :].rearrange("p u a b -> p (u a b)")
        nX, nH, nB2, nB3 = (G1f[:, k * NW:(k + 1) * NW] for k in range(4))
        nB4, nB5 = (EAf[:, k * NW:(k + 1) * NW] for k in range(2))
        Q1f = Q1[:, :, :, :].rearrange("p u c w -> p (u c w)")
        PRf = PR[:, :, :].rearrange("p c w -> p (c w)")
        q_all = PRf[:, 0:2 * NPR * D].rearrange("p (t d) -> p t d", d=D)
        nag = PRf[:, 0:2 * NPR * D]
        rows1 = Q1f[:, 0:NT * R1].rearrange("p (t w) -> p t w", t=NT)
        rden = Q1f[:, 4000:4000 + NT * H].rearrange("p (t h) -> p t h", t=NT)
        HIDDEN = (nH, nB2, nB3, nB4)
        nkv = [Q1f[:, 4608 + 1024 * k:4608 + 1024 * (k + 1)] for k in range(2)]

        def hold(eng, passed, s, value):
            eng.wait_ge(s, value)
            eng.sem_inc(passed, 1)

        block = ctx.enter_context(nc.Block())

        @block.sync
        def _(sp):
            loads = ((dstI[:, :], A["dst"].rearrange("(p t) -> p t", p=P)),
                     (Wa_s[:, :], A["Wa"]), (Wcat[:, 0:D], A["Wa"]), (Wcat[:, D:2 * D], A["Wg"]),
                     (attc[:, 0:1], A["att_w"][0:D, :]), (attc[:, 1:2], A["att_w"][D:2 * D, :]),
                     (Wcat[:, 131:132], A["gate_w"][0:D, :]), (Wcat[:, 129:130], A["gate_w"][2 * D:3 * D, :]),
                     (gw2r[:, :], A["gate_w"][D:2 * D, :].rearrange("d o -> o d").broadcast_to([P, D])),
                     (W1raw[0:D, :], A["eW1"]), (W1raw[D:P, :], A["eW1"]),
                     (engc[0:D, :], A["eng"].unsqueeze(1)), (engc[D:P, :], A["eng"].unsqueeze(1)),
                     (enbc[:, :], A["enb"].unsqueeze(1)),
                     (eb1c[:, :], A["eb1"].rearrange("(k p) -> p k", p=P)),
                     (b2c[0:D, :], A["eb2"].unsqueeze(1)), (b2c[D:P, :], A["eb2"].unsqueeze(1)),
                     (W2raw[:, :, :], A["eW2"].rearrange("(k p) d -> p k d", p=P)))
            assert len(loads) == NWIN
            for dst, s in loads:
                sp.dma_start(dst, s, allow_slow_non_contiguous=True).then_inc(w_in, 16)
            sp.wait_ge(p_dve, 1)
            sp.dma_start(s2exp[0:EP, :].rearrange("(p k t) o -> p k (t o)", p=P, k=2),
                         zeros[:, 0:T // 2].unsqueeze(1).broadcast_to([P, 2, T // 2])).then_inc(p_z, 16)
            sp.dma_start(st0[EP:EP + 1, :], zeros[0:1, 0:R0]).then_inc(st0_out[0], 16)
            sp.dma_start(st0[EP + 1:EP + 1 + P, :], zeros[:, 0:R0]).then_inc(st0_out[1], 16)
            sp.dma_start(st1[EP:EP + 1, :], zeros[0:1, 0:R1]).then_inc(st1_out[0], 16)
            sp.dma_start(st1[EP + 1:EP + 2, :], zeros[0:1, 0:R1]).then_inc(ea_out, 16)
            sp.dma_start(st1[EP + 2:EP + 1 + P, :], zeros[0:P - 1, 0:R1]).then_inc(st1_out[1], 16)
            for u in range(2):
                sp.dma_start(srcI[:, u, :], src_pt[:, u * C:(u + 1) * C]).then_inc(idx0[u], 16)
            with sp.Fori(0, NG) as g:
                sp.wait_ge(n0_free, g + 1)
                sp.dma_start(xg[:, :, :], A["x"][bass.ds(g * GN, GN), :].rearrange("(t p) d -> p t d", p=P)).then_inc(n0_x, 16)
                sp.wait_ge(n0_act, 4 * g + 4)
                sp.dma_start(tab0[bass.ds(g * GN, GN), :].rearrange("(t p) w -> p t w", p=P), tg[:, :, 0:W0]).then_inc(n0_tab, 16)
                sp.wait_ge(n0_tab, 16 * g + 16)
                sp.sem_inc(n0_free, 1)
            sp.wait_ge(p_dve, PD_RP)
            sp.dma_start(rptr[0:NT * P, :].rearrange("(t p) o -> p t o", p=P), rp_s[:, :, :]).then_inc(p_rp, 16)
            sp.wait_ge(p_dve, PD_END)
            sp.wait_ge(s2_put, 16 * NT)
            sp.wait_ge(s2_first, 16)
            sp.dma_start(s2exp[0:EP, :].rearrange("(p t) o -> p (t o)", p=P)[:, 0:1], rfix[:, W0 - 1:W0],
                         allow_slow_non_contiguous=True).then_inc(p_z, 16)
            sp.wait_ge(p_z, 32)

            def loads(c, u, index):
                if index:
                    sp.wait_ge(seen0, c + 1)
                    sp.dma_start(srcI[:, u, :], src_pt[:, bass.ds(c * C, C)]).then_inc(idx0[u], 16)
                sp.wait_ge(xe_free, c + 1)
                sp.dma_start(xe[:, u, :, :].rearrange("p c d -> p (c d)"), chunk_rows(A["edge_attr_64"], D, c)).then_inc(xe_in[u], 16)
                sp.wait_ge(done0, c + 1)
                sp.dma_start(ewC[:, u, :], ew_pt[:, bass.ds(c * C, C)]).then_inc(in0[u], 16)
                sp.dma_start(s2C[:, u, :], chunk_rows(s2exp, 1, c)).then_inc(in0[u], 16)
                sp.dma_start(chunk_rows(qexp, D, c).rearrange("p (k n) -> p k n", k=4),
                             zeros[:, :].unsqueeze(1).broadcast_to([P, 4, 896])).then_inc(zq, 16)

            for u in range(2):
                loads(u, u, False)
            with sp.Fori(1, NCH // 2) as i:
                for u in range(2):
                    loads(2 * i + u, u, True)
            sp.wait_ge(f_dve, 5)
            for u in range(2):
                sp.wait_ge(st0_out[u], 16 * (NCH // 2 + 1))
            sp.dma_start(xn0p.rearrange("p (t d) -> p t d", d=D), A["x"].rearrange("(t p) d -> p t d", p=P)).then_inc(u_x, 16)
            sp.wait_ge(u_act, 2 + NB)
            sp.dma_start(x1Td[:, :], xT0[:, :]).then_inc(u_out, 16)
            sp.wait_ge(u_out, 16)
            sp.wait_ge(zq, 16 * NCH)
            sp.wait_ge(ea_out, 16 * (NCH + 1))
            sp.wait_ge(l_b, 1)
            sp.dma_start(nX, x1Td[:, :]).then_inc(a_x, 16)
            sp.wait_ge(a_x, 16)
            with sp.Fori(0, L) as l:
                def row(name):
                    return A[name][bass.ds(l, 1), :]

                def col(j, name):
                    for q in range(2):
                        sp.dma_start(cb[q * D:(q + 1) * D, j:j + 1], row(name).rearrange("o d -> d o"),
                                     allow_slow_non_contiguous=True).then_inc(l_w, 16)

                def mat(dst, name, rows=slice(0, D)):
                    sp.dma_start(dst, A[name][bass.ds(l, 1), rows, :].rearrange("o a b -> (o a) b")).then_inc(l_w, 16)

                for j, name in ((N1G, "n1g"), (N1B, "n1b")):
                    col(j, name)
                for q in range(2):
                    rows = slice(q * D, (q + 1) * D)
                    for j, name in enumerate(("Wq", "Wkn", "Wvn")):
                        mat(Wqkv[rows, (3 * q + j) * D:(3 * q + j + 1) * D], name)
                    mat(Wkvp[rows, q * D:(q + 1) * D], "Wke")
                    mat(Wkvp[rows, (2 + q) * D:(3 + q) * D], "Wve")
                for j, name in enumerate(("bq", "bkn", "bvn", "bke", "bve")):
                    sp.dma_start(bqkv[:, j, :], row(name).broadcast_to([P, D])).then_inc(l_w, 16)
                for j, name in ((BSELF, "bself"), (BIH, "bih"), (BHH, "bhh"), (BOUT, "bout"), (MB2, "mb2"),
                                (N2G, "n2g"), (N2B, "n2b")):
                    col(j, name)
                for q in range(2):
                    rows = slice(q * D, (q + 1) * D)
                    for j, name in enumerate(("Wself", "Wih", "Whh", "Wout")):
                        mat(Wn[rows, j, q * D:(q + 1) * D], name)
                    mat(mW1s[rows, q, :], "mW1")
                    for kh in range(2):
                        mat(mW2s[:, kh, q, q * D:(q + 1) * D], "mW2", slice(kh * P, (kh + 1) * P))
                for kh in range(2):
                    sp.dma_start(mb1c[:, kh:kh + 1], A["mb1"][bass.ds(l, 1), kh * P:(kh + 1) * P].rearrange("o d -> d o"),
                                 allow_slow_non_contiguous=True).then_inc(l_w, 16)
                sp.dma_start(xTd[:, :], nX).then_inc(h_out, 16)
                for k in range(NB):
                    hold(sp, waits_sp, a_dve, l * A_DVE + 2 * NB + k + 1)
                    c0, w = BLK[k]
                    sp.dma_start(tabkv[2 * c0:2 * (c0 + w), :].rearrange("(t p) w -> p t w", p=P),
                                 nkv[k % 2][:, 0:2 * w].rearrange("p (t w) -> p t w", w=2 * D)).then_inc(a_out[k % 2], 16)
                sp.dma_start(hTd[:, :], nH).then_inc(h_out, 16)
                sp.dma_start(tabq[:, :].rearrange("(t p) d -> p t d", p=P), q_all[:, :, :]).then_inc(q_dram, 16)
                hold(sp, waits_sp, q_put, (l + 1) * (16 * NT))
                hold(sp, waits_sp, q_first, (l + 1) * 16)
                sp.dma_start(qexp[0:EP, :].rearrange("(p t) d -> p t d", p=P)[:, 0, :], qb[:, :]).then_inc(q_done, 16)
                hold(sp, waits_sp, q_done, (l + 1) * 16)
                hold(sp, waits_sp, h_out, (l + 1) * 32)
                for k in range(2):
                    hold(sp, waits_sp, a_out[k], (l + 1) * (16 * ((NB + 1 - k) // 2)))
                with sp.Fori(0, NCH // 2) as i:
                    for u in range(2):
                        c = 2 * i + u
                        sp.wait_ge(seen1, l * NCH + c + 1)
                        sp.dma_start(srcI[:, u, :], src_pt[:, bass.ds(c * C, C)]).then_inc(idx1[u], 16)
                        sp.wait_ge(done1, l * NCH + c + 1)
                        sp.dma_start(EA[:, u, :, :].rearrange("p a b -> p (a b)"),
                                     eaT[bass.ds(c, 1), :, :].rearrange("o p n -> (o p) n")).then_inc(ea_in[u], 16)
                        sp.dma_start(Q1[:, u, :, :].rearrange("p c d -> p (c d)"), chunk_rows(qexp, D, c)).then_inc(q_in[u], 16)
                hold(sp, waits_sp, f_dve, l * 5 + 10)
                sp.dma_start(nH, hTd[:, :]).then_inc(b_x, 16)
                sp.dma_start(nX, xTd[:, :]).then_inc(b_x, 16)
                hold(sp, waits_sp, b_dve, (l + 1) * B_DVE + 1)
            for q in range(2):
                for j, name in ((NGC, "ng"), (NBC, "nb")):
                    sp.dma_start(cb[q * D:(q + 1) * D, j:j + 1], A[name].unsqueeze(1), allow_slow_non_contiguous=True).then_inc(c_x, 16)
            sp.dma_start(nH, x1Td[:, :]).then_inc(c_x, 16)
            for k in range(NB):
                sp.wait_ge(c_dve, 4 * NB + k + 1)
                c0, w = BLK[k]
                sp.dma_start(out[2 * c0:2 * (c0 + w), :].rearrange("(t p) d -> p t d", p=P),
                             nag[:, c0:c0 + w].rearrange("p (t d) -> p t d", d=D)).then_inc(c_out, 16)
            sp.wait_ge(c_out, 16 * NB)

        @block.gpsimd
        def _(pool):
            exact = dict(allow_small_or_imprecise_dtypes=True)
            nc.gpsimd.iota(iotaR[:, :], [[1, P]], base=0, channel_multiplier=0, **exact)
            nc.gpsimd.iota(iotaC[:, :], [[1, 1]], base=0, channel_multiplier=1, **exact)
            nc.gpsimd.iota(iotaPT[:, :], [[1, 1]], base=0, channel_multiplier=T, **exact)
            nc.gpsimd.iota(iotaFX[:, :], [[1, 1]], base=EP + 1, channel_multiplier=1, **exact)
            nc.gpsimd.iota(nodeE[:, :], [[P, NT]], base=EP, channel_multiplier=1, **exact).then_inc(pool_c, 1)

            def gathers(u, G, tab, got):
                for t in range(C):
                    nc.gpsimd.indirect_dma_start(out=G[:, u, t, :], out_offset=None, in_=tab[:, :],
                                                 in_offset=IND(ap=srcI[:, u, t:t + 1], axis=0)).then_inc(got[u], 16)

            pool.wait_ge(n0_tab, 16 * NG)
            for u in range(2):
                pool.wait_ge(idx0[u], 16)
                gathers(u, G0, tab0, got0)
            pool.wait_ge(p_rp, 16)
            nc.gpsimd.indirect_dma_start(out=rpF[:, :], out_offset=None, in_=rptr[:, :],
                                         in_offset=IND(ap=firstI[:, 0:1], axis=0)).then_inc(rp_first, 16)
            pool.wait_ge(p_z, 16)
            for j in range(NT):
                nc.gpsimd.indirect_dma_start(out=s2exp[:, :], out_offset=IND(ap=startI[:, j:j + 1], axis=0),
                                             in_=s2n[:, j:j + 1], in_offset=None).then_inc(s2_put, 16)
            nc.gpsimd.indirect_dma_start(out=rfix[:, 0:W0], out_offset=None, in_=tab0[:, :],
                                         in_offset=IND(ap=firstI[:, 0:1], axis=0)).then_inc(s2_first, 16)
            with pool.Fori(1, NCH // 2) as i:
                for u in range(2):
                    pool.wait_ge(idx0[u], 16 * i + 16)
                    hold(pool, waits_pool, done0, 2 * i + u + 1)
                    gathers(u, G0, tab0, got0)

            def fix_and_fetch(st, R, o, outs, stored, rows):
                for u in range(2):
                    hold(pool, waits_pool, outs[u], stored)
                nc.gpsimd.indirect_dma_start(out=rfix[:, 0:R], out_offset=None, in_=st[:, :],
                                             in_offset=IND(ap=fixI[:, 0:1], axis=0)).then_inc(f_got, 16)
                hold(pool, waits_pool, f_dve, o * 5 + 5)
                nc.gpsimd.indirect_dma_start(out=st[:, :], out_offset=IND(ap=fixI[:, 0:1], axis=0),
                                             in_=wfix[:, 0:R], in_offset=None).then_inc(f_put, 16)
                hold(pool, waits_pool, f_put, o * 16 + 16)
                for j in range(NT):
                    nc.gpsimd.indirect_dma_start(out=rows[:, j, :], out_offset=None, in_=st[:, :],
                                                 in_offset=IND(ap=endI[:, j:j + 1], axis=0)).then_inc(rows_got, 16)

            fix_and_fetch(st0, R0, 0, st0_out, 16 * (NCH // 2 + 1), rows0)

            with pool.Fori(0, L) as l:
                for j in range(NT):
                    if j % 8 == 0:
                        hold(pool, waits_pool, a_dve, l * A_DVE + 2 * NB + j // 8 + 1)
                    nc.gpsimd.indirect_dma_start(out=qexp[:, :], out_offset=IND(ap=startI[:, j:j + 1], axis=0),
                                                 in_=q_all[:, j, :], in_offset=None).then_inc(q_put, 16)
                hold(pool, waits_pool, q_dram, l * 16 + 16)
                nc.gpsimd.indirect_dma_start(out=qb[:, :], out_offset=None, in_=tabq[:, :],
                                             in_offset=IND(ap=firstI[:, 0:1], axis=0)).then_inc(q_first, 16)
                for k in range(2):
                    hold(pool, waits_pool, a_out[k], (l + 1) * (16 * ((NB + 1 - k) // 2)))
                hold(pool, waits_pool, h_out, (l + 1) * 32)
                with pool.Fori(0, NCH // 2) as i:
                    for u in range(2):
                        c = 2 * i + u
                        pool.wait_ge(idx1[u], l * (NCH // 2 * 16) + i * 16 + 16)
                        hold(pool, waits_pool, done1, l * NCH + c + 1)
                        gathers(u, G1, tabkv, got1)
                fix_and_fetch(st1, R1, l + 1, st1_out, l * (NCH // 2 * 16) + 16 * (NCH // 2 + 1), rows1)

        @block.tensor
        def _(pe):
            mm, tr = nc.tensor.matmul, nc.tensor.transpose
            pe.wait_ge(w_in, 16 * NWIN)
            pe.wait_ge(p_dve, 2)
            tr(PS[0:D, 6, 0:D], Wa_s[:, :], ident[0:D, 0:D])
            mm(PS[:, 7, 0:1], W1raw[0:D, 0:P], enbc[:, :], start=True, stop=True)
            mm(PS[:, 7, 1:2], W1raw[0:D, P:2 * P], enbc[:, :], start=True, stop=True).then_inc(p_pe, 1)
            pe.wait_ge(p_dve, 4)
            mm(PS[0:D, 6, 64:66], WaT[:, :], attc[:, :], start=True, stop=True).then_inc(p_pe, 1)
            pe.wait_ge(p_dve, 5)
            zb = zw[:, :].bitcast(bf16)
            mm(PS[0:NT, 7, 0:P], zb[:, 0:NT], zb[:, 0:P], start=True, stop=False, skip_group_check=True)

            def degrees(c, u):
                pe.wait_ge(oh_ready, 2 * c + 2)
                for t in range(C):
                    last = mm(PS[0:NT, 7, 0:P], oh[u][:, t, 0:NT], oh[u][:, t, NT:OHW], start=False, stop=False,
                              skip_group_check=True)
                last.then_inc(oh_used, 1)

            pe.sem_inc(n0_free, 1)
            with pe.Fori(0, NG) as g:
                hold(pe, waits_pe, n0_x, 16 * g + 16)
                for j in range(TG):
                    last = tr(PSf[0:D, 2048 + j * P:2048 + (j + 1) * P], xg[:, j, :], ident[:, :])
                last.then_inc(n0_pe, 1)
                degrees(2 * g, 0)
                pe.wait_ge(n0_act, 4 * g + 1)
                for j in range(TG):
                    last = mm(PSf[:, j * 256:j * 256 + 132], xTg[0:D, j * P:(j + 1) * P], Wcat[:, :], start=True, stop=True)
                last.then_inc(n0_pe, 1)
                degrees(2 * g + 1, 1)
            with pe.Fori(NG, NCH // 2) as i:
                for u in range(2):
                    degrees(2 * i + u, u)
            mm(PS[0:NT, 7, 0:P], zb[:, 0:NT], zb[:, 0:P], start=False, stop=True, skip_group_check=True).then_inc(p_pe, 1)
            pe.wait_ge(n0_act, 4 * NG)
            pe.wait_ge(p_dve, 6)
            mm(PS[0:NT, 1, 0:1], tri[0:NT, 0:NT], cumR[0:NT, P - 1:P], start=True, stop=True).then_inc(p_pe, 1)
            pe.wait_ge(p_dve, 7)
            tr(PS[:, 2, 0:NT], endxR[0:NT, :], ident[0:NT, 0:NT])
            tr(PS[:, 3, 0:NT], degR[0:NT, :], ident[0:NT, 0:NT])
            tr(PS[0:V1, 4, 0:P], F1b[:, :], ident[:, :])
            tr(PS[0:V1, 5, 0:P], F2b[:, :], ident[:, :]).then_inc(p_pe, 1)
            pe.wait_ge(p_dve, PD_END)

            def turn(u, s):
                for j in range(4):
                    t = 8 * s + 2 * j
                    last = tr(PS[:, 0, j * P:(j + 1) * P], xe[:, u, t:t + 2, :].rearrange("p a d -> p (a d)"), ident[:, :])
                last.then_inc(m_pe, 1)

            with pe.Fori(0, NCH // 2) as i:
                for u in range(2):
                    c = 2 * i + u
                    pe.wait_ge(xn_ready, c + 1)
                    turn(u, 0)
                    for s in range(PT):
                        pe.wait_ge(m_act, 42 * c + (1 if s == 0 else 6 * s))
                        for r in range(2):
                            for kh in range(2):
                                last = mm(PS[:, 1 + 2 * r + kh, :], W1p[:, r, kh, :], xT8[:, :], start=True, stop=True)
                            last.then_inc(m_pe, 1)
                        if s < PT - 1:
                            turn(u, s + 1)
                        for r in range(2):
                            pe.wait_ge(m_act, 42 * c + 6 * s + 3 + 2 * r)
                            for kh in range(2):
                                last = mm(PS[:, 5, :], W2p[:, kh, r, :], hid8[:, r, kh, :],
                                          start=(r == 0 and kh == 0), stop=(r == 1 and kh == 1))
                        last.then_inc(m_pe, 1)

            def fix(V, o, maxes, fm):
                pe.wait_ge(f_dve, o * 5 + 1)
                if fm is not None:
                    tr(PS[0:D, 2, 0:P], fm, ident[:, :])
                tr(PS[0:V, 0, 0:P], MX[:, 0:V], ident[:, :])
                tr(PS[0:V, 1, 0:P], maxes, ident[:, :]).then_inc(f_pe, 1)
                pe.wait_ge(f_dve, o * 5 + 3)
                if fm is not None:
                    tr(PS[:, 5, 0:D], FMT[:, 1, :], ident[0:D, 0:D])
                tr(PS[:, 3, 0:V], sh[0:V, 0, :], ident[0:V, 0:V])
                tr(PS[:, 4, 0:V], sh[0:V, 1, :], ident[0:V, 0:V]).then_inc(f_pe, 1)

            fix(V0, 0, S0[:, 1, C, 1:1 + V0], S0[:, 1, C, 1 + V0:R0])
            pe.wait_ge(u_dve, 3)
            for k in range(NB):
                c0, w = BLK[k]
                for j in range(w // P):
                    m = c0 // P + j
                    last = tr(PS[:, k, j * P:(j + 1) * P], xn0p[:, m * P:(m + 1) * P], ident[:, :])
                last.then_inc(u_pe, 1)

            def per_block(step, done, sem_, base, first):
                for k in range(NB):
                    hold(pe, waits_pe, sem_, base + first + k + 1)
                    step(k, *BLK[k]).then_inc(done, 1)

            def means(src):
                return lambda k, c0, w: mm(PS[:, k, 0:w], onesD[:, :], src[:, c0:c0 + w], start=True, stop=True)

            pe.wait_ge(a_x, 16)
            with pe.Fori(0, L) as l:
                hold(pe, waits_pe, l_w, l * (16 * NLW) + 16 * NLW)
                hold(pe, waits_pe, b_dve, l * B_DVE + 1)
                for k in range(NB):
                    means(nX)(k, *BLK[k]).then_inc(a_pe, 1)
                per_block(means(nB3), a_pe, a_act, l * (2 * NB), 0)
                for k in range(NB):
                    c0, w = BLK[k]
                    hold(pe, waits_pe, a_dve, l * A_DVE + NB + k + 1)
                    if k == 0:
                        hold(pe, waits_pe, a_act, (l + 1) * (2 * NB))
                    if k >= 2:
                        hold(pe, waits_pe, a_dve, l * A_DVE + 2 * NB + k - 1)
                    for j in range(w // P):
                        last = mm(PS[:, 4 * (k % 2) + j, 0:6 * D], nH[:, c0 + j * P:c0 + (j + 1) * P], Wqkv[:, :], start=True, stop=True)
                    last.then_inc(a_pe, 1)
                with pe.Fori(0, NCH // 2) as i:
                    for u in range(2):
                        n = l * NCH + 2 * i + u
                        pe.wait_ge(got1[u], l * (NCH // 2 * 16 * C) + i * (16 * C) + 16 * C)
                        pe.sem_inc(seen1, 1)
                        pe.wait_ge(ea_in[u], l * (NCH // 2 * 16) + i * 16 + 16)
                        for s in range(PT):
                            b = 2 * (s % 4)
                            pe.wait_ge(k_used, n * PT + s + (2 if s < 3 else 1))
                            pe.wait_ge(v_moved, n * PT + s + (2 if s < 3 else 1))
                            for k in range(2):
                                mm(PS[:, b + k, :], ident[:, :], G1[:, u, 8 * s:8 * s + 8, k * D:(k + 1) * D],
                                   start=True, stop=False, skip_group_check=True)
                            for j in range(4):
                                for k in range(2):
                                    last = mm(PS[:, b + k, P * j:P * j + P], EA[:, u, 4 * s + j, :], Wkvp[:, k * P:(k + 1) * P],
                                              start=False, stop=True, skip_group_check=True)
                            last.then_inc(kv_ready, 1)
                fix(V1, l + 1, S1[:, 1, C, H:R1], None)
                B = l * B_DVE + 1

                def turned(k, c0, w):
                    for j in range(w // P):
                        last = tr(PS[:, k, j * P:(j + 1) * P], nag[:, c0 + j * P:c0 + (j + 1) * P], ident[:, :])
                    return last

                def gates(k, c0, w):
                    mm(PS[:, k, 0:w], Wn[:, 1, :], nB2[:, c0:c0 + w], start=True, stop=False)
                    return mm(PS[:, k, 0:w], Wn[:, 2, :], nH[:, c0:c0 + w], start=False, stop=True)

                def product(i, src):
                    return lambda k, c0, w: mm(PS[:, k, 0:w], Wn[:, i, :], src[:, c0:c0 + w], start=True, stop=True)

                def hidden(kh, q):
                    return lambda k, c0, w: mm(PS[:, k, 0:w], mW1s[:, q, kh * P:(kh + 1) * P], nB5[:, c0:c0 + w], start=True, stop=True)

                def folded(k, c0, w):
                    for n, src in enumerate(HIDDEN):
                        last = mm(PS[:, k, 0:w], mW2s[:, n // 2, n % 2, :], src[:, c0:c0 + w], start=(n == 0), stop=(n == 3))
                    return last

                a0 = l * (8 * NB)
                per_block(turned, b_pe, b_dve, B, 0)
                hold(pe, waits_pe, b_x, l * 32 + 32)
                per_block(gates, b_pe, b_act, a0, 0)
                per_block(product(0, nH), b_pe, b_act, a0, NB)
                per_block(product(3, nB4), b_pe, b_dve, B, NB)
                per_block(means(nX), b_pe, b_dve, B, 2 * NB)
                per_block(means(nB3), b_pe, b_act, a0, 2 * NB)
                per_block(hidden(0, 0), b_pe, b_dve, B, 4 * NB)
                for n in range(1, 4):
                    per_block(hidden(n // 2, n % 2), b_pe, b_act, a0, (3 + n) * NB)
                per_block(folded, b_pe, b_act, a0, 7 * NB)
            pe.wait_ge(c_x, 80)
            for k in range(NB):
                means(nX)(k, *BLK[k]).then_inc(c_pe, 1)

            def tail(step, sem_, first):
                for k in range(NB):
                    pe.wait_ge(sem_, first + k + 1)
                    step(k, *BLK[k]).then_inc(c_pe, 1)

            def back(k, c0, w):
                for j in range(w // P):
                    last = tr(PS[:, k, j * P:(j + 1) * P], nB5[:, c0 + j * P:c0 + (j + 1) * P], ident[:, :])
                return last

            tail(means(nB3), c_act, 0)
            tail(means(nB2), c_dve, NB)
            tail(means(nB3), c_act, 2 * NB)
            tail(back, c_dve, 3 * NB)

        @block.scalar
        def _(act):
            f = nc.scalar.activation
            with act.Fori(0, NG) as g:
                act.wait_ge(n0_pe, 2 * g + 1)
                f(xTg[0:D, :], PSf[0:D, 2048:2048 + GN], ACT.Copy).then_inc(n0_act, 1)
                act.wait_ge(n0_pe, 2 * g + 2)
                w = PSf[:, 0:2048].rearrange("p (t w) -> p t w", w=256)
                f(tg[:, :, :], w[:, 0:TG, 0:132], ACT.Copy).then_inc(n0_act, 1)
                f(s2n[:, bass.ds(g * TG, TG)], w[:, 0:TG, 130], ACT.Copy).then_inc(n0_act, 1)
                f(xg1[:, bass.ds(g * TG, TG)], w[:, 0:TG, 131], ACT.Copy).then_inc(n0_act, 1)

            act.wait_ge(p_dve, PD_END)
            act.sem_inc(xe_free, 2)

            def features(c, k):
                act.wait_ge(m_pe, 28 * c + k)
                f(xT8[:, :], PS[:, 0, :], ACT.Copy).then_inc(m_act, 1)

            with act.Fori(0, NCH // 2) as i:
                for u in range(2):
                    c = 2 * i + u
                    act.wait_ge(var_ready, c + 1)
                    f(sd8[:, :], rs8[:, :], ACT.Sqrt, bias=epsc[:, 0:1], scale=1.0 / D).then_inc(sqrt_ready, 1)
                    features(c, 1)
                    for s in range(PT):
                        for r in range(2):
                            act.wait_ge(m_pe, 28 * c + 4 * s + 2 + r)
                            for kh in range(2):
                                f(hid8[:, r, kh, :], PS[:, 1 + 2 * r + kh, :], ACT.Relu, bias=b1c[:, kh:kh + 1]).then_inc(m_act, 1)
                        if s < PT - 1:
                            features(c, 4 * s + 4)
                        if s == 0:
                            act.wait_ge(d0_ready, c + 1)
                            f(ee0[:, :, :], dd0[:, :, :], ACT.Exp).then_inc(e0_ready, 1)
                            act.wait_ge(ea_out, 16 * c + 16)
                        act.wait_ge(m_pe, 28 * c + (4 * s + 5 if s < PT - 1 else 28))
                        f(eaC[:, 4 * s:4 * s + 4, :].rearrange("p a b -> p (a b)"), PS[:, 5, :], ACT.Identity,
                          bias=b2c[:, 0:1]).then_inc(m_act, 1)
                    act.wait_ge(m_act, 42 * c + 42)
                    act.sem_inc(xe_free, 1)
                    act.dma_start(eaT[bass.ds(c, 1), :, :].rearrange("o p n -> (o p) n"),
                                  eaC[:, :, :].rearrange("p a b -> p (a b)")).then_inc(ea_out, 16)
                    act.wait_ge(done0, c + 3)
                    act.dma_start(chunk_rows(st0, R0, c), S0[:, u, 1:C + 1, :].rearrange("p c w -> p (c w)")).then_inc(st0_out[u], 16)

            def fix(V, o, scale):
                act.wait_ge(f_dve, o * 5 + 2)
                f(abE[0:V, :, :], ab[0:V, :, :], ACT.Exp, scale=scale).then_inc(f_act, 1)
                act.wait_ge(f_dve, o * 5 + 4)
                f(abE[:, :, 0:V], ab[:, :, 0:V], ACT.Exp, scale=scale).then_inc(f_act, 1)

            fix(V0, 0, 1.0)
            act.wait_ge(u_dve, 1)
            f(n49[4], n49[3], ACT.Sigmoid).then_inc(u_act, 1)
            act.wait_ge(u_dve, 2)
            f(n49[0], n49[7], ACT.Sqrt, bias=epsc[:, 0:1], scale=1.0 / D).then_inc(u_act, 1)
            for k in range(NB):
                c0, w = BLK[k]
                act.wait_ge(u_pe, k + 1)
                f(xT0[:, c0:c0 + w], PS[:, k, 0:w], ACT.Copy).then_inc(u_act, 1)

            def per_block(step, done, sem_, base, first):
                for k in range(NB):
                    act.wait_ge(sem_, base + first + k + 1)
                    step(k, *BLK[k]).then_inc(done, 1)

            def square(k, c0, w):
                return f(nB3[:, c0:c0 + w], nB5[:, c0:c0 + w], ACT.Square)

            def root(k, c0, w):
                return f(nB4[:, c0:c0 + w], PS[:, k, 0:w], ACT.Sqrt, bias=epsc[:, 0:1])

            with act.Fori(0, L) as l:
                per_block(square, a_act, a_dve, l * A_DVE, 0)
                per_block(root, a_act, a_pe, l * (3 * NB), NB)
                with act.Fori(0, NCH // 2) as i:
                    for u in range(2):
                        n = l * NCH + 2 * i + u
                        for s in range(PT):
                            b = 2 * (s % 4)
                            act.wait_ge(kv_ready, n * PT + s + 1)
                            f(G1[:, u, 8 * s:8 * s + 8, D:2 * D], PS[:, b + 1, :].rearrange("p (t d) -> p t d", t=8), ACT.Copy).then_inc(v_moved, 1)
                        act.wait_ge(d1_ready, n + 1)
                        f(ee1[:, :, :, :], dd1[:, :, :, :], ACT.Exp, scale=SCALE).then_inc(e1_ready, 1)
                        act.wait_ge(done1, n + 3)
                        act.dma_start(chunk_rows(st1, R1, 2 * i + u), S1[:, u, 1:C + 1, :].rearrange("p c w -> p (c w)")).then_inc(st1_out[u], 16)
                fix(V1, l + 1, SCALE)
                p0 = l * (11 * NB)
                per_block(lambda k, c0, w: f(nB2[:, c0:c0 + w], PS[:, k, 0:w], ACT.Copy), b_act, b_pe, p0, 0)
                per_block(lambda k, c0, w: f(nB3[:, c0:c0 + w], PS[:, k, 0:w], ACT.Sigmoid, bias=bgc[:, 0:1]), b_act, b_pe, p0, NB)
                per_block(square, b_act, b_dve, l * B_DVE + 1, 3 * NB)
                per_block(root, b_act, b_pe, p0, 5 * NB)
                for n in range(4):
                    per_block(lambda k, c0, w: f(HIDDEN[n][:, c0:c0 + w], PS[:, k, 0:w], ACT.Relu, bias=mb1c[:, n // 2:n // 2 + 1]),
                              b_act, b_pe, p0, (6 + n) * NB)
            for n in range(2):
                per_block(square, c_act, c_dve, 0, 2 * n * NB)
                per_block(root, c_act, c_pe, 0, (2 * n + 1) * NB)

        @block.vector
        def _(dve):
            v = nc.vector
            tt, ts, stt, cp, red = v.tensor_tensor, v.tensor_scalar, v.scalar_tensor_tensor, v.tensor_copy, v.tensor_reduce
            scan = v.tensor_tensor_scan
            settle = dve.drain

            def along(ap, shape):
                return ap.unsqueeze(len(shape) - 1).broadcast_to(shape)

            dve.sem_inc(oh_used, 2)
            v.memset(zeros[:, :], 0.0)
            v.memset(epsc[:, :], 1e-5)
            v.memset(onesD[:, :], 0.0)
            v.memset(zw[:, :], 0.0)
            v.memset(cont[:, 0:1], 0.0)
            v.memset(W1p[:, :, :, :], 0.0)
            v.memset(W2p[:, :, :, :], 0.0)
            v.memset(s2x[:, :], 0.0)
            settle()
            v.memset(onesD[0:D, 0:D], 1.0 / D)
            v.memset(onesD[D:P, D:P], 1.0 / D)
            settle().then_inc(p_dve, 1)
            dve.wait_ge(pool_c, 1)
            ts(ident[:, :], iotaR[:, :], iotaC[:, 0:1], None, ALU.is_equal)
            ts(tri[:, :], iotaR[:, :], iotaC[:, 0:1], None, ALU.is_gt).then_inc(p_dve, 1)
            dve.wait_ge(w_in, 16 * NWIN)
            ts(hiI[:, :], dstI[:, :], 7, None, ALU.logical_shift_right)
            ts(loI[:, :], dstI[:, :], 127, None, ALU.bitwise_and)
            cp(firstI[:, :], dstI[:, 0:1])
            cp(dstF[:, :], dstI[:, :])
            settle()
            cp(hiF[:, :], hiI[:, :])
            cp(loF[:, :], loI[:, :])
            tt(cont[:, 1:T], dstF[:, 1:T], dstF[:, 0:T - 1], ALU.is_equal)
            cp(F1b[:, :], dstF[:, 0:1].broadcast_to([P, V1]))
            cp(F2b[:, :], dstF[:, T - 1:T].broadcast_to([P, V1]))
            for r in range(2):
                rows = slice(r * D, (r + 1) * D)
                ts(W1p[rows, r, :, :].rearrange("p k n -> p (k n)"), W1raw[rows, :], engc[rows, 0:1], None, ALU.mult)
                cp(W2p[:, :, r, r * D:(r + 1) * D], W2raw[:, :, :])
            settle().then_inc(p_dve, 1)
            dve.wait_ge(p_pe, 1)
            cp(WaT[:, :], PS[0:D, 6, 0:D])
            tt(b1c[:, :], PS[:, 7, 0:2], eb1c[:, :], ALU.add).then_inc(p_dve, 1)
            dve.wait_ge(p_pe, 2)
            cp(Wcat[:, 128:129], PS[0:D, 6, 64:65])
            cp(Wcat[:, 130:131], PS[0:D, 6, 65:66]).then_inc(p_dve, 1)
            with dve.Fori(0, NCH // 2) as i:
                for u in range(2):
                    c = 2 * i + u
                    dve.wait_ge(oh_used, c + 1)
                    tt(oh[u][:, :, 0:NT], iotaR[:, 0:NT].unsqueeze(1).broadcast_to([P, C, NT]),
                       along(hiF[:, bass.ds(c * C, C)], [P, C, NT]), ALU.is_equal).then_inc(oh_ready, 1)
                    tt(oh[u][:, :, NT:OHW], iotaR[:, :].unsqueeze(1).broadcast_to([P, C, P]),
                       along(loF[:, bass.ds(c * C, C)], [P, C, P]), ALU.is_equal).then_inc(oh_ready, 1)
            dve.wait_ge(p_pe, 3)
            cp(degR[0:NT, :], PS[0:NT, 7, 0:P])
            settle()
            scan(cumR[0:NT, :], zeros[0:NT, 0:P], degR[0:NT, :], 0.0, ALU.add, ALU.add).then_inc(p_dve, 1)
            dve.wait_ge(p_pe, 4)
            cp(baseC[0:NT, :], PS[0:NT, 1, 0:1])
            settle()
            ts(endxR[0:NT, :], cumR[0:NT, :], baseC[0:NT, 0:1], None, ALU.add).then_inc(p_dve, 1)
            dve.wait_ge(p_pe, 5)
            ts(lastF[:, :], PS[:, 2, 0:NT], -1.0, None, ALU.add)
            cp(degn[:, :], PS[:, 3, 0:NT])
            settle()
            ts(neF[:, :], degn[:, :], 0.0, None, ALU.is_gt)
            tt(tmpN[:, :], lastF[:, :], degn[:, :], ALU.subtract)
            settle()
            ts(firstF[:, :], tmpN[:, :], 1.0, None, ALU.add)
            settle()
            stt(tmpN[:, :], lastF[:, :], -float(EP), neF[:, :], ALU.add, ALU.mult)
            settle()
            ts(endI[:, :], tmpN[:, :], float(EP), None, ALU.add)
            settle()
            tt(tmpN[:, :], firstF[:, :], nodeE[:, :], ALU.subtract)
            settle()
            tt(tmpN[:, :], tmpN[:, :], neF[:, :], ALU.mult)
            settle()
            tt(startI[:, :], tmpN[:, :], nodeE[:, :], ALU.add)
            cp(rp_s[:, :, 0], firstF[:, :])
            cp(rp_s[:, :, 1], lastF[:, :])
            settle().then_inc(p_dve, 1)
            cp(rowF[0:V1, :], PS[0:V1, 4, 0:P])
            cp(rowL[0:V1, :], PS[0:V1, 5, 0:P])
            v.memset(gF[0:V1, 0:1], 0.0)
            settle()
            tt(gF[0:V1, 1:P], rowF[0:V1, 1:P], rowL[0:V1, 0:P - 1], ALU.is_equal)
            settle()
            tt(rowF[0:V1, :], rowF[0:V1, :], rowL[0:V1, :], ALU.is_equal)
            settle()
            tt(gF[0:V1, :], gF[0:V1, :], rowF[0:V1, :], ALU.mult)
            settle()
            ts(gmask[:, :], gF[0:V1, :], -1.0, BIG, ALU.add, ALU.mult)
            dve.wait_ge(rp_first, 16)
            tt(vF[:, 0:1], rpF[:, 0:1], iotaPT[:, :], ALU.is_lt)
            ts(vF[:, 1:2], iotaPT[:, :], float(T), None, ALU.add)
            tt(vF[:, 2:3], rpF[:, 1:2], iotaFX[:, :], ALU.subtract)
            settle()
            tt(vF[:, 1:2], rpF[:, 1:2], vF[:, 1:2], ALU.is_lt)
            settle()
            tt(vF[:, 0:1], vF[:, 0:1], vF[:, 1:2], ALU.mult)
            settle()
            tt(vF[:, 0:1], vF[:, 0:1], vF[:, 2:3], ALU.mult)
            settle()
            tt(fixI[:, :], vF[:, 0:1], iotaFX[:, :], ALU.add)
            v.memset(S0[:, :, :, :], 0.0)
            settle().then_inc(p_dve, 1)
            dve.sem_inc(seen0, 2)
            dve.sem_inc(done0, 2)

            with dve.Fori(0, NCH // 2) as i:
                for u in range(2):
                    c = 2 * i + u
                    X = xe[:, u, :, :]
                    S, Sb = S0[:, u, :, :], S0[:, 1 - u, :, :]
                    G = G0[:, u, :, :]
                    sq = S[:, 1:C + 1, R0 - D:R0]
                    dve.wait_ge(xe_in[u], 16 * i + 16)
                    dve.wait_ge(st0_out[u], 16 * i + 16)
                    red(mu8[:, :], X, AX.X, ALU.add)
                    settle()
                    ts(mu8[:, :], mu8[:, :], 1.0 / D, None, ALU.mult)
                    settle()
                    tt(X, X, along(mu8[:, :], [P, C, D]), ALU.subtract)
                    settle()
                    tt(sq, X, X, ALU.mult)
                    settle()
                    red(rs8[:, :], sq, AX.X, ALU.add).then_inc(var_ready, 1)
                    cp(contC[:, :], cont[:, bass.ds(c * C, C)])
                    cp(s2x[:, 0:1], s2x[:, C:C + 1])
                    cp(S[:, 0, :], Sb[:, C, :])
                    settle()
                    ts(maskC[:, :], contC[:, :], -1.0, BIG, ALU.add, ALU.mult)
                    dve.wait_ge(in0[u], 32 * i + 32)
                    scan(s2x[:, 1:C + 1], contC[:, :], s2C[:, u, :], s2x[:, 0:1], ALU.mult, ALU.add)
                    dve.wait_ge(sqrt_ready, c + 1)
                    v.reciprocal(rs8[:, :], sd8[:, :])
                    settle()
                    tt(X, X, along(rs8[:, :], [P, C, D]), ALU.mult).then_inc(xn_ready, 1)
                    dve.wait_ge(got0[u], i * (16 * C) + 16 * C)
                    dve.sem_inc(seen0, 1)
                    tt(al0[:, :], G[:, :, 2 * D], ewC[:, u, :], ALU.mult)
                    tt(uw0[:, :], G[:, :, 2 * D + 1], ewC[:, u, :], ALU.mult)
                    settle()
                    tt(al0[:, :], al0[:, :], s2x[:, 1:C + 1], ALU.add)
                    settle()
                    stt(al0[:, :], al0[:, :], 0.01, al0[:, :], ALU.mult, ALU.max)
                    settle()
                    scan(S[:, 1:C + 1, 0], maskC[:, :], al0[:, :], S[:, 0, 0:1], ALU.add, ALU.max)
                    settle()
                    tt(dd0[:, 0, :], S[:, 0:C, 0], maskC[:, :], ALU.add)
                    tt(dd0[:, 1, :], al0[:, :], S[:, 1:C + 1, 0], ALU.subtract)
                    settle()
                    tt(dd0[:, 0, :], dd0[:, 0, :], S[:, 1:C + 1, 0], ALU.subtract).then_inc(d0_ready, 1)
                    tt(G[:, :, D:2 * D], G[:, :, D:2 * D], along(ewC[:, u, :], [P, C, D]), ALU.mult)
                    settle()
                    scan(S[:, 1:C + 1, 2 + D], contC[:, :], uw0[:, :], S[:, 0, 2 + D:3 + D], ALU.mult, ALU.add)
                    for k in range(D):
                        scan(S[:, 1:C + 1, 3 + D + k], maskC[:, :], G[:, :, D + k], S[:, 0, 3 + D + k:4 + D + k], ALU.add, ALU.max)
                    dve.wait_ge(e0_ready, c + 1)
                    tt(G[:, :, 0:D], G[:, :, 0:D], along(ee0[:, 1, :], [P, C, D]), ALU.mult)
                    scan(S[:, 1:C + 1, 1], ee0[:, 0, :], ee0[:, 1, :], S[:, 0, 1:2], ALU.mult, ALU.add)
                    settle()
                    for k in range(D):
                        last = scan(S[:, 1:C + 1, 2 + k], ee0[:, 0, :], G[:, :, k], S[:, 0, 2 + k:3 + k], ALU.mult, ALU.add)
                    settle().then_inc(done0, 1)

            def fix(V, o, state, spread, copied, fm):
                spread()
                settle().then_inc(f_dve, 1)
                dve.wait_ge(f_pe, o * 2 + 1)
                cp(MXT[0:V, :], PS[0:V, 0, 0:P])
                cp(VT[0:V, :], PS[0:V, 1, 0:P])
                if fm:
                    cp(FMT[:, 0, :], PS[0:D, 2, 0:P])
                settle()
                scan(MT[0:V, :], gmask[0:V, :], MXT[0:V, :], -BIG, ALU.add, ALU.max)
                if fm:
                    v.memset(FMT[:, 1, 0:1], -BIG)
                    settle()
                    scan(FMT[:, 1, 1:P], gmask[0:D, 0:P - 1], FMT[:, 0, 0:P - 1], -BIG, ALU.add, ALU.max)
                settle()
                tt(ab[0:V, 0, 1:P], MT[0:V, 0:P - 1], gmask[0:V, 1:P], ALU.add)
                v.memset(ab[0:V, 0, 0:1], -BIG)
                tt(ab[0:V, 1, :], MXT[0:V, :], MT[0:V, :], ALU.subtract)
                settle()
                tt(ab[0:V, 0, 1:P], ab[0:V, 0, 1:P], MT[0:V, 1:P], ALU.subtract).then_inc(f_dve, 1)
                dve.wait_ge(f_act, o * 2 + 1)
                tt(VT[0:V, :], VT[0:V, :], abE[0:V, 1, :], ALU.mult)
                v.memset(sh[0:V, 0, 0:1], -BIG)
                v.memset(sh[0:V, 1, 0:1], 0.0)
                cp(sh[0:V, 0, 1:P], MT[0:V, 0:P - 1])
                settle()
                scan(sh[0:V, 1, 1:P], abE[0:V, 0, 0:P - 1], VT[0:V, 0:P - 1], 0.0, ALU.mult, ALU.add)
                settle().then_inc(f_dve, 1)
                dve.wait_ge(f_pe, o * 2 + 2)
                dve.wait_ge(f_got, o * 16 + 16)
                copied()
                settle()
                tt(wide[:, 0, 0:V], MX[:, 0:V], PS[:, 3, 0:V], ALU.max)
                cp(wide[:, 1, 0:V], PS[:, 4, 0:V])
                settle()
                tt(ab[:, 0, 0:V], PS[:, 3, 0:V], wide[:, 0, 0:V], ALU.subtract)
                tt(ab[:, 1, 0:V], MX[:, 0:V], wide[:, 0, 0:V], ALU.subtract)
                settle().then_inc(f_dve, 1)
                dve.wait_ge(f_act, o * 2 + 2)
                return

            def join(V, first, nmax, R, fm):
                tt(wide[:, 1, 0:V], wide[:, 1, 0:V], abE[:, 0, 0:V], ALU.mult)
                tt(wfix[:, first:first + V], rfix[:, first:first + V], abE[:, 1, 0:V], ALU.mult)
                cp(wfix[:, 0:nmax], wide[:, 0, 0:nmax])
                if fm:
                    tt(wfix[:, R - D:R], rfix[:, R - D:R], PS[:, 5, 0:D], ALU.max)
                settle()
                tt(wfix[:, first:first + V], wfix[:, first:first + V], wide[:, 1, 0:V], ALU.add)
                settle().then_inc(f_dve, 1)

            def spread0(row):
                cp(MX[:, 0:V0 - 1], row[:, 0:1].broadcast_to([P, V0 - 1]))
                v.memset(MX[:, V0 - 1:V0], 0.0)

            fix(V0, 0, None, lambda: spread0(S0[:, 1, C, :]), lambda: spread0(rfix), True)
            join(V0, 1, 1, R0, True)

            dve.wait_ge(rows_got, 16 * NT)
            ts(n49[0], rows0[:, :, 1], 1e-30, None, ALU.max)
            ts(n49[3], degn[:, :], 1.0, None, ALU.max)
            tt(tp0, rows0[:, :, 3 + D:R0], gw2r[:, :].unsqueeze(1).broadcast_to([P, NT, D]), ALU.mult)
            settle()
            v.reciprocal(n49[1], n49[0])
            v.reciprocal(n49[5], n49[3])
            red(n49[2], tp0, AX.X, ALU.add)
            settle()
            tt(n49[3], rows0[:, :, 2 + D], n49[5], ALU.mult)
            settle()
            tt(n49[3], n49[3], n49[2], ALU.add)
            settle()
            tt(n49[3], n49[3], xg1[:, :], ALU.add).then_inc(u_dve, 1)
            dve.wait_ge(u_act, 1)
            tt(n49[5], n49[4], n49[1], ALU.mult)
            dve.wait_ge(u_x, 16)
            settle()
            tt(tq0, rows0[:, :, 2:2 + D], along(n49[5], [P, NT, D]), ALU.mult)
            settle()
            tt(xn0, xn0, tq0, ALU.add)
            settle()
            red(n49[6], xn0, AX.X, ALU.add)
            settle()
            ts(n49[6], n49[6], 1.0 / D, None, ALU.mult)
            settle()
            tt(xn0, xn0, along(n49[6], [P, NT, D]), ALU.subtract)
            settle()
            tt(tp0, xn0, xn0, ALU.mult)
            settle()
            red(n49[7], tp0, AX.X, ALU.add).then_inc(u_dve, 1)
            dve.wait_ge(u_act, 2)
            v.reciprocal(n49[1], n49[0])
            settle()
            tt(xn0, xn0, along(n49[1], [P, NT, D]), ALU.mult)
            settle().then_inc(u_dve, 1)

            dve.wait_ge(u_out, 16)
            dve.wait_ge(ea_out, 16 * (NCH + 1))
            for block_weights in (Wkvp[:, :], Wqkv[:, :], Wn[:, :, :], mW1s[:, :, :], mW2s[:, :, :, :]):
                v.memset(block_weights, 0.0)
            v.memset(S1[:, :, :, :], 0.0)
            v.memset(qlb[:, :], 0.0)
            settle().then_inc(l_b, 1)
            dve.sem_inc(done1, 2)
            dve.sem_inc(seen1, 2)
            dve.sem_inc(k_used, 4)
            dve.sem_inc(v_moved, 4)
            dve.sem_inc(b_dve, 1)

            def per_block(step, done, sem_, base, first):
                for k in range(NB):
                    dve.wait_ge(sem_, base + first + k + 1)
                    step(k, *BLK[k]).then_inc(done, 1)

            def centre(src):
                return lambda k, c0, w: tt(nB5[:, c0:c0 + w], src[:, c0:c0 + w], PS[:, k, 0:w], ALU.subtract)

            def normed(dst, g_, b_):
                def step(k, c0, w):
                    v.reciprocal(nB4[:, c0:c0 + w], nB4[:, c0:c0 + w])
                    settle()
                    out_ = tt(nB5[:, c0:c0 + w], nB5[:, c0:c0 + w], nB4[:, c0:c0 + w], ALU.mult)
                    if g_ is not None:
                        settle()
                        out_ = ts(dst[:, c0:c0 + w], nB5[:, c0:c0 + w], cb[:, g_:g_ + 1], cb[:, b_:b_ + 1], ALU.mult, ALU.add)
                    return out_
                return step

            dve.wait_ge(a_x, 16)
            with dve.Fori(0, L) as l:
                dve.wait_ge(l_w, l * (16 * NLW) + 16 * NLW)
                tt(bqkv[:, 1:3, :], bqkv[:, 1:3, :], bqkv[:, 3:5, :], ALU.add)
                tt(bgc[:, :], cb[:, BIH:BIH + 1], cb[:, BHH:BHH + 1], ALU.add)
                per_block(centre(nX), a_dve, a_pe, l * (3 * NB), 0)
                for k in range(NB):
                    dve.wait_ge(a_act, l * (2 * NB) + NB + k + 1)
                    normed(nH, N1G, N1B)(k, *BLK[k])
                    settle().then_inc(a_dve, 1)
                for k in range(NB):
                    c0, w = BLK[k]
                    dve.wait_ge(a_pe, l * (3 * NB) + 2 * NB + k + 1)
                    if k >= 2:
                        dve.wait_ge(a_out[k % 2], l * (16 * ((NB + 1 - k % 2) // 2)) + 16 * (k // 2))
                    s_ = PS[:, 4 * (k % 2):4 * (k % 2) + w // P, 0:6 * D].rearrange("p j (q w) -> p j q w", q=2)
                    kv_ = nkv[k % 2][:, 0:2 * w].rearrange("p (j q w) -> p j q w", q=2, w=2 * D)
                    q_ = q_all[:, 2 * c0 // P:2 * (c0 + w) // P, :].rearrange("p (j q) d -> p j q d", q=2)
                    for q in range(2):
                        tt(kv_[:, :, q, :], s_[:, :, q, D:3 * D],
                           bqkv[:, 1:3, :].rearrange("p a d -> p (a d)").unsqueeze(1).broadcast_to([P, w // P, 2 * D]), ALU.add)
                        tt(q_[:, :, q, :], s_[:, :, q, 0:D], bqkv[:, 0, :].unsqueeze(1).broadcast_to([P, w // P, D]), ALU.add)
                    settle().then_inc(a_dve, 1)
                with dve.Fori(0, NCH // 2) as i:
                    for u in range(2):
                        c = 2 * i + u
                        n = l * NCH + c
                        S, Sb = S1[:, u, :, :], S1[:, 1 - u, :, :]
                        Q, Qb = Q1[:, u, :, :], Q1[:, 1 - u, :, :]
                        G = G1[:, u, :, :]
                        cp(contC[:, :], cont[:, bass.ds(c * C, C)])
                        dve.wait_ge(st1_out[u], l * (16 * (NCH // 2)) + i * 16 + 16)
                        cp(S[:, 0, :], Sb[:, C, :])
                        settle()
                        ts(maskC[:, :], contC[:, :], -1.0, BIG, ALU.add, ALU.mult)
                        dve.wait_ge(q_in[u], l * (16 * (NCH // 2)) + i * 16 + 16)
                        cp(ql[:, :], qlb[:, :])
                        settle()
                        for k in range(D):
                            scan(Q[:, :, k], contC[:, :], Q[:, :, k], ql[:, k:k + 1], ALU.mult, ALU.add)
                        settle()
                        cp(qlb[:, :], Q[:, C - 1, :])
                        for s in range(PT):
                            b = 2 * (s % 4)
                            dve.wait_ge(kv_ready, n * PT + s + 1)
                            tt(PR[:, 8 * s:8 * s + 8, :], PS[:, b, :].rearrange("p (t d) -> p t d", t=8),
                               Q[:, 8 * s:8 * s + 8, :], ALU.mult).then_inc(k_used, 1)
                        settle()
                        red(al1[:, :, :], PR[:, :, :].rearrange("p t (h d) -> p t h d", h=H), AX.X, ALU.add)
                        settle()
                        for h in range(H):
                            scan(S[:, 1:C + 1, h], maskC[:, :], al1[:, :, h], S[:, 0, h:h + 1], ALU.add, ALU.max)
                        settle()
                        tt(dd1[:, 0, :, :], S[:, 0:C, 0:H], along(maskC[:, :], [P, C, H]), ALU.add)
                        tt(dd1[:, 1, :, :], al1[:, :, :], S[:, 1:C + 1, 0:H], ALU.subtract)
                        settle()
                        tt(dd1[:, 0, :, :], dd1[:, 0, :, :], S[:, 1:C + 1, 0:H], ALU.subtract).then_inc(d1_ready, 1)
                        dve.wait_ge(e1_ready, n + 1)
                        vals = G[:, :, D:2 * D].rearrange("p t (h d) -> p t h d", h=H)
                        tt(vals, vals, along(ee1[:, 1, :, :], [P, C, H, HD]), ALU.mult)
                        for h in range(H):
                            scan(S[:, 1:C + 1, H + h], ee1[:, 0, :, h], ee1[:, 1, :, h], S[:, 0, H + h:H + h + 1], ALU.mult, ALU.add)
                        settle()
                        for k in range(D):
                            scan(S[:, 1:C + 1, 2 * H + k], ee1[:, 0, :, k // HD], G[:, :, D + k], S[:, 0, 2 * H + k:2 * H + k + 1], ALU.mult, ALU.add)
                        settle().then_inc(done1, 1)

                def spread1(row):
                    cp(MX[:, 0:H], row[:, 0:H])
                    cp(MX[:, H:V1].rearrange("p (h d) -> p h d", h=H), along(row[:, 0:H], [P, H, HD]))

                fix(V1, l + 1, None, lambda: spread1(S1[:, 1, C, :]), lambda: spread1(rfix), False)
                join(V1, H, H, R1, False)
                dve.wait_ge(rows_got, l * (16 * NT) + 32 * NT)
                ts(rden[:, :, :], rows1[:, :, H:2 * H], 1e-16, None, ALU.add)
                settle()
                v.reciprocal(rden[:, :, :], rden[:, :, :])
                settle()
                v.memset(nag[:, NT * D:], 0.0)
                for k in range(NB):
                    c0, w = BLK[k]
                    t0, t1 = 2 * c0 // P, min(2 * (c0 + w) // P, NT)
                    tt(nag[:, t0 * D:t1 * D].rearrange("p (t h d) -> p t h d", h=H, d=HD),
                       rows1[:, t0:t1, 2 * H:R1].rearrange("p t (h d) -> p t h d", h=H),
                       rden[:, t0:t1, :].unsqueeze(3).broadcast_to([P, t1 - t0, H, HD]), ALU.mult)
                    settle().then_inc(b_dve, 1)
                p0 = l * (11 * NB)
                a0 = l * (8 * NB)

                def mix(k, c0, w):
                    stt(nB4[:, c0:c0 + w], PS[:, k, 0:w], cb[:, BSELF:BSELF + 1], nB2[:, c0:c0 + w], ALU.add, ALU.subtract)
                    settle()
                    tt(nB4[:, c0:c0 + w], nB4[:, c0:c0 + w], nB3[:, c0:c0 + w], ALU.mult)
                    settle()
                    return tt(nB4[:, c0:c0 + w], nB4[:, c0:c0 + w], nB2[:, c0:c0 + w], ALU.add)

                def onto_x(bias):
                    return lambda k, c0, w: stt(nX[:, c0:c0 + w], PS[:, k, 0:w], cb[:, bias:bias + 1], nX[:, c0:c0 + w], ALU.add, ALU.add)

                per_block(mix, b_dve, b_pe, p0, 2 * NB)
                per_block(onto_x(BOUT), b_dve, b_pe, p0, 3 * NB)
                per_block(centre(nX), b_dve, b_pe, p0, 4 * NB)
                per_block(normed(nB5, N2G, N2B), b_dve, b_act, a0, 3 * NB)
                per_block(onto_x(MB2), b_dve, b_pe, p0, 10 * NB)
                settle()

            per_block(centre(nX), c_dve, c_pe, 0, 0)
            for k in range(NB):
                c0, w = BLK[k]
                dve.wait_ge(c_act, NB + k + 1)
                normed(nB2, NGC, NBC)(k, c0, w)
                settle()
                tt(nB2[:, c0:c0 + w], nB2[:, c0:c0 + w], nH[:, c0:c0 + w], ALU.add).then_inc(c_dve, 1)
            per_block(centre(nB2), c_dve, c_pe, 0, 2 * NB)
            per_block(normed(None, None, None), c_dve, c_act, 0, 3 * NB)
            per_block(lambda k, c0, w: cp(nag[:, c0:c0 + w], PS[:, k, 0:w]), c_dve, c_pe, 0, 4 * NB)

        first.close()
        second.close()


_INS = {'x': 'x', 'src': 'src', 'dst': 'dst', 'edge_attr_64': 'edge_attr_64', 'edge_weight1': 'edge_weight1',
        'Wa': 'L0_gnn_Wa', 'att_w': 'L0_gnn_att_w', 'Wg': 'L0_gnn_Wg', 'gate_w': 'L0_gnn_gate_w'}
_INS.update({n: 'L1_gnn_' + n for n in (
    'eng', 'enb', 'eW1', 'eb1', 'eW2', 'eb2', 'Wq', 'bq', 'Wkn', 'bkn', 'Wke', 'bke', 'Wvn', 'bvn', 'Wve', 'bve',
    'Wself', 'bself', 'Wih', 'bih', 'Whh', 'bhh', 'Wout', 'bout', 'n1g', 'n1b', 'n2g', 'n2b',
    'mW1', 'mb1', 'mW2', 'mb2', 'ng', 'nb')})


def kernel(**inputs):
    import numpy as _np
    import concourse.bacc as _bacc
    from concourse import mybir as _mybir
    from concourse.bass_utils import run_bass_kernel_spmd as _run

    nc = _bacc.Bacc("TRN2", target_bir_lowering=False, num_devices=1)
    rows = {'x': (NP, 0), 'src': (EP, 0), 'dst': (EP, N), 'edge_attr_64': (EP, 0), 'edge_weight1': (EP, 0)}
    arrays, aps = {}, {}
    for short, name in _INS.items():
        a = _np.ascontiguousarray(inputs[name])
        if short in rows:
            n, fill = rows[short]
            padded = _np.full((n,) + a.shape[1:], fill, a.dtype)
            padded[:a.shape[0]] = a
            a = padded
        arrays[f"in_{short}"] = a
        aps[short] = nc.dram_tensor(f"in_{short}", a.shape, _mybir.dt.from_np(a.dtype), kind="ExternalInput").ap()
    out = nc.dram_tensor("out_0", (NP, D), _mybir.dt.float32, kind="ExternalOutput").ap()
    build(nc, aps, out)
    r = _run(nc, [arrays], core_ids=[0])
    return r.results[0]["out_0"][:N]
```

```python
import concourse.bass as bass
from concourse import mybir
from contextlib import ExitStack

P = 128
N = 6250
E = 200000
D = 64
H = 8
HD = D // H
L = 3
HID = 4 * D
C = 56
NCH = 28
T = C * NCH
EP = P * T
NT = 49
NPR = (NT + 1) // 2
NP = 2 * NPR * P
NW = NPR * P
TG = 7
NG = NT // TG
GN = TG * P
BLK = [(512 * k, min(512, NW - 512 * k)) for k in range(-(-NW // 512))]
NB = len(BLK)
PAIRS = C // 2
PT = C // 8
BIG = 1e30
R0 = 3 + 2 * D
V0 = 2 + D
R1 = 2 * H + D
V1 = H + D
W0 = 2 * D + 3
SCALE = float(HD) ** -0.5
NWIN = 18
NTW, NLW = 19, 30
A_DVE = 3 * NB
B_PE, B_ACT, B_DVE = 11, 8, 5
HALVES = (range(0, 3), range(3, NB))

PD_RP, PD_END = 8, 9
BSELF, BIH, BHH, BOUT, MB2, N1G, N1B, N2G, N2B, NGC, NBC = range(11)


def after(steps, step, k):
    half = HALVES[0] if k in HALVES[0] else HALVES[1]
    return steps * half.start + step * len(half) + k - half.start + 1


def build(nc, A, out):
    f32, bf16, i32 = mybir.dt.float32, mybir.dt.bfloat16, mybir.dt.int32
    ALU, ACT, AX = mybir.AluOpType, mybir.ActivationFunctionType, mybir.AxisListType
    IND = bass.IndirectOffsetOnAxis
    ctx = ExitStack()

    def dram(name, shape, dt=f32):
        return nc.dram_tensor(name, shape, dt, kind="Internal").ap()

    tab0 = dram("tab0", (NT * P, W0))
    tabkv = dram("tabkv", (NP, 2 * D))
    tabq = dram("tabq", (NP, D))
    s2exp = dram("s2exp", (EP + NP, 1))
    qexp = dram("qexp", (EP + NP, D))
    st0 = dram("st0", (EP + 1 + P, R0))
    st1 = dram("st1", (EP + 1 + P, R1))
    eaT = dram("eaT", (NCH, P, PAIRS * P))
    xTd = dram("xTd", (P, NW))
    x1Td = dram("x1Td", (P, NW))
    hTd = dram("hTd", (P, NW))
    rptr = dram("rptr", (NT * P, 2))

    def chunk_rows(t, width, c):
        return t[0:EP, :].rearrange("(p t) w -> p (t w)", p=P)[:, bass.ds(c * (C * width), C * width)]

    src_pt = A["src"].rearrange("(p t) -> p t", p=P)
    ew_pt = A["edge_weight1"].rearrange("(p t) o -> p (t o)", p=P)

    with ctx:
        def sbx(stack):
            return lambda name, shape, dt=f32: stack.enter_context(nc.sbuf_tensor(name, shape, dt))

        def sem(name):
            return ctx.enter_context(nc.semaphore(name))

        sb = sbx(ctx)
        ident = sb("ident", [P, P])
        onesD = sb("onesD", [P, P])
        cont = sb("cont", [P, T])
        srcI = sb("srcI", [P, 2, C], i32)
        firstI = sb("firstI", [P, 1], i32)
        endI = sb("endI", [P, NT], i32)
        startI = sb("startI", [P, NT], i32)
        fixI = sb("fixI", [P, 1], i32)
        gmask = sb("gmask", [V1, P])
        contC = sb("contC", [P, C])
        maskC = sb("maskC", [P, C])
        zeros = sb("zeros", [P, C * D // 8])
        iotaFX = sb("iotaFX", [P, 1])
        epsc = sb("epsc", [P, 1])
        MX = sb("MX", [P, V1])
        MXT = sb("MXT", [V1, P])
        MT = sb("MT", [V1, P])
        VT = sb("VT", [V1, P])
        sh = sb("sh", [V1, 2, P])
        ab = sb("ab", [P, 2, P])
        abE = sb("abE", [P, 2, P])
        FMT = sb("FMT", [D, 2, P])
        wide = sb("wide", [P, 2, V1])
        rfix = sb("rfix", [P, R0])
        wfix = sb("wfix", [P, R0])
        Wkvp = sb("Wkvp", [P, 4 * D])
        Wqkv = sb("Wqkv", [P, 6 * D])
        Wn = sb("Wn", [P, 4, P])
        mW1s = sb("mW1s", [P, 2, HID])
        mW2s = sb("mW2s", [P, 2, 2, P])
        mb1c = sb("mb1c", [P, 2])
        bqkv = sb("bqkv", [P, 5, D])
        cb = sb("cb", [P, 12])
        bgc = sb("bgc", [P, 1])
        bkv = sb("bkv", [P, 2, D])
        PS = ctx.enter_context(nc.psum_tensor("PS", [P, 8, 512], f32))
        PSf = PS[:, :, :].rearrange("p b n -> p (b n)")

        w_in = sem("w_in")
        pool_c = sem("pool_c")
        p_dve = sem("p_dve")
        p_pe = sem("p_pe")
        p_rp = sem("p_rp")
        rp_first = sem("rp_first")
        p_z = sem("p_z")
        oh_ready = sem("oh_ready")
        oh_used = sem("oh_used")
        waits_sp, waits_pool, waits_pe = sem("waits_sp"), sem("waits_pool"), sem("waits_pe")
        n0_x, n0_pe, n0_act, n0_tab, n0_free = (sem(n) for n in ("n0_x", "n0_pe", "n0_act", "n0_tab", "n0_free"))
        s2_put = sem("s2_put")
        s2_first = sem("s2_first")
        idx0 = [sem(f"idx0_{u}") for u in range(2)]
        in0 = [sem(f"in0_{u}") for u in range(2)]
        xe_in = [sem(f"xe_in{u}") for u in range(2)]
        got0 = [sem(f"got0_{u}") for u in range(2)]
        seen0 = sem("seen0")
        done0 = sem("done0")
        xe_free = sem("xe_free")
        d0_ready, e0_ready = sem("d0_ready"), sem("e0_ready")
        ln_ready = sem("ln_ready")
        cen_ready, sq_ready = sem("cen_ready"), sem("sq_ready")
        var_ready, sqrt_ready, xn_ready = sem("var_ready"), sem("sqrt_ready"), sem("xn_ready")
        st0_out = [sem(f"st0_out{u}") for u in range(2)]
        m_pe, m_act = sem("m_pe"), sem("m_act")
        ea_out = sem("ea_out")
        zq = sem("zq")
        f_pe, f_dve, f_act, f_got, f_put = (sem(n) for n in ("f_pe", "f_dve", "f_act", "f_got", "f_put"))
        rows_got = [sem(f"rows_got{k}") for k in range(NB)]
        u_x, u_dve, u_act, u_pe, u_out = (sem(n) for n in ("u_x", "u_dve", "u_act", "u_pe", "u_out"))
        l_w = sem("l_w")
        l_t = sem("l_t")
        a_x, a_pe, a_dve, a_act, h_out = (sem(n) for n in ("a_x", "a_pe", "a_dve", "a_act", "h_out"))
        a_out = [sem(f"a_out{k}") for k in range(2)]
        q_dram, q_put, q_first, q_done = (sem(n) for n in ("q_dram", "q_put", "q_first", "q_done"))
        idx1 = [sem(f"idx1_{u}") for u in range(2)]
        q_in = [sem(f"q_in{u}") for u in range(2)]
        ea_in = [sem(f"ea_in{u}") for u in range(2)]
        got1 = [[sem(f"got1_{u}_{k}") for k in range(PT)] for u in range(2)]
        seen1 = sem("seen1")
        done1 = sem("done1")
        kv_ready = sem("kv_ready")
        k_used = sem("k_used")
        v_moved = sem("v_moved")
        d1_ready, e1_ready = sem("d1_ready"), sem("e1_ready")
        st1_out = [sem(f"st1_out{u}") for u in range(2)]
        sums_ready = sem("sums_ready")
        b_x, b_pe, b_dve, b_act, b_out = (sem(n) for n in ("b_x", "b_pe", "b_dve", "b_act", "b_out"))
        c_x, c_pe, c_dve, c_act, c_out = (sem(n) for n in ("c_x", "c_pe", "c_dve", "c_act", "c_out"))

        first = ExitStack()
        sb = sbx(first)
        Wcat = sb("Wcat", [D, 132])
        Wa_s = sb("Wa_s", [D, D])
        WaT = sb("WaT", [D, D])
        attc = sb("attc", [D, 2])
        gw2r = sb("gw2r", [P, D])
        W1raw = sb("W1raw", [P, HID])
        engc = sb("engc", [P, 1])
        enbc = sb("enbc", [D, 1])
        eb1c = sb("eb1c", [P, 2])
        b1c = sb("b1c", [P, 2])
        b2c = sb("b2c", [P, 1])
        W1p = sb("W1p", [P, 2, 2, P])
        W2p = sb("W2p", [P, 2, 2, P])
        W2raw = sb("W2raw", [P, 2, D])
        s2n = sb("s2n", [P, NT])
        xg1 = sb("xg1", [P, NT])
        degn = sb("degn", [P, NT])
        G0 = sb("G0", [P, 2, C, W0])
        S0 = sb("S0", [P, 2, C + 1, R0])
        xe = sb("xe", [P, 2, C, D])
        eaC = sb("eaC", [P, PAIRS, P])
        xT8 = sb("xT8", [P, 512])
        hid8 = sb("hid8", [P, 2, 2, 512])
        ewC = sb("ewC", [P, 2, C])
        s2C = sb("s2C", [P, 2, C])
        s2x = sb("s2x", [P, C + 1])
        al0 = sb("al0", [P, C])
        uw0 = sb("uw0", [P, C])
        dd0 = sb("dd0", [P, 2, C])
        ee0 = sb("ee0", [P, 2, C])
        mu8 = sb("mu8", [P, C])
        sd8 = sb("sd8", [P, C])
        rs8 = sb("rs8", [P, C])
        G0f = G0[:, :, :, :].rearrange("p u c w -> p (u c w)")
        S0f = S0[:, :, :, :].rearrange("p u c w -> p (u c w)")
        xef = xe[:, :, :, :].rearrange("p u c w -> p (u c w)")
        eaf = eaC[:, :, :].rearrange("p a b -> p (a b)")
        OHW = NT + P
        rep = G0f[:, C * W0:C * W0 + C * OHW // 2].bitcast(bf16)
        dstI, hiI, loI = (xef[:, 2460 + k * T:2460 + (k + 1) * T].bitcast(i32) for k in range(3))
        dstF = S0f[:, C * OHW:C * OHW + T]
        hiB, loB = (S0f[:, C * OHW + k * T:C * OHW + (k + 1) * T].bitcast(bf16)[:, 0:T] for k in (1, 2))
        oh = [S0f[:, u * (C * OHW // 2):(u + 1) * (C * OHW // 2)].bitcast(bf16)
              .rearrange("p (w c) -> p c w", c=C) for u in range(2)]
        ohf = [S0f[:, u * (C * OHW // 2):(u + 1) * (C * OHW // 2)].bitcast(bf16) for u in range(2)]
        at = [0]

        def eview(n):
            at[0] += n
            return eaf[:, at[0] - n:at[0]]

        iotaR = eview(P)
        iotaC = eview(1)
        iotaPT = eview(1)
        nodeE = eview(NT)
        tri = eview(P)
        degR = eview(P)
        cumR = eview(P)
        baseC = eview(1)
        endxR = eview(P)
        lastF = eview(NT)
        firstF = eview(NT)
        neF = eview(NT)
        tmpN = eview(NT)
        F1b = eview(V1)
        F2b = eview(V1)
        rowF = eview(P)
        rowL = eview(P)
        gF = eview(P)
        rpF = eview(2)
        vF = eview(4)
        rp_s = eview(2 * NT).rearrange("p (t o) -> p t o", o=2)
        zw = eview(P)
        xg = xef[:, 0:TG * D].rearrange("p (t d) -> p t d", t=TG)
        xTg = xef[:, 512:512 + GN]
        tg = xef[:, 1536:1536 + TG * 132].rearrange("p (t w) -> p t w", t=TG)
        rows0 = G0f[:, 0:NT * R0].rearrange("p (t w) -> p t w", t=NT)
        xn0p = S0f[:, 0:2 * NPR * D]
        xn0 = xn0p[:, 0:NT * D].rearrange("p (t d) -> p t d", t=NT)
        tp0 = S0f[:, 2 * NPR * D:(2 * NPR + NT) * D].rearrange("p (t d) -> p t d", t=NT)
        tq0 = S0f[:, (2 * NPR + NT) * D:(2 * NPR + 2 * NT) * D].rearrange("p (t d) -> p t d", t=NT)
        n49 = [S0f[:, 2 * (NPR + NT) * D + NT * k:2 * (NPR + NT) * D + NT * (k + 1)] for k in range(8)]
        xT0 = G0f[:, NT * R0:NT * R0 + NW]
        first.close()

        second = ExitStack()
        sb = sbx(second)
        G1 = sb("G1", [P, 2, C, 2 * D])
        Q1 = sb("Q1", [P, 2, C, D])
        PR = sb("PR", [P, C, D])
        S1 = sb("S1", [P, 2, C + 1, R1])
        EA = sb("EA", [P, 2, PAIRS, P])
        al1 = sb("al1", [P, C, H])
        dd1 = sb("dd1", [P, 2, C, H])
        ee1 = sb("ee1", [P, 2, C, H])
        qb = sb("qb", [P, D])
        ql = sb("ql", [P, D])
        qlb = sb("qlb", [P, D])
        G1f = G1[:, :, :, :].rearrange("p u c w -> p (u c w)")
        EAf = EA[:, :, :, :].rearrange("p u a b -> p (u a b)")
        nX, nH, nB2, nB3 = (G1f[:, k * NW:(k + 1) * NW] for k in range(4))
        nB4, nB5 = (EAf[:, k * NW:(k + 1) * NW] for k in range(2))
        Q1f = Q1[:, :, :, :].rearrange("p u c w -> p (u c w)")
        PRf = PR[:, :, :].rearrange("p c w -> p (c w)")
        q_all = PRf[:, 0:2 * NPR * D].rearrange("p (t d) -> p t d", d=D)
        nag = PRf[:, 0:2 * NPR * D]
        rows1 = Q1f[:, 0:NT * R1].rearrange("p (t w) -> p t w", t=NT)
        rden = Q1f[:, 4000:4000 + NT * H].rearrange("p (t h) -> p t h", t=NT)
        HIDDEN = (nH, nB2, nB3, nB4)
        nkv = [Q1f[:, 4608 + 1024 * k:4608 + 1024 * (k + 1)] for k in range(2)]

        def hold(eng, passed, s, value):
            eng.wait_ge(s, value)
            eng.sem_inc(passed, 1)

        block = ctx.enter_context(nc.Block())

        @block.sync
        def _(sp):
            loads = ((dstI[:, :], A["dst"].rearrange("(p t) -> p t", p=P)),
                     (Wa_s[:, :], A["Wa"]), (Wcat[:, 0:D], A["Wa"]), (Wcat[:, D:2 * D], A["Wg"]),
                     (attc[:, 0:1], A["att_w"][0:D, :]), (attc[:, 1:2], A["att_w"][D:2 * D, :]),
                     (Wcat[:, 131:132], A["gate_w"][0:D, :]), (Wcat[:, 129:130], A["gate_w"][2 * D:3 * D, :]),
                     (gw2r[:, :], A["gate_w"][D:2 * D, :].rearrange("d o -> o d").broadcast_to([P, D])),
                     (W1raw[0:D, :], A["eW1"]), (W1raw[D:P, :], A["eW1"]),
                     (engc[0:D, :], A["eng"].unsqueeze(1)), (engc[D:P, :], A["eng"].unsqueeze(1)),
                     (enbc[:, :], A["enb"].unsqueeze(1)),
                     (eb1c[:, :], A["eb1"].rearrange("(k p) -> p k", p=P)),
                     (b2c[0:D, :], A["eb2"].unsqueeze(1)), (b2c[D:P, :], A["eb2"].unsqueeze(1)),
                     (W2raw[:, :, :], A["eW2"].rearrange("(k p) d -> p k d", p=P)))
            assert len(loads) == NWIN
            for dst, s in loads:
                sp.dma_start(dst, s, allow_slow_non_contiguous=True).then_inc(w_in, 16)

            def load_features(g):
                sp.dma_start(xg[:, :, :], A["x"][bass.ds(g * GN, GN), :].rearrange("(t p) d -> p t d", p=P)).then_inc(n0_x, 16)

            load_features(0)

            def col(l, j, name, s):
                for q in range(2):
                    sp.dma_start(cb[q * D:(q + 1) * D, j:j + 1], A[name][bass.ds(l, 1), :].rearrange("o d -> d o"),
                                 allow_slow_non_contiguous=True).then_inc(s, 16)

            def mat(l, dst, name, s, rows=slice(0, D)):
                sp.dma_start(dst, A[name][bass.ds(l, 1), rows, :].rearrange("o a b -> (o a) b")).then_inc(s, 16)

            def table_weights(l):
                for j, name in ((N1G, "n1g"), (N1B, "n1b")):
                    col(l, j, name, l_t)
                for q in range(2):
                    rows = slice(q * D, (q + 1) * D)
                    for j, name in enumerate(("Wq", "Wkn", "Wvn")):
                        mat(l, Wqkv[rows, (3 * q + j) * D:(3 * q + j + 1) * D], name, l_t)
                    mat(l, Wkvp[rows, q * D:(q + 1) * D], "Wke", l_t)
                    mat(l, Wkvp[rows, (2 + q) * D:(3 + q) * D], "Wve", l_t)
                for j, name in enumerate(("bq", "bkn", "bvn", "bke", "bve")):
                    sp.dma_start(bqkv[:, j, :], A[name][bass.ds(l, 1), :].broadcast_to([P, D])).then_inc(l_t, 16)

            sp.wait_ge(p_dve, 1)
            sp.dma_start(s2exp[0:EP, :].rearrange("(p k t) o -> p k (t o)", p=P, k=4),
                         zeros[:, 0:T // 4].unsqueeze(1).broadcast_to([P, 4, T // 4])).then_inc(p_z, 16)
            sp.dma_start(st0[EP:EP + 1, :], zeros[0:1, 0:R0]).then_inc(st0_out[0], 16)
            sp.dma_start(st0[EP + 1:EP + 1 + P, :], zeros[:, 0:R0]).then_inc(st0_out[1], 16)
            sp.dma_start(st1[EP:EP + 1, :], zeros[0:1, 0:R1]).then_inc(st1_out[0], 16)
            sp.dma_start(st1[EP + 1:EP + 2, :], zeros[0:1, 0:R1]).then_inc(ea_out, 16)
            sp.dma_start(st1[EP + 2:EP + 1 + P, :], zeros[0:P - 1, 0:R1]).then_inc(st1_out[1], 16)
            for u in range(2):
                sp.dma_start(srcI[:, u, :], src_pt[:, u * C:(u + 1) * C]).then_inc(idx0[u], 16)
            table_weights(0)
            def store_tables(g):
                sp.wait_ge(n0_act, 4 * g + 4)
                sp.dma_start(tab0[bass.ds(g * GN, GN), :].rearrange("(t p) w -> p t w", p=P), tg[:, :, 0:W0]).then_inc(n0_tab, 16)

            with sp.Fori(0, NG - 1) as g:
                sp.wait_ge(n0_pe, 2 * g + 1)
                load_features(g + 1)
                store_tables(g)
                sp.wait_ge(n0_tab, 16 * g + 16)
                sp.sem_inc(n0_free, 1)
            store_tables(NG - 1)
            sp.wait_ge(p_dve, PD_RP)
            sp.dma_start(rptr[0:NT * P, :].rearrange("(t p) o -> p t o", p=P), rp_s[:, :, :]).then_inc(p_rp, 16)
            sp.wait_ge(p_dve, PD_END)
            sp.wait_ge(s2_put, 16 * NT)
            sp.wait_ge(s2_first, 16)
            sp.dma_start(s2exp[0:EP, :].rearrange("(p t) o -> p (t o)", p=P)[:, 0:1], rfix[:, W0 - 1:W0],
                         allow_slow_non_contiguous=True).then_inc(p_z, 16)
            sp.wait_ge(p_z, 32)

            def loads(c, u, index):
                if index:
                    sp.wait_ge(seen0, c + 1)
                    sp.dma_start(srcI[:, u, :], src_pt[:, bass.ds(c * C, C)]).then_inc(idx0[u], 16)
                sp.wait_ge(xe_free, c + 1)
                sp.dma_start(xe[:, u, :, :].rearrange("p c d -> p (c d)"), chunk_rows(A["edge_attr_64"], D, c)).then_inc(xe_in[u], 16)
                sp.wait_ge(done0, c + 1)
                sp.dma_start(ewC[:, u, :], ew_pt[:, bass.ds(c * C, C)]).then_inc(in0[u], 16)
                sp.dma_start(s2C[:, u, :], chunk_rows(s2exp, 1, c)).then_inc(in0[u], 16)
                sp.dma_start(chunk_rows(qexp, D, c).rearrange("p (k n) -> p k n", k=8),
                             zeros[:, :].unsqueeze(1).broadcast_to([P, 8, C * D // 8])).then_inc(zq, 16)

            for u in range(2):
                loads(u, u, False)
            with sp.Fori(1, NCH // 2) as i:
                for u in range(2):
                    loads(2 * i + u, u, True)
            sp.wait_ge(f_dve, 5)
            for u in range(2):
                sp.wait_ge(st0_out[u], 16 * (NCH // 2 + 1))
            sp.dma_start(xn0p.rearrange("p (t d) -> p t d", d=D), A["x"].rearrange("(t p) d -> p t d", p=P)).then_inc(u_x, 16)
            sp.wait_ge(u_act, 1 + 2 * NB)
            sp.dma_start(x1Td[:, :], xT0[:, :]).then_inc(u_out, 16)
            sp.wait_ge(u_out, 16)
            sp.wait_ge(zq, 16 * NCH)
            sp.wait_ge(ea_out, 16 * (NCH + 1))
            sp.dma_start(nX, x1Td[:, :]).then_inc(a_x, 16)
            sp.wait_ge(a_x, 16)
            with sp.Fori(0, L) as l:
                for j, name in ((BSELF, "bself"), (BIH, "bih"), (BHH, "bhh"), (BOUT, "bout"), (MB2, "mb2"),
                                (N2G, "n2g"), (N2B, "n2b")):
                    col(l, j, name, l_w)
                for q in range(2):
                    rows = slice(q * D, (q + 1) * D)
                    for j, name in enumerate(("Wself", "Wih", "Whh", "Wout")):
                        mat(l, Wn[rows, j, q * D:(q + 1) * D], name, l_w)
                    mat(l, mW1s[rows, q, :], "mW1", l_w)
                    for kh in range(2):
                        mat(l, mW2s[:, kh, q, q * D:(q + 1) * D], "mW2", l_w, slice(kh * P, (kh + 1) * P))
                for kh in range(2):
                    sp.dma_start(mb1c[:, kh:kh + 1], A["mb1"][bass.ds(l, 1), kh * P:(kh + 1) * P].rearrange("o d -> d o"),
                                 allow_slow_non_contiguous=True).then_inc(l_w, 16)
                sp.dma_start(xTd[:, :], nX).then_inc(h_out, 16)
                for k in range(NB):
                    hold(sp, waits_sp, a_dve, l * A_DVE + 2 * NB + k + 1)
                    c0, w = BLK[k]
                    sp.dma_start(tabkv[2 * c0:2 * (c0 + w), :].rearrange("(t p) w -> p t w", p=P),
                                 nkv[k % 2][:, 0:2 * w].rearrange("p (t w) -> p t w", w=2 * D)).then_inc(a_out[k % 2], 16)
                sp.dma_start(hTd[:, :], nH).then_inc(h_out, 16)
                sp.dma_start(tabq[:, :].rearrange("(t p) d -> p t d", p=P), q_all[:, :, :]).then_inc(q_dram, 16)
                hold(sp, waits_sp, q_put, (l + 1) * (16 * NT))
                hold(sp, waits_sp, q_first, (l + 1) * 16)
                sp.dma_start(qexp[0:EP, :].rearrange("(p t) d -> p t d", p=P)[:, 0, :], qb[:, :]).then_inc(q_done, 16)
                hold(sp, waits_sp, q_done, (l + 1) * 16)
                hold(sp, waits_sp, h_out, (l + 1) * 32)
                for k in range(2):
                    hold(sp, waits_sp, a_out[k], (l + 1) * (16 * ((NB + 1 - k) // 2)))
                with sp.Fori(0, NCH // 2) as i:
                    for u in range(2):
                        c = 2 * i + u
                        sp.wait_ge(seen1, l * NCH + c + 1)
                        sp.dma_start(srcI[:, u, :], src_pt[:, bass.ds(c * C, C)]).then_inc(idx1[u], 16)
                        sp.wait_ge(done1, l * NCH + c + 1)
                        sp.dma_start(EA[:, u, :, :].rearrange("p a b -> p (a b)"),
                                     eaT[bass.ds(c, 1), :, :].rearrange("o p n -> (o p) n")).then_inc(ea_in[u], 16)
                        sp.dma_start(Q1[:, u, :, :].rearrange("p c d -> p (c d)"), chunk_rows(qexp, D, c)).then_inc(q_in[u], 16)
                hold(sp, waits_sp, f_dve, l * 5 + 10)
                sp.dma_start(nH, hTd[:, :]).then_inc(b_x, 16)
                sp.dma_start(nX, xTd[:, :]).then_inc(b_x, 16)
                table_weights(l + 1)
                hold(sp, waits_sp, b_dve, (l + 1) * (B_DVE * NB) + 1)
            for q in range(2):
                for j, name in ((NGC, "ng"), (NBC, "nb")):
                    sp.dma_start(cb[q * D:(q + 1) * D, j:j + 1], A[name].unsqueeze(1), allow_slow_non_contiguous=True).then_inc(c_x, 16)
            sp.dma_start(nH, x1Td[:, :]).then_inc(c_x, 16)
            for k in range(NB):
                sp.wait_ge(c_dve, 4 * NB + k + 1)
                c0, w = BLK[k]
                sp.dma_start(out[2 * c0:2 * (c0 + w), :].rearrange("(t p) d -> p t d", p=P),
                             nag[:, c0:c0 + w].rearrange("p (t d) -> p t d", d=D)).then_inc(c_out, 16)
            sp.wait_ge(c_out, 16 * NB)

        @block.gpsimd
        def _(pool):
            exact = dict(allow_small_or_imprecise_dtypes=True)
            nc.gpsimd.iota(iotaR[:, :], [[1, P]], base=0, channel_multiplier=0, **exact)
            nc.gpsimd.iota(iotaC[:, :], [[1, 1]], base=0, channel_multiplier=1, **exact)
            nc.gpsimd.iota(iotaPT[:, :], [[1, 1]], base=0, channel_multiplier=T, **exact)
            nc.gpsimd.iota(iotaFX[:, :], [[1, 1]], base=EP + 1, channel_multiplier=1, **exact)
            nc.gpsimd.iota(nodeE[:, :], [[P, NT]], base=EP, channel_multiplier=1, **exact)
            for first, w in ((0, NT), (NT, P)):
                last = nc.gpsimd.iota(rep[:, first * C:(first + w) * C].rearrange("p (w c) -> p w c", c=C),
                                      [[1, w], [0, C]], base=0, channel_multiplier=0, **exact)
            last.then_inc(pool_c, 1)

            def gathers(u, G, tab, got):
                for t in range(C):
                    nc.gpsimd.indirect_dma_start(out=G[:, u, t, :], out_offset=None, in_=tab[:, :],
                                                 in_offset=IND(ap=srcI[:, u, t:t + 1], axis=0)).then_inc(got(t), 16)

            pool.wait_ge(n0_tab, 16 * NG)
            pool.wait_ge(idx0[0], 16)
            gathers(0, G0, tab0, lambda t: got0[0])
            pool.wait_ge(p_rp, 16)
            nc.gpsimd.indirect_dma_start(out=rpF[:, :], out_offset=None, in_=rptr[:, :],
                                         in_offset=IND(ap=firstI[:, 0:1], axis=0)).then_inc(rp_first, 16)
            pool.wait_ge(p_z, 16)
            for j in range(NT):
                nc.gpsimd.indirect_dma_start(out=s2exp[:, :], out_offset=IND(ap=startI[:, j:j + 1], axis=0),
                                             in_=s2n[:, j:j + 1], in_offset=None).then_inc(s2_put, 16)
            nc.gpsimd.indirect_dma_start(out=rfix[:, 0:W0], out_offset=None, in_=tab0[:, :],
                                         in_offset=IND(ap=firstI[:, 0:1], axis=0)).then_inc(s2_first, 16)
            pool.wait_ge(p_dve, 6)
            pool.wait_ge(idx0[1], 16)
            gathers(1, G0, tab0, lambda t: got0[1])
            with pool.Fori(1, NCH // 2) as i:
                for u in range(2):
                    pool.wait_ge(idx0[u], 16 * i + 16)
                    hold(pool, waits_pool, done0, 2 * i + u + 1)
                    gathers(u, G0, tab0, lambda t: got0[u])

            def fix_and_fetch(st, R, o, outs, stored, rows):
                for u in range(2):
                    hold(pool, waits_pool, outs[u], stored)
                nc.gpsimd.indirect_dma_start(out=rfix[:, 0:R], out_offset=None, in_=st[:, :],
                                             in_offset=IND(ap=fixI[:, 0:1], axis=0)).then_inc(f_got, 16)
                hold(pool, waits_pool, f_dve, o * 5 + 5)
                nc.gpsimd.indirect_dma_start(out=st[:, :], out_offset=IND(ap=fixI[:, 0:1], axis=0),
                                             in_=wfix[:, 0:R], in_offset=None).then_inc(f_put, 16)
                hold(pool, waits_pool, f_put, o * 16 + 16)
                for j in range(NT):
                    nc.gpsimd.indirect_dma_start(out=rows[:, j, :], out_offset=None, in_=st[:, :],
                                                 in_offset=IND(ap=endI[:, j:j + 1], axis=0)).then_inc(rows_got[j // 8], 16)

            fix_and_fetch(st0, R0, 0, st0_out, 16 * (NCH // 2 + 1), rows0)

            with pool.Fori(0, L) as l:
                for j in range(NT):
                    if j % 8 == 0:
                        hold(pool, waits_pool, a_dve, l * A_DVE + 2 * NB + j // 8 + 1)
                    nc.gpsimd.indirect_dma_start(out=qexp[:, :], out_offset=IND(ap=startI[:, j:j + 1], axis=0),
                                                 in_=q_all[:, j, :], in_offset=None).then_inc(q_put, 16)
                hold(pool, waits_pool, q_dram, l * 16 + 16)
                nc.gpsimd.indirect_dma_start(out=qb[:, :], out_offset=None, in_=tabq[:, :],
                                             in_offset=IND(ap=firstI[:, 0:1], axis=0)).then_inc(q_first, 16)
                for k in range(2):
                    hold(pool, waits_pool, a_out[k], (l + 1) * (16 * ((NB + 1 - k) // 2)))
                hold(pool, waits_pool, h_out, (l + 1) * 32)
                with pool.Fori(0, NCH // 2) as i:
                    for u in range(2):
                        c = 2 * i + u
                        pool.wait_ge(idx1[u], l * (NCH // 2 * 16) + i * 16 + 16)
                        hold(pool, waits_pool, done1, l * NCH + c + 1)
                        gathers(u, G1, tabkv, lambda t: got1[u][t // 8])
                fix_and_fetch(st1, R1, l + 1, st1_out, l * (NCH // 2 * 16) + 16 * (NCH // 2 + 1), rows1)

        @block.tensor
        def _(pe):
            mm, tr = nc.tensor.matmul, nc.tensor.transpose
            pe.wait_ge(w_in, 16 * NWIN)
            pe.wait_ge(p_dve, 2)
            tr(PS[0:D, 6, 0:D], Wa_s[:, :], ident[0:D, 0:D])
            mm(PS[:, 7, 0:1], W1raw[0:D, 0:P], enbc[:, :], start=True, stop=True)
            mm(PS[:, 7, 1:2], W1raw[0:D, P:2 * P], enbc[:, :], start=True, stop=True).then_inc(p_pe, 1)
            pe.wait_ge(p_dve, 4)
            mm(PS[0:D, 6, 64:66], WaT[:, :], attc[:, :], start=True, stop=True).then_inc(p_pe, 1)
            pe.wait_ge(p_dve, 5)
            zb = zw[:, :].bitcast(bf16)
            mm(PS[0:NT, 7, 0:P], zb[:, 0:NT], zb[:, 0:P], start=True, stop=False, skip_group_check=True)

            def degrees(c, u):
                pe.wait_ge(oh_ready, 2 * c + 2)
                for t in range(C):
                    last = mm(PS[0:NT, 7, 0:P], oh[u][:, t, 0:NT], oh[u][:, t, NT:OHW], start=False, stop=False,
                              skip_group_check=True)
                last.then_inc(oh_used, 1)

            pe.sem_inc(n0_free, 1)
            with pe.Fori(0, NG) as g:
                hold(pe, waits_pe, n0_x, 16 * g + 16)
                for j in range(TG):
                    last = tr(PSf[0:D, 2048 + j * P:2048 + (j + 1) * P], xg[:, j, :], ident[:, :])
                last.then_inc(n0_pe, 1)
                degrees(2 * g, 0)
                pe.wait_ge(n0_act, 4 * g + 1)
                for j in range(TG):
                    last = mm(PSf[:, j * 256:j * 256 + 132], xTg[0:D, j * P:(j + 1) * P], Wcat[:, :], start=True, stop=True)
                last.then_inc(n0_pe, 1)
                degrees(2 * g + 1, 1)
            with pe.Fori(NG, NCH // 2) as i:
                for u in range(2):
                    degrees(2 * i + u, u)
            mm(PS[0:NT, 7, 0:P], zb[:, 0:NT], zb[:, 0:P], start=False, stop=True, skip_group_check=True).then_inc(p_pe, 1)
            pe.wait_ge(n0_act, 4 * NG)
            pe.wait_ge(p_dve, 6)
            mm(PS[0:NT, 1, 0:1], tri[0:NT, 0:NT], cumR[0:NT, P - 1:P], start=True, stop=True).then_inc(p_pe, 1)
            pe.wait_ge(p_dve, 7)
            tr(PS[:, 2, 0:NT], endxR[0:NT, :], ident[0:NT, 0:NT])
            tr(PS[:, 3, 0:NT], degR[0:NT, :], ident[0:NT, 0:NT])
            tr(PS[0:V1, 4, 0:P], F1b[:, :], ident[:, :])
            tr(PS[0:V1, 5, 0:P], F2b[:, :], ident[:, :]).then_inc(p_pe, 1)
            pe.wait_ge(p_dve, PD_END)

            def turn(u, s):
                for j in range(4):
                    t = 8 * s + 2 * j
                    last = tr(PS[:, 0, j * P:(j + 1) * P], xe[:, u, t:t + 2, :].rearrange("p a d -> p (a d)"), ident[:, :])
                last.then_inc(m_pe, 1)

            with pe.Fori(0, NCH // 2) as i:
                for u in range(2):
                    c = 2 * i + u
                    pe.wait_ge(xn_ready, c + 1)
                    turn(u, 0)
                    for s in range(PT):
                        pe.wait_ge(m_act, 42 * c + (1 if s == 0 else 6 * s))
                        for r in range(2):
                            for kh in range(2):
                                last = mm(PS[:, 1 + 2 * r + kh, :], W1p[:, r, kh, :], xT8[:, :], start=True, stop=True)
                            last.then_inc(m_pe, 1)
                        if s < PT - 1:
                            turn(u, s + 1)
                        for r in range(2):
                            pe.wait_ge(m_act, 42 * c + 6 * s + 3 + 2 * r)
                            for kh in range(2):
                                last = mm(PS[:, 5, :], W2p[:, kh, r, :], hid8[:, r, kh, :],
                                          start=(r == 0 and kh == 0), stop=(r == 1 and kh == 1))
                        last.then_inc(m_pe, 1)

            def fix(V, o, maxes, fm):
                pe.wait_ge(f_dve, o * 5 + 1)
                if fm is not None:
                    tr(PS[0:D, 2, 0:P], fm, ident[:, :])
                tr(PS[0:V, 0, 0:P], MX[:, 0:V], ident[:, :])
                tr(PS[0:V, 1, 0:P], maxes, ident[:, :]).then_inc(f_pe, 1)
                pe.wait_ge(f_dve, o * 5 + 3)
                if fm is not None:
                    tr(PS[:, 5, 0:D], FMT[:, 1, :], ident[0:D, 0:D])
                tr(PS[:, 3, 0:V], sh[0:V, 0, :], ident[0:V, 0:V])
                tr(PS[:, 4, 0:V], sh[0:V, 1, :], ident[0:V, 0:V]).then_inc(f_pe, 1)

            fix(V0, 0, S0[:, 1, C, 1:1 + V0], S0[:, 1, C, 1 + V0:R0])
            for k in range(NB):
                c0, w = BLK[k]
                pe.wait_ge(u_dve, NB + 2 + k)
                for j in range(w // P):
                    m = c0 // P + j
                    last = tr(PS[:, k, j * P:(j + 1) * P], xn0p[:, m * P:(m + 1) * P], ident[:, :])
                last.then_inc(u_pe, 1)

            def per_block(step, done, sem_, base, first):
                for k in range(NB):
                    hold(pe, waits_pe, sem_, base + first + k + 1)
                    step(k, *BLK[k]).then_inc(done, 1)

            def means(src):
                return lambda k, c0, w: mm(PS[:, k, 0:w], onesD[:, :], src[:, c0:c0 + w], start=True, stop=True)

            pe.wait_ge(a_x, 16)
            with pe.Fori(0, L) as l:
                hold(pe, waits_pe, l_t, (l + 1) * (16 * NTW))
                hold(pe, waits_pe, b_dve, l * (B_DVE * NB) + 1)
                for k in range(NB):
                    means(nX)(k, *BLK[k]).then_inc(a_pe, 1)
                per_block(means(nB3), a_pe, a_act, l * (2 * NB), 0)
                for k in range(NB):
                    c0, w = BLK[k]
                    hold(pe, waits_pe, a_dve, l * A_DVE + NB + k + 1)
                    if k == 0:
                        hold(pe, waits_pe, a_act, (l + 1) * (2 * NB))
                    if k >= 2:
                        hold(pe, waits_pe, a_dve, l * A_DVE + 2 * NB + k - 1)
                    for j in range(w // P):
                        last = mm(PS[:, 4 * (k % 2) + j, 0:6 * D], nH[:, c0 + j * P:c0 + (j + 1) * P], Wqkv[:, :], start=True, stop=True)
                    last.then_inc(a_pe, 1)
                with pe.Fori(0, NCH // 2) as i:
                    for u in range(2):
                        n = l * NCH + 2 * i + u
                        pe.wait_ge(ea_in[u], l * (NCH // 2 * 16) + i * 16 + 16)
                        for s in range(PT):
                            pe.wait_ge(got1[u][s], l * (NCH // 2 * 128) + i * 128 + 128)
                            if s == PT - 1:
                                pe.sem_inc(seen1, 1)
                            b = 2 * (s % 4)
                            pe.wait_ge(k_used, n * PT + s + (2 if s < 3 else 1))
                            pe.wait_ge(v_moved, n * PT + s + (2 if s < 3 else 1))
                            for k in range(2):
                                mm(PS[:, b + k, :], ident[:, :], G1[:, u, 8 * s:8 * s + 8, k * D:(k + 1) * D],
                                   start=True, stop=False, skip_group_check=True)
                            for j in range(4):
                                for k in range(2):
                                    last = mm(PS[:, b + k, P * j:P * j + P], EA[:, u, 4 * s + j, :], Wkvp[:, k * P:(k + 1) * P],
                                              start=False, stop=True, skip_group_check=True)
                            last.then_inc(kv_ready, 1)
                fix(V1, l + 1, S1[:, 1, C, H:R1], None)
                hold(pe, waits_pe, l_w, (l + 1) * (16 * NLW))
                B = l * (B_DVE * NB) + 1

                def turned(k, c0, w):
                    for j in range(w // P):
                        last = tr(PS[:, k, j * P:(j + 1) * P], nag[:, c0 + j * P:c0 + (j + 1) * P], ident[:, :])
                    return last

                def gates(k, c0, w):
                    mm(PS[:, k, 0:w], Wn[:, 1, :], nB2[:, c0:c0 + w], start=True, stop=False)
                    return mm(PS[:, k, 0:w], Wn[:, 2, :], nH[:, c0:c0 + w], start=False, stop=True)

                def product(i, src):
                    return lambda k, c0, w: mm(PS[:, k, 0:w], Wn[:, i, :], src[:, c0:c0 + w], start=True, stop=True)

                def hidden(kh, q):
                    return lambda k, c0, w: mm(PS[:, k, 0:w], mW1s[:, q, kh * P:(kh + 1) * P], nB5[:, c0:c0 + w], start=True, stop=True)

                def folded(k, c0, w):
                    for n, src in enumerate(HIDDEN):
                        last = mm(PS[:, k, 0:w], mW2s[:, n // 2, n % 2, :], src[:, c0:c0 + w], start=(n == 0), stop=(n == 3))
                    return last

                A_ = l * (B_ACT * NB)

                def on(half, step, sem_, base, steps, awaited):
                    for k in half:
                        hold(pe, waits_pe, sem_, base + after(steps, awaited, k))
                        step(k, *BLK[k]).then_inc(b_pe, 1)

                for half in HALVES:
                    for k in half:
                        hold(pe, waits_pe, sums_ready, l * NB + k + 1)
                        turned(k, *BLK[k]).then_inc(b_pe, 1)
                    if half is HALVES[0]:
                        hold(pe, waits_pe, b_x, l * 32 + 32)
                    on(half, gates, b_act, A_, B_ACT, 0)
                    on(half, product(0, nH), b_act, A_, B_ACT, 1)
                    on(half, product(3, nB4), b_dve, B, B_DVE, 0)
                    on(half, means(nX), b_dve, B, B_DVE, 1)
                    on(half, means(nB3), b_act, A_, B_ACT, 2)
                    on(half, hidden(0, 0), b_dve, B, B_DVE, 3)
                    for n in range(1, 4):
                        on(half, hidden(n // 2, n % 2), b_act, A_, B_ACT, 3 + n)
                    on(half, folded, b_act, A_, B_ACT, 7)
            pe.wait_ge(c_x, 80)
            for k in range(NB):
                means(nX)(k, *BLK[k]).then_inc(c_pe, 1)

            def tail(step, sem_, first):
                for k in range(NB):
                    pe.wait_ge(sem_, first + k + 1)
                    step(k, *BLK[k]).then_inc(c_pe, 1)

            def back(k, c0, w):
                for j in range(w // P):
                    last = tr(PS[:, k, j * P:(j + 1) * P], nB5[:, c0 + j * P:c0 + (j + 1) * P], ident[:, :])
                return last

            tail(means(nB3), c_act, 0)
            tail(means(nB2), c_dve, NB)
            tail(means(nB3), c_act, 2 * NB)
            tail(back, c_dve, 3 * NB)

        @block.scalar
        def _(act):
            f = nc.scalar.activation
            with act.Fori(0, NG) as g:
                act.wait_ge(n0_pe, 2 * g + 1)
                f(xTg[0:D, :], PSf[0:D, 2048:2048 + GN], ACT.Copy).then_inc(n0_act, 1)
                act.wait_ge(n0_free, g + 1)
                act.wait_ge(n0_pe, 2 * g + 2)
                w = PSf[:, 0:2048].rearrange("p (t w) -> p t w", w=256)
                f(tg[:, :, :], w[:, 0:TG, 0:132], ACT.Copy).then_inc(n0_act, 1)
                f(s2n[:, bass.ds(g * TG, TG)], w[:, 0:TG, 130], ACT.Copy).then_inc(n0_act, 1)
                f(xg1[:, bass.ds(g * TG, TG)], w[:, 0:TG, 131], ACT.Copy).then_inc(n0_act, 1)

            act.wait_ge(p_dve, PD_END)
            act.sem_inc(xe_free, 2)

            def features(c, k):
                act.wait_ge(m_pe, 28 * c + k)
                f(xT8[:, :], PS[:, 0, :], ACT.Copy).then_inc(m_act, 1)

            def squares(c, u):
                act.wait_ge(cen_ready, c + 1)
                f(S0[:, u, 1:C + 1, R0 - D:R0], xe[:, u, :, :], ACT.Square).then_inc(sq_ready, 1)

            def weights(c):
                act.wait_ge(d0_ready, c + 1)
                f(ee0[:, :, :], dd0[:, :, :], ACT.Exp).then_inc(e0_ready, 1)

            def roots(c):
                act.wait_ge(var_ready, c + 1)
                f(sd8[:, :], rs8[:, :], ACT.Sqrt, bias=epsc[:, 0:1], scale=1.0 / D).then_inc(sqrt_ready, 1)

            def edges(c, u, ahead):
                features(c, 1)
                for s in range(PT):
                    for r in range(2):
                        act.wait_ge(m_pe, 28 * c + 4 * s + 2 + r)
                        for kh in range(2):
                            f(hid8[:, r, kh, :], PS[:, 1 + 2 * r + kh, :], ACT.Relu, bias=b1c[:, kh:kh + 1]).then_inc(m_act, 1)
                    if ahead and s == PT - 2:
                        roots(c + 1)
                    if s < PT - 1:
                        features(c, 4 * s + 4)
                    if s == 0:
                        act.wait_ge(ea_out, 16 * c + 16)
                    act.wait_ge(m_pe, 28 * c + (4 * s + 5 if s < PT - 1 else 28))
                    f(eaC[:, 4 * s:4 * s + 4, :].rearrange("p a b -> p (a b)"), PS[:, 5, :], ACT.Identity,
                      bias=b2c[:, 0:1]).then_inc(m_act, 1)
                    if s == PT - 3:
                        act.wait_ge(done0, c + 3)
                        act.dma_start(chunk_rows(st0, R0, c), S0[:, u, 1:C + 1, :].rearrange("p c w -> p (c w)")).then_inc(st0_out[u], 16)
                    if ahead and s == PT - 3:
                        squares(c + 1, 1 - u)
                        weights(c + 1)
                act.wait_ge(m_act, 42 * c + 42)
                act.sem_inc(xe_free, 1)
                act.dma_start(eaT[bass.ds(c, 1), :, :].rearrange("o p n -> (o p) n"),
                              eaC[:, :, :].rearrange("p a b -> p (a b)")).then_inc(ea_out, 16)

            squares(0, 0)
            weights(0)
            roots(0)
            with act.Fori(0, NCH // 2 - 1) as i:
                edges(2 * i, 0, True)
                edges(2 * i + 1, 1, True)
            edges(NCH - 2, 0, True)
            edges(NCH - 1, 1, False)

            def fix(V, o, scale):
                act.wait_ge(f_dve, o * 5 + 2)
                f(abE[0:V, :, :], ab[0:V, :, :], ACT.Exp, scale=scale).then_inc(f_act, 1)
                act.wait_ge(f_dve, o * 5 + 4)
                f(abE[:, :, 0:V], ab[:, :, 0:V], ACT.Exp, scale=scale).then_inc(f_act, 1)

            fix(V0, 0, 1.0)
            for k in range(NB):
                at = slice(8 * k, min(8 * k + 8, NT))
                act.wait_ge(u_dve, k + 1)
                f(n49[4][:, at], n49[3][:, at], ACT.Sigmoid).then_inc(u_act, 1)
            act.wait_ge(u_dve, NB + 1)
            f(n49[0], n49[7], ACT.Sqrt, bias=epsc[:, 0:1], scale=1.0 / D).then_inc(u_act, 1)
            for k in range(NB):
                c0, w = BLK[k]
                act.wait_ge(u_pe, k + 1)
                f(xT0[:, c0:c0 + w], PS[:, k, 0:w], ACT.Copy).then_inc(u_act, 1)

            def per_block(step, done, sem_, base, first):
                for k in range(NB):
                    act.wait_ge(sem_, base + first + k + 1)
                    step(k, *BLK[k]).then_inc(done, 1)

            def square(k, c0, w):
                return f(nB3[:, c0:c0 + w], nB5[:, c0:c0 + w], ACT.Square)

            def inverse_root(done, sem_, value, norm, blocks=range(NB)):
                for k in blocks:
                    c0, w = BLK[k]
                    act.wait_ge(sem_, value(k))
                    f(nB4[:, c0:c0 + w], PS[:, k, 0:w], ACT.Ln, bias=epsc[:, 0:1]).then_inc(ln_ready, 1)
                for k in blocks:
                    c0, w = BLK[k]
                    act.wait_ge(ln_ready, norm * NB + k + 1)
                    f(nB4[:, c0:c0 + w], nB4[:, c0:c0 + w], ACT.Exp, scale=-0.5).then_inc(done, 1)

            with act.Fori(0, L) as l:
                per_block(square, a_act, a_dve, l * A_DVE, 0)
                inverse_root(a_act, a_pe, lambda k: l * (3 * NB) + NB + k + 1, 2 * l)
                with act.Fori(0, NCH // 2) as i:
                    for u in range(2):
                        n = l * NCH + 2 * i + u
                        for s in range(PT):
                            b = 2 * (s % 4)
                            act.wait_ge(kv_ready, n * PT + s + 1)
                            f(G1[:, u, 8 * s:8 * s + 8, D:2 * D], PS[:, b + 1, :].rearrange("p (t d) -> p t d", t=8), ACT.Copy).then_inc(v_moved, 1)
                        act.wait_ge(d1_ready, n + 1)
                        f(ee1[:, :, :, :], dd1[:, :, :, :], ACT.Exp, scale=SCALE).then_inc(e1_ready, 1)
                        act.wait_ge(done1, n + 3)
                        act.dma_start(chunk_rows(st1, R1, 2 * i + u), S1[:, u, 1:C + 1, :].rearrange("p c w -> p (c w)")).then_inc(st1_out[u], 16)
                fix(V1, l + 1, SCALE)
                P_ = l * (B_PE * NB)

                def on(half, step, sem_, base, steps, awaited):
                    for k in half:
                        act.wait_ge(sem_, base + after(steps, awaited, k))
                        step(k, *BLK[k]).then_inc(b_act, 1)

                for half in HALVES:
                    on(half, lambda k, c0, w: f(nB2[:, c0:c0 + w], PS[:, k, 0:w], ACT.Copy), b_pe, P_, B_PE, 0)
                    on(half, lambda k, c0, w: f(nB3[:, c0:c0 + w], PS[:, k, 0:w], ACT.Sigmoid, bias=bgc[:, 0:1]), b_pe, P_, B_PE, 1)
                    on(half, square, b_dve, l * (B_DVE * NB) + 1, B_DVE, 2)
                    inverse_root(b_act, b_pe, lambda k: P_ + after(B_PE, 5, k), 2 * l + 1, half)
                    for n in range(4):
                        on(half, lambda k, c0, w: f(HIDDEN[n][:, c0:c0 + w], PS[:, k, 0:w], ACT.Relu, bias=mb1c[:, n // 2:n // 2 + 1]),
                           b_pe, P_, B_PE, 6 + n)
            for n in range(2):
                per_block(square, c_act, c_dve, 0, 2 * n * NB)
                inverse_root(c_act, c_pe, lambda k: (2 * n + 1) * NB + k + 1, 2 * L + n)

        @block.vector
        def _(dve):
            v = nc.vector
            tt, ts, stt, cp, red = v.tensor_tensor, v.tensor_scalar, v.scalar_tensor_tensor, v.tensor_copy, v.tensor_reduce
            scan = v.tensor_tensor_scan
            settle = dve.drain

            def along(ap, shape):
                return ap.unsqueeze(len(shape) - 1).broadcast_to(shape)

            dve.sem_inc(oh_used, 2)
            v.memset(zeros[:, :], 0.0)
            v.memset(epsc[:, :], 1e-5)
            v.memset(onesD[:, :], 0.0)
            v.memset(zw[:, :], 0.0)
            v.memset(cont[:, 0:1], 0.0)
            v.memset(W1p[:, :, :, :], 0.0)
            v.memset(W2p[:, :, :, :], 0.0)
            v.memset(s2x[:, :], 0.0)
            for block_weights in (Wkvp[:, :], Wqkv[:, :], Wn[:, :, :], mW1s[:, :, :], mW2s[:, :, :, :]):
                v.memset(block_weights, 0.0)
            settle()
            v.memset(onesD[0:D, 0:D], 1.0 / D)
            v.memset(onesD[D:P, D:P], 1.0 / D)
            settle().then_inc(p_dve, 1)
            dve.wait_ge(pool_c, 1)
            ts(ident[:, :], iotaR[:, :], iotaC[:, 0:1], None, ALU.is_equal)
            ts(tri[:, :], iotaR[:, :], iotaC[:, 0:1], None, ALU.is_gt).then_inc(p_dve, 1)
            dve.wait_ge(w_in, 16 * NWIN)
            ts(hiI[:, :], dstI[:, :], 7, None, ALU.logical_shift_right)
            ts(loI[:, :], dstI[:, :], 127, None, ALU.bitwise_and)
            cp(firstI[:, :], dstI[:, 0:1])
            cp(dstF[:, :], dstI[:, :])
            settle()
            cp(hiB, hiI[:, :])
            cp(loB, loI[:, :])
            tt(cont[:, 1:T], dstF[:, 1:T], dstF[:, 0:T - 1], ALU.is_equal)
            cp(F1b[:, :], dstF[:, 0:1].broadcast_to([P, V1]))
            cp(F2b[:, :], dstF[:, T - 1:T].broadcast_to([P, V1]))
            for r in range(2):
                rows = slice(r * D, (r + 1) * D)
                ts(W1p[rows, r, :, :].rearrange("p k n -> p (k n)"), W1raw[rows, :], engc[rows, 0:1], None, ALU.mult)
                cp(W2p[:, :, r, r * D:(r + 1) * D], W2raw[:, :, :])
            settle().then_inc(p_dve, 1)
            dve.wait_ge(p_pe, 1)
            cp(WaT[:, :], PS[0:D, 6, 0:D])
            tt(b1c[:, :], PS[:, 7, 0:2], eb1c[:, :], ALU.add).then_inc(p_dve, 1)
            dve.wait_ge(p_pe, 2)
            cp(Wcat[:, 128:129], PS[0:D, 6, 64:65])
            cp(Wcat[:, 130:131], PS[0:D, 6, 65:66]).then_inc(p_dve, 1)
            with dve.Fori(0, NCH // 2) as i:
                for u in range(2):
                    c = 2 * i + u
                    dve.wait_ge(oh_used, c + 1)
                    for first, w, of in ((0, NT, hiB), (NT, P, loB)):
                        cols = slice(first * C, (first + w) * C)
                        tt(ohf[u][:, cols].rearrange("p (w c) -> p w c", c=C), rep[:, cols].rearrange("p (w c) -> p w c", c=C),
                           of[:, bass.ds(c * C, C)].unsqueeze(1).broadcast_to([P, w, C]), ALU.is_equal).then_inc(oh_ready, 1)
            dve.wait_ge(p_pe, 3)
            cp(degR[0:NT, :], PS[0:NT, 7, 0:P])
            settle()
            scan(cumR[0:NT, :], zeros[0:NT, 0:P], degR[0:NT, :], 0.0, ALU.add, ALU.add).then_inc(p_dve, 1)
            dve.wait_ge(p_pe, 4)
            cp(baseC[0:NT, :], PS[0:NT, 1, 0:1])
            settle()
            ts(endxR[0:NT, :], cumR[0:NT, :], baseC[0:NT, 0:1], None, ALU.add).then_inc(p_dve, 1)
            dve.wait_ge(p_pe, 5)
            ts(lastF[:, :], PS[:, 2, 0:NT], -1.0, None, ALU.add)
            cp(degn[:, :], PS[:, 3, 0:NT])
            settle()
            ts(neF[:, :], degn[:, :], 0.0, None, ALU.is_gt)
            tt(tmpN[:, :], lastF[:, :], degn[:, :], ALU.subtract)
            settle()
            ts(firstF[:, :], tmpN[:, :], 1.0, None, ALU.add)
            settle()
            stt(tmpN[:, :], lastF[:, :], -float(EP), neF[:, :], ALU.add, ALU.mult)
            settle()
            ts(endI[:, :], tmpN[:, :], float(EP), None, ALU.add)
            settle()
            tt(tmpN[:, :], firstF[:, :], nodeE[:, :], ALU.subtract)
            settle()
            tt(tmpN[:, :], tmpN[:, :], neF[:, :], ALU.mult)
            settle()
            tt(startI[:, :], tmpN[:, :], nodeE[:, :], ALU.add)
            cp(rp_s[:, :, 0], firstF[:, :])
            cp(rp_s[:, :, 1], lastF[:, :])
            settle().then_inc(p_dve, 1)
            cp(rowF[0:V1, :], PS[0:V1, 4, 0:P])
            cp(rowL[0:V1, :], PS[0:V1, 5, 0:P])
            v.memset(gF[0:V1, 0:1], 0.0)
            settle()
            tt(gF[0:V1, 1:P], rowF[0:V1, 1:P], rowL[0:V1, 0:P - 1], ALU.is_equal)
            settle()
            tt(rowF[0:V1, :], rowF[0:V1, :], rowL[0:V1, :], ALU.is_equal)
            settle()
            tt(gF[0:V1, :], gF[0:V1, :], rowF[0:V1, :], ALU.mult)
            settle()
            ts(gmask[:, :], gF[0:V1, :], -1.0, BIG, ALU.add, ALU.mult)
            dve.wait_ge(rp_first, 16)
            tt(vF[:, 0:1], rpF[:, 0:1], iotaPT[:, :], ALU.is_lt)
            ts(vF[:, 1:2], iotaPT[:, :], float(T), None, ALU.add)
            tt(vF[:, 2:3], rpF[:, 1:2], iotaFX[:, :], ALU.subtract)
            settle()
            tt(vF[:, 1:2], rpF[:, 1:2], vF[:, 1:2], ALU.is_lt)
            settle()
            tt(vF[:, 0:1], vF[:, 0:1], vF[:, 1:2], ALU.mult)
            settle()
            tt(vF[:, 0:1], vF[:, 0:1], vF[:, 2:3], ALU.mult)
            settle()
            tt(fixI[:, :], vF[:, 0:1], iotaFX[:, :], ALU.add)
            v.memset(S0[:, 1, C, :], 0.0)
            settle().then_inc(p_dve, 1)
            dve.sem_inc(seen0, 2)
            dve.sem_inc(done0, 2)

            with dve.Fori(0, NCH // 2) as i:
                for u in range(2):
                    c = 2 * i + u
                    X = xe[:, u, :, :]
                    S, Sb = S0[:, u, :, :], S0[:, 1 - u, :, :]
                    G = G0[:, u, :, :]
                    sq = S[:, 1:C + 1, R0 - D:R0]
                    dve.wait_ge(xe_in[u], 16 * i + 16)
                    dve.wait_ge(st0_out[u], 16 * i + 16)
                    red(mu8[:, :], X, AX.X, ALU.add)
                    cp(contC[:, :], cont[:, bass.ds(c * C, C)])
                    cp(s2x[:, 0:1], s2x[:, C:C + 1])
                    cp(S[:, 0, :], Sb[:, C, :])
                    settle()
                    ts(mu8[:, :], mu8[:, :], 1.0 / D, None, ALU.mult)
                    ts(maskC[:, :], contC[:, :], -1.0, BIG, ALU.add, ALU.mult)
                    settle()
                    tt(X, X, along(mu8[:, :], [P, C, D]), ALU.subtract).then_inc(cen_ready, 1)
                    dve.wait_ge(in0[u], 32 * i + 32)
                    scan(s2x[:, 1:C + 1], contC[:, :], s2C[:, u, :], s2x[:, 0:1], ALU.mult, ALU.add)
                    dve.wait_ge(got0[u], i * (16 * C) + 16 * C)
                    dve.sem_inc(seen0, 1)
                    tt(al0[:, :], G[:, :, 2 * D], ewC[:, u, :], ALU.mult)
                    tt(uw0[:, :], G[:, :, 2 * D + 1], ewC[:, u, :], ALU.mult)
                    settle()
                    tt(al0[:, :], al0[:, :], s2x[:, 1:C + 1], ALU.add)
                    settle()
                    stt(al0[:, :], al0[:, :], 0.01, al0[:, :], ALU.mult, ALU.max)
                    settle()
                    scan(S[:, 1:C + 1, 0], maskC[:, :], al0[:, :], S[:, 0, 0:1], ALU.add, ALU.max)
                    settle()
                    tt(dd0[:, 0, :], S[:, 0:C, 0], maskC[:, :], ALU.add)
                    tt(dd0[:, 1, :], al0[:, :], S[:, 1:C + 1, 0], ALU.subtract)
                    settle()
                    tt(dd0[:, 0, :], dd0[:, 0, :], S[:, 1:C + 1, 0], ALU.subtract).then_inc(d0_ready, 1)
                    tt(G[:, :, D:2 * D], G[:, :, D:2 * D], along(ewC[:, u, :], [P, C, D]), ALU.mult)
                    dve.wait_ge(sq_ready, c + 1)
                    red(rs8[:, :], sq, AX.X, ALU.add).then_inc(var_ready, 1)
                    dve.wait_ge(sqrt_ready, c + 1)
                    v.reciprocal(rs8[:, :], sd8[:, :])
                    settle()
                    tt(X, X, along(rs8[:, :], [P, C, D]), ALU.mult).then_inc(xn_ready, 1)
                    scan(S[:, 1:C + 1, 2 + D], contC[:, :], uw0[:, :], S[:, 0, 2 + D:3 + D], ALU.mult, ALU.add)
                    for k in range(D):
                        scan(S[:, 1:C + 1, 3 + D + k], maskC[:, :], G[:, :, D + k], S[:, 0, 3 + D + k:4 + D + k], ALU.add, ALU.max)
                    dve.wait_ge(e0_ready, c + 1)
                    tt(G[:, :, 0:D], G[:, :, 0:D], along(ee0[:, 1, :], [P, C, D]), ALU.mult)
                    scan(S[:, 1:C + 1, 1], ee0[:, 0, :], ee0[:, 1, :], S[:, 0, 1:2], ALU.mult, ALU.add)
                    settle()
                    for k in range(D):
                        last = scan(S[:, 1:C + 1, 2 + k], ee0[:, 0, :], G[:, :, k], S[:, 0, 2 + k:3 + k], ALU.mult, ALU.add)
                    settle().then_inc(done0, 1)

            def fix(V, o, state, spread, copied, fm):
                spread()
                settle().then_inc(f_dve, 1)
                dve.wait_ge(f_pe, o * 2 + 1)
                cp(MXT[0:V, :], PS[0:V, 0, 0:P])
                cp(VT[0:V, :], PS[0:V, 1, 0:P])
                if fm:
                    cp(FMT[:, 0, :], PS[0:D, 2, 0:P])
                settle()
                scan(MT[0:V, :], gmask[0:V, :], MXT[0:V, :], -BIG, ALU.add, ALU.max)
                if fm:
                    v.memset(FMT[:, 1, 0:1], -BIG)
                    settle()
                    scan(FMT[:, 1, 1:P], gmask[0:D, 0:P - 1], FMT[:, 0, 0:P - 1], -BIG, ALU.add, ALU.max)
                settle()
                tt(ab[0:V, 0, 1:P], MT[0:V, 0:P - 1], gmask[0:V, 1:P], ALU.add)
                v.memset(ab[0:V, 0, 0:1], -BIG)
                tt(ab[0:V, 1, :], MXT[0:V, :], MT[0:V, :], ALU.subtract)
                settle()
                tt(ab[0:V, 0, 1:P], ab[0:V, 0, 1:P], MT[0:V, 1:P], ALU.subtract).then_inc(f_dve, 1)
                dve.wait_ge(f_act, o * 2 + 1)
                tt(VT[0:V, :], VT[0:V, :], abE[0:V, 1, :], ALU.mult)
                v.memset(sh[0:V, 0, 0:1], -BIG)
                v.memset(sh[0:V, 1, 0:1], 0.0)
                cp(sh[0:V, 0, 1:P], MT[0:V, 0:P - 1])
                settle()
                scan(sh[0:V, 1, 1:P], abE[0:V, 0, 0:P - 1], VT[0:V, 0:P - 1], 0.0, ALU.mult, ALU.add)
                settle().then_inc(f_dve, 1)
                dve.wait_ge(f_pe, o * 2 + 2)
                dve.wait_ge(f_got, o * 16 + 16)
                copied()
                settle()
                tt(wide[:, 0, 0:V], MX[:, 0:V], PS[:, 3, 0:V], ALU.max)
                cp(wide[:, 1, 0:V], PS[:, 4, 0:V])
                settle()
                tt(ab[:, 0, 0:V], PS[:, 3, 0:V], wide[:, 0, 0:V], ALU.subtract)
                tt(ab[:, 1, 0:V], MX[:, 0:V], wide[:, 0, 0:V], ALU.subtract)
                settle().then_inc(f_dve, 1)
                dve.wait_ge(f_act, o * 2 + 2)
                return

            def join(V, first, nmax, R, fm):
                tt(wide[:, 1, 0:V], wide[:, 1, 0:V], abE[:, 0, 0:V], ALU.mult)
                tt(wfix[:, first:first + V], rfix[:, first:first + V], abE[:, 1, 0:V], ALU.mult)
                cp(wfix[:, 0:nmax], wide[:, 0, 0:nmax])
                if fm:
                    tt(wfix[:, R - D:R], rfix[:, R - D:R], PS[:, 5, 0:D], ALU.max)
                settle()
                tt(wfix[:, first:first + V], wfix[:, first:first + V], wide[:, 1, 0:V], ALU.add)
                settle().then_inc(f_dve, 1)

            def spread0(row):
                cp(MX[:, 0:V0 - 1], row[:, 0:1].broadcast_to([P, V0 - 1]))
                v.memset(MX[:, V0 - 1:V0], 0.0)

            fix(V0, 0, None, lambda: spread0(S0[:, 1, C, :]), lambda: spread0(rfix), True)
            join(V0, 1, 1, R0, True)

            ts(n49[3], degn[:, :], 1.0, None, ALU.max)
            settle()
            v.reciprocal(n49[2], n49[3])
            for k in range(NB):
                at = slice(8 * k, min(8 * k + 8, NT))
                n = at.stop - at.start
                dve.wait_ge(rows_got[k], 16 * n)
                ts(n49[0][:, at], rows0[:, at, 1], 1e-30, None, ALU.max)
                tt(tp0[:, at, :], rows0[:, at, 3 + D:R0], gw2r[:, :].unsqueeze(1).broadcast_to([P, n, D]), ALU.mult)
                settle()
                v.reciprocal(n49[1][:, at], n49[0][:, at])
                red(n49[6][:, at], tp0[:, at, :], AX.X, ALU.add)
                tt(n49[3][:, at], rows0[:, at, 2 + D], n49[2][:, at], ALU.mult)
                settle()
                tt(n49[3][:, at], n49[3][:, at], n49[6][:, at], ALU.add)
                settle()
                tt(n49[3][:, at], n49[3][:, at], xg1[:, at], ALU.add).then_inc(u_dve, 1)
                dve.wait_ge(u_act, k + 1)
                tt(n49[5][:, at], n49[4][:, at], n49[1][:, at], ALU.mult)
                if k == 0:
                    dve.wait_ge(u_x, 16)
                settle()
                tt(tq0[:, at, :], rows0[:, at, 2:2 + D], along(n49[5][:, at], [P, n, D]), ALU.mult)
                settle()
                tt(xn0[:, at, :], xn0[:, at, :], tq0[:, at, :], ALU.add)
                settle()
                red(n49[6][:, at], xn0[:, at, :], AX.X, ALU.add)
                settle()
                ts(n49[6][:, at], n49[6][:, at], 1.0 / D, None, ALU.mult)
                settle()
                tt(xn0[:, at, :], xn0[:, at, :], along(n49[6][:, at], [P, n, D]), ALU.subtract)
                settle()
                tt(tp0[:, at, :], xn0[:, at, :], xn0[:, at, :], ALU.mult)
                settle()
                last = red(n49[7][:, at], tp0[:, at, :], AX.X, ALU.add)
            last.then_inc(u_dve, 1)
            dve.wait_ge(u_act, NB + 1)
            v.reciprocal(n49[1], n49[0])
            settle()
            for k in range(NB):
                at = slice(8 * k, min(8 * k + 8, NT))
                tt(xn0[:, at, :], xn0[:, at, :], along(n49[1][:, at], [P, at.stop - at.start, D]), ALU.mult).then_inc(u_dve, 1)

            dve.wait_ge(u_out, 16)
            dve.wait_ge(ea_out, 16 * (NCH + 1))
            v.memset(S1[:, 1, C, :], 0.0)
            v.memset(qlb[:, :], 0.0)
            settle()
            dve.sem_inc(done1, 2)
            dve.sem_inc(seen1, 2)
            dve.sem_inc(k_used, 4)
            dve.sem_inc(v_moved, 4)
            dve.sem_inc(b_dve, 1)

            def per_block(step, done, sem_, base, first):
                for k in range(NB):
                    dve.wait_ge(sem_, base + first + k + 1)
                    step(k, *BLK[k]).then_inc(done, 1)

            def centre(src):
                return lambda k, c0, w: tt(nB5[:, c0:c0 + w], src[:, c0:c0 + w], PS[:, k, 0:w], ALU.subtract)

            def normed(dst, g_, b_):
                def step(k, c0, w):
                    out_ = tt(nB5[:, c0:c0 + w], nB5[:, c0:c0 + w], nB4[:, c0:c0 + w], ALU.mult)
                    if g_ is not None:
                        settle()
                        out_ = ts(dst[:, c0:c0 + w], nB5[:, c0:c0 + w], cb[:, g_:g_ + 1], cb[:, b_:b_ + 1], ALU.mult, ALU.add)
                    return out_
                return step

            dve.wait_ge(a_x, 16)
            with dve.Fori(0, L) as l:
                dve.wait_ge(l_t, (l + 1) * (16 * NTW))
                tt(bkv[:, :, :], bqkv[:, 1:3, :], bqkv[:, 3:5, :], ALU.add)
                per_block(centre(nX), a_dve, a_pe, l * (3 * NB), 0)
                for k in range(NB):
                    dve.wait_ge(a_act, l * (2 * NB) + NB + k + 1)
                    normed(nH, N1G, N1B)(k, *BLK[k])
                    settle().then_inc(a_dve, 1)
                for k in range(NB):
                    c0, w = BLK[k]
                    dve.wait_ge(a_pe, l * (3 * NB) + 2 * NB + k + 1)
                    if k >= 2:
                        dve.wait_ge(a_out[k % 2], l * (16 * ((NB + 1 - k % 2) // 2)) + 16 * (k // 2))
                    s_ = PS[:, 4 * (k % 2):4 * (k % 2) + w // P, 0:6 * D].rearrange("p j (q w) -> p j q w", q=2)
                    kv_ = nkv[k % 2][:, 0:2 * w].rearrange("p (j q w) -> p j q w", q=2, w=2 * D)
                    q_ = q_all[:, 2 * c0 // P:2 * (c0 + w) // P, :].rearrange("p (j q) d -> p j q d", q=2)
                    for q in range(2):
                        tt(kv_[:, :, q, :], s_[:, :, q, D:3 * D],
                           bkv[:, :, :].rearrange("p a d -> p (a d)").unsqueeze(1).broadcast_to([P, w // P, 2 * D]), ALU.add)
                        tt(q_[:, :, q, :], s_[:, :, q, 0:D], bqkv[:, 0, :].unsqueeze(1).broadcast_to([P, w // P, D]), ALU.add)
                    settle().then_inc(a_dve, 1)
                with dve.Fori(0, NCH // 2) as i:
                    for u in range(2):
                        c = 2 * i + u
                        n = l * NCH + c
                        S, Sb = S1[:, u, :, :], S1[:, 1 - u, :, :]
                        Q, Qb = Q1[:, u, :, :], Q1[:, 1 - u, :, :]
                        G = G1[:, u, :, :]
                        cp(contC[:, :], cont[:, bass.ds(c * C, C)])
                        dve.wait_ge(st1_out[u], l * (16 * (NCH // 2)) + i * 16 + 16)
                        cp(S[:, 0, :], Sb[:, C, :])
                        settle()
                        ts(maskC[:, :], contC[:, :], -1.0, BIG, ALU.add, ALU.mult)
                        dve.wait_ge(q_in[u], l * (16 * (NCH // 2)) + i * 16 + 16)
                        cp(ql[:, :], qlb[:, :])
                        settle()
                        for k in range(D):
                            scan(Q[:, :, k], contC[:, :], Q[:, :, k], ql[:, k:k + 1], ALU.mult, ALU.add)
                        settle()
                        cp(qlb[:, :], Q[:, C - 1, :])
                        for s in range(PT):
                            b = 2 * (s % 4)
                            dve.wait_ge(kv_ready, n * PT + s + 1)
                            tt(PR[:, 8 * s:8 * s + 8, :], PS[:, b, :].rearrange("p (t d) -> p t d", t=8),
                               Q[:, 8 * s:8 * s + 8, :], ALU.mult).then_inc(k_used, 1)
                        settle()
                        red(al1[:, :, :], PR[:, :, :].rearrange("p t (h d) -> p t h d", h=H), AX.X, ALU.add)
                        settle()
                        for h in range(H):
                            scan(S[:, 1:C + 1, h], maskC[:, :], al1[:, :, h], S[:, 0, h:h + 1], ALU.add, ALU.max)
                        settle()
                        tt(dd1[:, 0, :, :], S[:, 0:C, 0:H], along(maskC[:, :], [P, C, H]), ALU.add)
                        tt(dd1[:, 1, :, :], al1[:, :, :], S[:, 1:C + 1, 0:H], ALU.subtract)
                        settle()
                        tt(dd1[:, 0, :, :], dd1[:, 0, :, :], S[:, 1:C + 1, 0:H], ALU.subtract).then_inc(d1_ready, 1)
                        dve.wait_ge(e1_ready, n + 1)
                        vals = G[:, :, D:2 * D].rearrange("p t (h d) -> p t h d", h=H)
                        tt(vals, vals, along(ee1[:, 1, :, :], [P, C, H, HD]), ALU.mult)
                        for h in range(H):
                            scan(S[:, 1:C + 1, H + h], ee1[:, 0, :, h], ee1[:, 1, :, h], S[:, 0, H + h:H + h + 1], ALU.mult, ALU.add)
                        settle()
                        for k in range(D):
                            scan(S[:, 1:C + 1, 2 * H + k], ee1[:, 0, :, k // HD], G[:, :, D + k], S[:, 0, 2 * H + k:2 * H + k + 1], ALU.mult, ALU.add)
                        settle().then_inc(done1, 1)

                def spread1(row):
                    cp(MX[:, 0:H], row[:, 0:H])
                    cp(MX[:, H:V1].rearrange("p (h d) -> p h d", h=H), along(row[:, 0:H], [P, H, HD]))

                fix(V1, l + 1, None, lambda: spread1(S1[:, 1, C, :]), lambda: spread1(rfix), False)
                join(V1, H, H, R1, False)
                dve.wait_ge(l_w, (l + 1) * (16 * NLW))
                tt(bgc[:, :], cb[:, BIH:BIH + 1], cb[:, BHH:BHH + 1], ALU.add)
                v.memset(nag[:, NT * D:], 0.0)

                def sums(half):
                    for k in half:
                        c0, w = BLK[k]
                        t0, t1 = 2 * c0 // P, min(2 * (c0 + w) // P, NT)
                        dve.wait_ge(rows_got[k], (l + 2) * (16 * (t1 - t0)))
                        ts(rden[:, t0:t1, :], rows1[:, t0:t1, H:2 * H], 1e-16, None, ALU.add)
                        settle()
                        v.reciprocal(rden[:, t0:t1, :], rden[:, t0:t1, :])
                        settle()
                        tt(nag[:, t0 * D:t1 * D].rearrange("p (t h d) -> p t h d", h=H, d=HD),
                           rows1[:, t0:t1, 2 * H:R1].rearrange("p t (h d) -> p t h d", h=H),
                           rden[:, t0:t1, :].unsqueeze(3).broadcast_to([P, t1 - t0, H, HD]), ALU.mult)
                        settle().then_inc(sums_ready, 1)

                def mix(k, c0, w):
                    stt(nB4[:, c0:c0 + w], PS[:, k, 0:w], cb[:, BSELF:BSELF + 1], nB2[:, c0:c0 + w], ALU.add, ALU.subtract)
                    settle()
                    tt(nB4[:, c0:c0 + w], nB4[:, c0:c0 + w], nB3[:, c0:c0 + w], ALU.mult)
                    settle()
                    return tt(nB4[:, c0:c0 + w], nB4[:, c0:c0 + w], nB2[:, c0:c0 + w], ALU.add)

                def onto_x(bias):
                    return lambda k, c0, w: stt(nX[:, c0:c0 + w], PS[:, k, 0:w], cb[:, bias:bias + 1], nX[:, c0:c0 + w], ALU.add, ALU.add)

                P_ = l * (B_PE * NB)

                def on(half, step, sem_, base, steps, awaited):
                    for k in half:
                        dve.wait_ge(sem_, base + after(steps, awaited, k))
                        step(k, *BLK[k]).then_inc(b_dve, 1)

                sums(HALVES[0])
                for half in HALVES:
                    on(half, mix, b_pe, P_, B_PE, 2)
                    on(half, onto_x(BOUT), b_pe, P_, B_PE, 3)
                    on(half, centre(nX), b_pe, P_, B_PE, 4)
                    on(half, normed(nB5, N2G, N2B), b_act, l * (B_ACT * NB), B_ACT, 3)
                    if half is HALVES[0]:
                        sums(HALVES[1])
                    on(half, onto_x(MB2), b_pe, P_, B_PE, 10)
                settle()

            per_block(centre(nX), c_dve, c_pe, 0, 0)
            for k in range(NB):
                c0, w = BLK[k]
                dve.wait_ge(c_act, NB + k + 1)
                normed(nB2, NGC, NBC)(k, c0, w)
                settle()
                tt(nB2[:, c0:c0 + w], nB2[:, c0:c0 + w], nH[:, c0:c0 + w], ALU.add).then_inc(c_dve, 1)
            per_block(centre(nB2), c_dve, c_pe, 0, 2 * NB)
            per_block(normed(None, None, None), c_dve, c_act, 0, 3 * NB)
            per_block(lambda k, c0, w: cp(nag[:, c0:c0 + w], PS[:, k, 0:w]), c_dve, c_pe, 0, 4 * NB)

        first.close()
        second.close()


_INS = {'x': 'x', 'src': 'src', 'dst': 'dst', 'edge_attr_64': 'edge_attr_64', 'edge_weight1': 'edge_weight1',
        'Wa': 'L0_gnn_Wa', 'att_w': 'L0_gnn_att_w', 'Wg': 'L0_gnn_Wg', 'gate_w': 'L0_gnn_gate_w'}
_INS.update({n: 'L1_gnn_' + n for n in (
    'eng', 'enb', 'eW1', 'eb1', 'eW2', 'eb2', 'Wq', 'bq', 'Wkn', 'bkn', 'Wke', 'bke', 'Wvn', 'bvn', 'Wve', 'bve',
    'Wself', 'bself', 'Wih', 'bih', 'Whh', 'bhh', 'Wout', 'bout', 'n1g', 'n1b', 'n2g', 'n2b',
    'mW1', 'mb1', 'mW2', 'mb2', 'ng', 'nb')})


_TABLE_WEIGHTS = ('n1g', 'n1b', 'Wq', 'Wkn', 'Wvn', 'Wke', 'Wve', 'bq', 'bkn', 'bvn', 'bke', 'bve')


def kernel(**inputs):
    import numpy as _np
    import concourse.bacc as _bacc
    from concourse import mybir as _mybir
    from concourse.bass_utils import run_bass_kernel_spmd as _run

    nc = _bacc.Bacc("TRN2", target_bir_lowering=False, num_devices=1)
    rows = {'x': (NP, 0), 'src': (EP, 0), 'dst': (EP, N), 'edge_attr_64': (EP, 0), 'edge_weight1': (EP, 0)}
    arrays, aps = {}, {}
    for short, name in _INS.items():
        a = _np.ascontiguousarray(inputs[name])
        if short in rows:
            n, fill = rows[short]
            padded = _np.full((n,) + a.shape[1:], fill, a.dtype)
            padded[:a.shape[0]] = a
            a = padded
        if short in _TABLE_WEIGHTS:
            a = _np.concatenate([a, _np.zeros_like(a[:1])])
        arrays[f"in_{short}"] = a
        aps[short] = nc.dram_tensor(f"in_{short}", a.shape, _mybir.dt.from_np(a.dtype), kind="ExternalInput").ap()
    out = nc.dram_tensor("out_0", (NP, D), _mybir.dt.float32, kind="ExternalOutput").ap()
    build(nc, aps, out)
    r = _run(nc, [arrays], core_ids=[0])
    return r.results[0]["out_0"][:N]
```
